# Optimizing a Trainium2 kernel written in Bass

```python
import numpy as np
import jax
import jax.numpy as jnp

def _softmax(x, axis=-1):
    return jax.nn.softmax(x, axis=axis)

def _gelu(x):
    return jax.nn.gelu(x, approximate=True)

def _silu(x):
    return jax.nn.silu(x)

def _sigmoid(x):
    return jax.nn.sigmoid(x)

def _layernorm(x, axis=-1, eps=1e-05):
    m = jnp.mean(x, axis=axis, keepdims=True)
    v = jnp.var(x, axis=axis, keepdims=True)
    return (x - m) / jnp.sqrt(v + eps)

def _scatter_add(tgt, idx, src, axis=0):
    return tgt.at[idx].add(src)

def _segment_sum(src, seg, n):
    return jax.ops.segment_sum(src, seg, n)
kernel_name = 'mk_hybrid_d1_jaxref_r8_3a0e45'

def setup_inputs(seed: int=0):
    np.random.seed(seed)
    _w = jnp.asarray

    def _L0_attn_a_setup():
        import jax, jax.numpy as jnp
        import numpy as np
        H = 16
        GRID = 16
        TOK_PER_FRAME = GRID * GRID

        def _rope(x, pos, dim):
            half = dim // 2
            omega = jnp.arange(half, dtype=x.dtype) / (dim / 2.0)
            inv = 1.0 / 10000.0 ** omega
            freq = pos.astype(x.dtype)[:, None] * inv
            sin = jnp.concatenate([jnp.sin(freq), jnp.sin(freq)], axis=-1)
            cos = jnp.concatenate([jnp.cos(freq), jnp.cos(freq)], axis=-1)
            y = x.reshape(*x.shape[:-1], half, 2)
            y1, y2 = (y[..., 0], y[..., 1])
            rot = jnp.stack((-y2, y1), axis=-1).reshape(x.shape)
            return x * cos + rot * sin

        def _apply_3d_rope(qk, f_ids, h_ids, w_ids, d_dim):
            s = 0
            parts = []
            for pos in (f_ids, h_ids, w_ids):
                parts.append(_rope(qk[..., s:s + d_dim], pos, d_dim))
                s += d_dim
            if s < qk.shape[-1]:
                parts.append(qk[..., s:])
            return jnp.concatenate(parts, axis=-1)
        key = jax.random.key(seed)
        ks = jax.random.split(key, 5)
        D = 128
        B, N = (4, 256)
        sc = 0.02
        return {'hidden_states': jax.random.normal(ks[0], (B, N, D), jnp.float32), 'Wq': jax.random.normal(ks[1], (D, D), jnp.float32) * sc, 'bq': jnp.zeros((D,), jnp.float32), 'Wk': jax.random.normal(ks[2], (D, D), jnp.float32) * sc, 'bk': jnp.zeros((D,), jnp.float32), 'Wv': jax.random.normal(ks[3], (D, D), jnp.float32) * sc, 'bv': jnp.zeros((D,), jnp.float32), 'Wo': jax.random.normal(ks[4], (D, D), jnp.float32) * sc, 'bo': jnp.zeros((D,), jnp.float32)}
    _L0_attn_a_in = _L0_attn_a_setup()

    def _L0_attn_b_setup():
        import jax, jax.numpy as jnp
        import numpy as np
        THETA = 10000.0

        def _rope(x, cos, sin):
            xr = x.reshape(*x.shape[:-1], -1, 2)
            x0, x1 = (xr[..., 0], xr[..., 1])
            o0 = x0 * cos - x1 * sin
            o1 = x0 * sin + x1 * cos
            return jnp.stack([o0, o1], axis=-1).reshape(x.shape)
        key = jax.random.key(seed)
        ks = jax.random.split(key, 7)
        B, S, D = (4, 256, 128)
        sd = 1.0 / np.sqrt(D)
        return {'x': jax.random.normal(ks[0], (B, S, D), dtype=jnp.float32), 'wq_w': jax.random.normal(ks[1], (D, D), dtype=jnp.float32) * sd, 'wq_b': jax.random.normal(ks[2], (D,), dtype=jnp.float32) * 0.01, 'wk_w': jax.random.normal(ks[3], (D, D), dtype=jnp.float32) * sd, 'wk_b': jax.random.normal(ks[4], (D,), dtype=jnp.float32) * 0.01, 'wv_w': jax.random.normal(ks[5], (D, D), dtype=jnp.float32) * sd, 'wv_b': jax.random.normal(ks[6], (D,), dtype=jnp.float32) * 0.01}
    _L0_attn_b_in = _L0_attn_b_setup()

    def _L0_ffn_setup():
        import jax, jax.numpy as jnp
        import numpy as np
        B, L, C1, C2, K, K_IN = (4, 128, 128, 128, 32, 32)
        BN_EPS = 1e-05

        def _gated_bottleneck(x2d, conv_w, conv_b, gamma, beta, lin_w, lin_b):
            n = x2d.shape[0]
            g = conv_w.shape[0]
            xc = jnp.einsum('ngf,gf->ng', x2d.reshape(n, g, 4), conv_w) + conv_b
            mean = jnp.mean(xc, axis=0)
            var = jnp.mean((xc - mean) ** 2, axis=0)
            xn = (xc - mean) * jax.lax.rsqrt(var + BN_EPS) * gamma + beta
            xa = jax.nn.gelu(xn, approximate=False)
            return xa @ lin_w.T + lin_b
        key = jax.random.key(seed)
        ks = jax.random.split(key, 8)
        g = C1 // 4
        w_std = (2.0 / C2) ** 0.5
        lin_std = (1.0 / g) ** 0.5
        return {'x': jax.random.normal(ks[0], (B, L, C1), jnp.float32), 'weight': jax.random.normal(ks[1], (C1, C2), jnp.float32) * w_std, 'bias': jnp.zeros((C2,), jnp.float32), 'so_conv_w': jax.random.normal(ks[2], (g, 4), jnp.float32) * 0.5, 'so_conv_b': jnp.zeros((g,), jnp.float32), 'so_gamma': jnp.ones((g,), jnp.float32), 'so_beta': jnp.zeros((g,), jnp.float32), 'so_lin_w': jax.random.normal(ks[3], (C2, g), jnp.float32) * lin_std, 'so_lin_b': jnp.zeros((C2,), jnp.float32), 'si_conv_w': jax.random.normal(ks[4], (g, 4), jnp.float32) * 0.5, 'si_conv_b': jnp.zeros((g,), jnp.float32), 'si_gamma': jnp.ones((g,), jnp.float32), 'si_beta': jnp.zeros((g,), jnp.float32), 'si_lin_w': jax.random.normal(ks[5], (C1, g), jnp.float32) * lin_std, 'si_lin_b': jnp.zeros((C1,), jnp.float32)}
    _L0_ffn_in = _L0_ffn_setup()
    _d = {'L0_attn_a_hidden_states': _L0_attn_a_in['hidden_states'], 'L0_attn_a_Wq': _L0_attn_a_in['Wq'], 'L0_attn_a_bq': _L0_attn_a_in['bq'], 'L0_attn_a_Wk': _L0_attn_a_in['Wk'], 'L0_attn_a_bk': _L0_attn_a_in['bk'], 'L0_attn_a_Wv': _L0_attn_a_in['Wv'], 'L0_attn_a_bv': _L0_attn_a_in['bv'], 'L0_attn_a_Wo': _L0_attn_a_in['Wo'], 'L0_attn_a_bo': _L0_attn_a_in['bo'], 'L0_attn_b_wq_w': _L0_attn_b_in['wq_w'], 'L0_attn_b_wq_b': _L0_attn_b_in['wq_b'], 'L0_attn_b_wk_w': _L0_attn_b_in['wk_w'], 'L0_attn_b_wk_b': _L0_attn_b_in['wk_b'], 'L0_attn_b_wv_w': _L0_attn_b_in['wv_w'], 'L0_attn_b_wv_b': _L0_attn_b_in['wv_b'], 'L0_ffn_weight': _L0_ffn_in['weight'], 'L0_ffn_bias': _L0_ffn_in['bias'], 'L0_ffn_so_conv_w': _L0_ffn_in['so_conv_w'], 'L0_ffn_so_conv_b': _L0_ffn_in['so_conv_b'], 'L0_ffn_so_gamma': _L0_ffn_in['so_gamma'], 'L0_ffn_so_beta': _L0_ffn_in['so_beta'], 'L0_ffn_so_lin_w': _L0_ffn_in['so_lin_w'], 'L0_ffn_so_lin_b': _L0_ffn_in['so_lin_b'], 'L0_ffn_si_conv_w': _L0_ffn_in['si_conv_w'], 'L0_ffn_si_conv_b': _L0_ffn_in['si_conv_b'], 'L0_ffn_si_gamma': _L0_ffn_in['si_gamma'], 'L0_ffn_si_beta': _L0_ffn_in['si_beta'], 'L0_ffn_si_lin_w': _L0_ffn_in['si_lin_w'], 'L0_ffn_si_lin_b': _L0_ffn_in['si_lin_b']}
    _x0 = _d['L0_attn_a_hidden_states']
    _d['L0_attn_a_hidden_states'] = jax.random.normal(jax.random.fold_in(jax.random.key(seed), 1), (32, 256, 128), dtype=_x0.dtype)
    del _x0
    return _d

def reference(L0_attn_a_hidden_states, L0_attn_a_Wq, L0_attn_a_bq, L0_attn_a_Wk, L0_attn_a_bk, L0_attn_a_Wv, L0_attn_a_bv, L0_attn_a_Wo, L0_attn_a_bo, L0_attn_b_wq_w, L0_attn_b_wq_b, L0_attn_b_wk_w, L0_attn_b_wk_b, L0_attn_b_wv_w, L0_attn_b_wv_b, L0_ffn_weight, L0_ffn_bias, L0_ffn_so_conv_w, L0_ffn_so_conv_b, L0_ffn_so_gamma, L0_ffn_so_beta, L0_ffn_so_lin_w, L0_ffn_so_lin_b, L0_ffn_si_conv_w, L0_ffn_si_conv_b, L0_ffn_si_gamma, L0_ffn_si_beta, L0_ffn_si_lin_w, L0_ffn_si_lin_b):

    def _L0_attn_a_ref(hidden_states, Wq, bq, Wk, bk, Wv, bv, Wo, bo):
        import jax, jax.numpy as jnp
        import numpy as np
        H = 16
        GRID = 16
        TOK_PER_FRAME = GRID * GRID

        def _rope(x, pos, dim):
            half = dim // 2
            omega = jnp.arange(half, dtype=x.dtype) / (dim / 2.0)
            inv = 1.0 / 10000.0 ** omega
            freq = pos.astype(x.dtype)[:, None] * inv
            sin = jnp.concatenate([jnp.sin(freq), jnp.sin(freq)], axis=-1)
            cos = jnp.concatenate([jnp.cos(freq), jnp.cos(freq)], axis=-1)
            y = x.reshape(*x.shape[:-1], half, 2)
            y1, y2 = (y[..., 0], y[..., 1])
            rot = jnp.stack((-y2, y1), axis=-1).reshape(x.shape)
            return x * cos + rot * sin

        def _apply_3d_rope(qk, f_ids, h_ids, w_ids, d_dim):
            s = 0
            parts = []
            for pos in (f_ids, h_ids, w_ids):
                parts.append(_rope(qk[..., s:s + d_dim], pos, d_dim))
                s += d_dim
            if s < qk.shape[-1]:
                parts.append(qk[..., s:])
            return jnp.concatenate(parts, axis=-1)
        B, N, D = hidden_states.shape
        hd = D // H
        d_dim = 2 * (hd // 3 // 2)

        def heads(x):
            return x.reshape(B, N, H, hd).transpose(0, 2, 1, 3)
        q = heads(hidden_states @ Wq + bq)
        k = heads(hidden_states @ Wk + bk)
        v = heads(hidden_states @ Wv + bv)
        ids = jnp.arange(N)
        f_ids = ids // TOK_PER_FRAME
        rem = ids - TOK_PER_FRAME * f_ids
        h_ids = rem // GRID
        w_ids = rem - GRID * h_ids
        q = _apply_3d_rope(q, f_ids, h_ids, w_ids, d_dim)
        k = _apply_3d_rope(k, f_ids, h_ids, w_ids, d_dim)
        scale = hd ** (-0.5)
        attn = jnp.einsum('bhqd,bhkd->bhqk', q, k) * scale
        attn = jax.nn.softmax(attn.astype(jnp.float32), axis=-1).astype(q.dtype)
        ctx = jnp.einsum('bhqk,bhkd->bhqd', attn, v)
        ctx = ctx.transpose(0, 2, 1, 3).reshape(B, N, D)
        return ctx @ Wo + bo

    def _L0_attn_b_ref(x, wq_w, wq_b, wk_w, wk_b, wv_w, wv_b):
        import jax, jax.numpy as jnp
        import numpy as np
        THETA = 10000.0

        def _rope(x, cos, sin):
            xr = x.reshape(*x.shape[:-1], -1, 2)
            x0, x1 = (xr[..., 0], xr[..., 1])
            o0 = x0 * cos - x1 * sin
            o1 = x0 * sin + x1 * cos
            return jnp.stack([o0, o1], axis=-1).reshape(x.shape)
        B, S, D = x.shape
        q = jnp.einsum('bsd,ed->bse', x, wq_w) + wq_b
        k = jnp.einsum('bsd,ed->bse', x, wk_w) + wk_b
        v = jnp.einsum('bsd,ed->bse', x, wv_w) + wv_b
        inv_freq = 1.0 / THETA ** (jnp.arange(0, D, 2, dtype=jnp.float32) / D)
        ang = jnp.arange(S, dtype=jnp.float32)[:, None] * inv_freq[None, :]
        cos, sin = (jnp.cos(ang), jnp.sin(ang))
        q = _rope(q, cos, sin)
        k = _rope(k, cos, sin)
        scores = jnp.einsum('bqd,bkd->bqk', q, k) / jnp.sqrt(jnp.float32(D))
        probs = jax.nn.softmax(scores.astype(jnp.float32), axis=-1)
        return jnp.einsum('bqk,bkd->bqd', probs, v)

    def _L0_ffn_ref(x, weight, bias, so_conv_w, so_conv_b, so_gamma, so_beta, so_lin_w, so_lin_b, si_conv_w, si_conv_b, si_gamma, si_beta, si_lin_w, si_lin_b):
        import jax, jax.numpy as jnp
        import numpy as np
        B, L, C1, C2, K, K_IN = (4, 128, 128, 128, 32, 32)
        BN_EPS = 1e-05

        def _gated_bottleneck(x2d, conv_w, conv_b, gamma, beta, lin_w, lin_b):
            n = x2d.shape[0]
            g = conv_w.shape[0]
            xc = jnp.einsum('ngf,gf->ng', x2d.reshape(n, g, 4), conv_w) + conv_b
            mean = jnp.mean(xc, axis=0)
            var = jnp.mean((xc - mean) ** 2, axis=0)
            xn = (xc - mean) * jax.lax.rsqrt(var + BN_EPS) * gamma + beta
            xa = jax.nn.gelu(xn, approximate=False)
            return xa @ lin_w.T + lin_b
        b, l, c1 = x.shape
        c2 = weight.shape[1]
        x2d = x.reshape(b * l, c1)
        bi = jnp.arange(b)[:, None, None]
        li = jnp.arange(l)[None, :, None]
        score_out = jax.nn.softmax(_gated_bottleneck(x2d, so_conv_w, so_conv_b, so_gamma, so_beta, so_lin_w, so_lin_b).reshape(b, l, c2), axis=-1)
        s_v_out, s_i_out = jax.lax.top_k(score_out, K)
        full = jnp.einsum('blc,co->blo', x, weight)
        out_k = jnp.take_along_axis(full, s_i_out, axis=-1) * s_v_out
        out_branch = jnp.zeros((b, l, c2), x.dtype).at[bi, li, s_i_out].add(out_k)
        score_in = jax.nn.softmax(_gated_bottleneck(x2d, si_conv_w, si_conv_b, si_gamma, si_beta, si_lin_w, si_lin_b).reshape(b, l, c1), axis=-1)
        s_v_in, s_i_in = jax.lax.top_k(score_in, K_IN)
        x_gated = jnp.take_along_axis(x, s_i_in, axis=-1) * s_v_in
        x_sparse = jnp.zeros((b, l, c1), x.dtype).at[bi, li, s_i_in].add(x_gated)
        in_branch = jnp.einsum('blc,co->blo', x_sparse, weight)
        return out_branch + in_branch + bias
    x = L0_attn_a_hidden_states
    x = x + _L0_attn_a_ref(_layernorm(x, axis=-1), L0_attn_a_Wq, L0_attn_a_bq, L0_attn_a_Wk, L0_attn_a_bk, L0_attn_a_Wv, L0_attn_a_bv, L0_attn_a_Wo, L0_attn_a_bo)
    x = x + _L0_ffn_ref(_layernorm(x, axis=-1), L0_ffn_weight, L0_ffn_bias, L0_ffn_so_conv_w, L0_ffn_so_conv_b, L0_ffn_so_gamma, L0_ffn_so_beta, L0_ffn_so_lin_w, L0_ffn_so_lin_b, L0_ffn_si_conv_w, L0_ffn_si_conv_b, L0_ffn_si_gamma, L0_ffn_si_beta, L0_ffn_si_lin_w, L0_ffn_si_lin_b)
    x = x + _L0_attn_b_ref(_layernorm(x, axis=-1), L0_attn_b_wq_w, L0_attn_b_wq_b, L0_attn_b_wk_w, L0_attn_b_wk_b, L0_attn_b_wv_w, L0_attn_b_wv_b)
    x = x + _L0_ffn_ref(_layernorm(x, axis=-1), L0_ffn_weight, L0_ffn_bias, L0_ffn_so_conv_w, L0_ffn_so_conv_b, L0_ffn_so_gamma, L0_ffn_so_beta, L0_ffn_so_lin_w, L0_ffn_so_lin_b, L0_ffn_si_conv_w, L0_ffn_si_conv_b, L0_ffn_si_gamma, L0_ffn_si_beta, L0_ffn_si_lin_w, L0_ffn_si_lin_b)
    return x

_drawn_inputs = setup_inputs


def setup_inputs(seed=0):
    import zlib

    import numpy as np

    out = dict(_drawn_inputs(seed))
    spreads = {'L0_attn_a_bq': (0.0, 0.8),
     'L0_attn_a_bk': (0.0, 0.8),
     'L0_attn_a_bv': (0.0, 0.1),
     'L0_attn_a_bo': (0.0, 0.1),
     'L0_ffn_bias': (0.0, 0.1),
     'L0_ffn_so_conv_b': (0.0, 2.0),
     'L0_ffn_so_gamma': (1.0, 0.6),
     'L0_ffn_so_beta': (0.0, 0.8),
     'L0_ffn_so_lin_b': (0.0, 0.8),
     'L0_ffn_si_conv_b': (0.0, 2.0),
     'L0_ffn_si_gamma': (1.0, 0.6),
     'L0_ffn_si_beta': (0.0, 0.8),
     'L0_ffn_si_lin_b': (0.0, 0.8)}
    factors = {'L0_attn_a_Wq': 8.0,
     'L0_attn_a_Wk': 8.0,
     'L0_attn_a_Wv': 8.0,
     'L0_attn_b_wq_b': 50.908,
     'L0_attn_b_wk_b': 64.0,
     'L0_attn_b_wv_b': 5.551,
     'L0_ffn_so_conv_w': 3.182,
     'L0_ffn_so_lin_w': 2.891,
     'L0_ffn_si_conv_w': 3.186,
     'L0_ffn_si_lin_w': 2.944}
    for name, (base, spread) in spreads.items():
        noise = np.random.default_rng([zlib.crc32(name.encode()), seed]).standard_normal(out[name].shape)
        drawn = base * np.exp(spread * noise) if base else spread * noise
        out[name] = jnp.asarray(drawn.astype(out[name].dtype))
    for name, factor in factors.items():
        out[name] = (out[name] * factor).astype(out[name].dtype)
    return out
```

```python
from contextlib import ExitStack

import concourse.bass as bass
from concourse import mybir

F32 = mybir.dt.float32
BF16 = mybir.dt.bfloat16
ALU = mybir.AluOpType
ACT = mybir.ActivationFunctionType
AX = mybir.AxisListType

P = 128
NSEQ, SEQ, D = 32, 256, 128
QT = SEQ // P
NH, HD = 16, 8
NPAIR = NH // 2
NSLOT = 6
ROWS = NSLOT * HD
DATA = 2 * ROWS
MAXROWS = 6
VW = 32
NG = D // 4
NL = 2 * NG
ROUNDS = 4
NGATE = QT * 2
EPS = 1e-5
LOWEST = -3.0e38
RING = 3
FIRST_LOOPED, LOOP_TRIPS = 4, 9
STEPS = NSEQ + 3


def steps(eng, step):
    for s in range(FIRST_LOOPED):
        step(s, s % RING)
    with eng.Fori(0, LOOP_TRIPS) as trip:
        for r in range(RING):
            step(trip * RING + (FIRST_LOOPED + r), (FIRST_LOOPED + r) % RING)
    for s in range(FIRST_LOOPED + LOOP_TRIPS * RING, STEPS):
        step(s, s % RING)


def live(b):
    return not isinstance(b, int) or 0 <= b < NSEQ


def need(eng, sem, value):
    if isinstance(value, int) and value <= 0:
        return
    eng.wait_ge(sem, value)


def settle(eng, m, sem, value):
    if isinstance(value, int):
        need(eng, sem, value)
        return
    register = eng.compute_val(value)
    eng.wait_ge(m.fills, 1)
    eng.wait_ge(sem, register)


def counter(order, users):
    mine = [e for e in order if (e[0], e[2]) in users]

    def turn(s, what, k=0):
        place = [(e[0], e[2]) for e in mine].index((what, k))
        if isinstance(s, int):
            return (sum(live(i - e[1]) for i in range(s) for e in mine)
                    + sum(live(s - e[1]) for e in mine[:place]))
        start = sum(live(i - e[1]) for i in range(FIRST_LOOPED) for e in mine)
        return (s - FIRST_LOOPED) * len(mine) + (start + place)

    return turn


class Model:
    pass


def program(nc, t, out):
    with ExitStack() as ctx:
        m = Model()

        def sb(name, shape, dt=F32):
            return ctx.enter_context(nc.sbuf_tensor(name, shape, dt))

        def dram(name, shape, dt=F32):
            return nc.dram_tensor(name, shape, dt).ap()

        m.x = sb("x", [P, NSEQ * QT, D])
        m.gate_in = sb("gate_in", [NL, NSEQ * SEQ])
        m.bn_parts = sb("bn_parts", [NL, NSEQ, 6])
        m.ident = sb("ident", [P, P])
        m.ident_bf = sb("ident_bf", [P, P], BF16)
        m.w_qkv_a = sb("w_qkv_a", [P, 3 * D])
        m.b_qkv_a = sb("b_qkv_a", [P, 3 * D])
        m.w_o = sb("w_o", [P, D])
        m.b_o = sb("b_o", [P, D])
        m.rope_a = sb("rope_a", [P, QT, 2, 32])
        m.w_qkv_b = sb("w_qkv_b", [P, 3 * D])
        m.b_qkv_b = sb("b_qkv_b", [P, 3 * D])
        m.rope_b = sb("rope_b", [P, QT, 2, D])
        m.w_conv = sb("w_conv", [P, NL])
        m.norm_gate = sb("norm_gate", [NL, 3])
        m.w_gate = sb("w_gate", [NL + 1, 2 * D])
        m.w_ffn = sb("w_ffn", [P, D])
        m.b_ffn = sb("b_ffn", [P, D])
        m.neg_half = sb("neg_half", [P, QT])

        m.ln_st = sb("ln_st", [P, QT, 6])
        m.ln_mv = sb("ln_mv", [P, QT, 2])
        m.ln_rstd = sb("ln_rstd", [P, QT])
        m.ln2_st = sb("ln2_st", [P, QT, 6])
        m.ln2_mv = sb("ln2_mv", [P, QT, 2])
        m.ln2_rstd = sb("ln2_rstd", [P, QT])
        m.xn = sb("xn", [P, RING, QT, D])
        m.xn2 = sb("xn2", [P, RING, QT, D])
        m.xnT = sb("xnT", [P, SEQ])
        m.xnT2 = sb("xnT2", [P, RING, SEQ])
        m.qk_raw = sb("qk_raw", [P, QT, 2 * D])
        m.v_raw = sb("v_raw", [P, QT, D])
        m.qk = sb("qk", [P, QT, 2 * D])
        m.rot = sb("rot", [P, QT, 2 * D])
        m.qkT = sb("qkT", [P, 2 * SEQ])

        m.stack_hbm = dram("stack_hbm", [2, 2, NSLOT, HD * NPAIR, SEQ], BF16)
        m.nmax_hbm = dram("nmax_hbm", [2, 24, SEQ], BF16)
        m.xn_hbm = dram("xn_hbm", [2, NSEQ, P, QT * D])
        m.xnT_hbm = dram("xnT_hbm", [2, NSEQ, P, SEQ])

        m.consts = ctx.enter_context(nc.semaphore("consts"))
        m.x_first = ctx.enter_context(nc.semaphore("x_first"))
        m.x_all = ctx.enter_context(nc.semaphore("x_all"))
        m.fills = ctx.enter_context(nc.semaphore("fills"))

        tables = [(m.ident, "ident"), (m.ident_bf, "ident_bf"), (m.w_qkv_a, "w_qkv_a"), (m.w_o, "w_o"),
                  (m.rope_a, "rope_a"), (m.w_qkv_b, "w_qkv_b"), (m.rope_b, "rope_b"), (m.w_conv, "w_conv"),
                  (m.norm_gate, "norm_gate"), (m.w_gate, "w_gate"), (m.w_ffn, "w_ffn")]
        rows = [(m.b_qkv_a, "b_qkv_a"), (m.b_o, "b_o"), (m.b_qkv_b, "b_qkv_b"), (m.b_ffn, "b_ffn")]
        m.n_consts = 16 * (len(tables) + len(rows))
        x_dram = t["x"].rearrange("b (q p) d -> p (b q) d", p=P)
        m.out_dram = out.rearrange("b (q p) d -> p b q d", p=P)

        with nc.Block() as block:
            @block.sync
            def _(sp):
                sp.dma_start(m.x[:, 0:8, :], x_dram[:, 0:8, :]).then_inc(m.x_first, 16)
                for dst, name in tables:
                    sp.dma_start(dst[:], t[name]).then_inc(m.consts, 16)
                for dst, name in rows:
                    sp.dma_start(dst[:], t[name].partition_broadcast(P)).then_inc(m.consts, 16)
                sp.dma_start(m.x[:, 8:, :], x_dram[:, 8:, :]).then_inc(m.x_all, 16)

            @block.vector
            def _(dve):
                nc.vector.memset(m.neg_half[:], -0.5).then_inc(m.fills, 1)

        attention_a(nc, m, t)
        for n in range(2):
            gate_norm(nc, m, n)
            feed_forward(nc, m, n)



class Norm:

    def __init__(self, ctx, nc, name):
        self.parts_ok = ctx.enter_context(nc.semaphore(name + "_parts_ok"))
        self.stats_ok = ctx.enter_context(nc.semaphore(name + "_stats_ok"))
        self.eps_ok = ctx.enter_context(nc.semaphore(name + "_eps_ok"))
        self.rstd_ok = ctx.enter_context(nc.semaphore(name + "_rstd_ok"))
        self.xn_ok = ctx.enter_context(nc.semaphore(name + "_xn_ok"))


def norm_stats(nc, dve, m, sems, st, mv, b):
    settle(dve, m, sems.xn_ok, QT * b)
    for qt in range(QT):
        nc.vector.bn_stats(st[:, qt, :], m.x[:, b * QT + qt, :]).then_inc(sems.parts_ok, 1)
    for qt in range(QT):
        settle(dve, m, sems.parts_ok, QT * b + QT)
        nc.vector.bn_aggr(mv[:, qt, :], st[:, qt, :]).then_inc(sems.stats_ok, 1)


def norm_rstd(nc, pool, m, sems, mv, rstd, b):
    settle(pool, m, sems.stats_ok, QT * (b + 1))
    nc.gpsimd.tensor_scalar(rstd[:], mv[:, :, 1], EPS, None, ALU.add).then_inc(sems.eps_ok, 1)
    pool.wait_ge(sems.eps_ok, b + 1)
    nc.gpsimd.tensor_tensor(rstd[:], rstd[:], m.neg_half[:], ALU.pow).then_inc(sems.rstd_ok, 1)


def norm_scale(nc, dve, m, sems, mv, rstd, dst, b):
    dve.wait_ge(sems.rstd_ok, b + 1)
    for qt in range(QT):
        nc.vector.tensor_scalar(dst[:, qt, :], m.x[:, b * QT + qt, :], mv[:, qt, 0:1], rstd[:, qt:qt + 1],
                                ALU.subtract, ALU.mult).then_inc(sems.xn_ok, 1)


def add_bias(nc, pool, m, b_qkv, chain, b):
    nc.gpsimd.tensor_tensor(m.qk[:], m.qk_raw[:], b_qkv[:, 0:2 * D].unsqueeze(1).broadcast_to([P, QT, 2 * D]),
                            ALU.add).then_inc(chain, 1)
    pool.wait_ge(chain, 8 * b + 1)



ORDER_A = [
    ("st", 2, 0), ("pv", 3, 3), ("max", 1, 0), ("mT", 2, 1), ("xnT", 0, 0), ("max", 1, 1), ("max", 1, 2),
    ("st", 2, 1), ("ctx", 3, 1), ("max", 1, 3), ("qk", 0, 0), ("max", 1, 4),
    ("st", 2, 2), ("v", 0, 0), ("max", 1, 5), ("ctxT", 3, 0), ("max", 1, 6),
    ("st", 2, 3), ("pv", 2, 0), ("max", 1, 7), ("qkT", 0, 0), ("max", 1, 8),
    ("st", 2, 4), ("proj", 3, 0), ("max", 1, 9), ("mT", 1, 0), ("max", 1, 10),
    ("st", 2, 5), ("pv", 2, 1), ("max", 1, 11), ("scale2", 3, 0), ("xnT2", 3, 0), ("max", 1, 12),
    ("st", 2, 6), ("max", 1, 13), ("ctx", 2, 0), ("ln", -1, 0), ("max", 1, 14),
    ("st", 2, 7), ("pv", 2, 2), ("conv", 3, 0), ("max", 1, 15), ("scale", -1, 0),
]
MISC_A = [("mT", 1), ("xnT", 0), ("ctx", 1), ("qk", 0), ("v", 0), ("ctxT", 0), ("qkT", 0), ("proj", 0),
          ("mT", 0), ("xnT2", 0), ("ctx", 0), ("conv", 0)]


def attention_a(nc, m, t):
    with ExitStack() as ctx:
        def sb(name, shape, dt=F32):
            return ctx.enter_context(nc.sbuf_tensor(name, shape, dt))

        def psum(name, shape):
            return ctx.enter_context(nc.psum_tensor(name, shape, F32))

        def sem(name):
            return ctx.enter_context(nc.semaphore("a_" + name))

        rest = sb("rest", [P, 2 * SEQ])
        parts = sb("parts", [P, 3, 2 * SEQ], BF16)
        q_stack = sb("q_stack", [P, RING, NPAIR, SEQ], BF16)
        k_stack = sb("k_stack", [P, RING, NH, SEQ], BF16)
        v_aug = sb("v_aug", [P, RING, QT, NH, VW])
        nmax = sb("nmax", [P, 2, QT, 2, 4])
        nmax_rest = sb("nmax_rest", [P, 2, QT, 2, 4])
        nmax_parts = sb("nmax_parts", [P, 2, QT, 2, 3, 4], BF16)
        nmaxT = sb("nmaxT", [24, 2, SEQ], BF16)
        probs = sb("probs", [P, 4, 2, QT, SEQ])
        ctxT_raw = sb("ctxT_raw", [P, 2, 2, SEQ])
        z_inv = sb("z_inv", [P, QT, 8])
        ctx_tok = sb("ctx_tok", [P, QT, D])
        ctxT = sb("ctxT", [P, SEQ])
        xb = sb("xb", [P, QT, D])
        st_bank = psum("st_bank", [P, 2, 2, QT, SEQ])
        s_bank = psum("s_bank", [P, 2, QT, SEQ])
        pv_bank = psum("pv_bank", [P, 2, SEQ])
        misc_bank = psum("misc_bank", [P, 2 * SEQ])
        misc = misc_bank[:]
        misc_bf = misc.bitcast(BF16)
        turn = counter(ORDER_A, MISC_A)

        misc_ps = sem("misc_ps")
        misc_read = sem("misc_read")
        norm, norm2 = Norm(ctx, nc, "a_ln"), Norm(ctx, nc, "a_ln2")
        chain = sem("chain")
        qk_ok = sem("qk_ok")
        v_ok = sem("v_ok")
        cut = sem("cut")
        parts_ok = sem("parts_ok")
        stack_out = sem("stack_out")
        stack_in = sem("stack_in")
        k_clear = sem("k_clear")
        k_ones = sem("k_ones")
        v_fill = sem("v_fill")
        s_ps = sem("s_ps")
        max_ok = sem("max_ok")
        cut_max = sem("cut_max")
        nmax_ok = sem("nmax_ok")
        mT_out = sem("mT_out")
        mT_in = sem("mT_in")
        st_ps = sem("st_ps")
        probs_ok = sem("probs_ok")
        pv_ps = sem("pv_ps")
        pv_ok = sem("pv_ok")
        z_ok = sem("z_ok")
        xb_ok = sem("xb_ok")
        g_ok = sem("g_ok")
        bn_ok = sem("bn_ok")
        kept = sem("kept")

        with nc.Block() as block:
            @block.tensor
            def _(pe):
                pe.wait_ge(m.consts, m.n_consts)
                pe.wait_ge(k_ones, 16 * RING)
                pe.wait_ge(v_fill, 2)

                def step(s, u):
                    for what, lag, k in ORDER_A:
                        b, v = s - lag, (u - lag) % RING
                        if not live(b):
                            continue
                        if (what, k) in MISC_A:
                            n = turn(s, what, k)
                            need(pe, misc_read, n)
                        if what == "st":
                            if k % 4 == 0:
                                pe.wait_ge(mT_in, 16 * (2 * b + k // 4 + 1))
                            need(pe, probs_ok, 8 * b + k - 1)
                            for par in range(2):
                                for kt in range(QT):
                                    mm = nc.tensor.matmul(
                                        st_bank[:, k % 2, par, kt, :],
                                        k_stack[0:DATA + MAXROWS, v, 2 * k + par, kt * P:(kt + 1) * P],
                                        q_stack[0:DATA + MAXROWS, v, k, :], start=True, stop=True)
                            mm.then_inc(st_ps, 1)
                        elif what == "pv":
                            pe.wait_ge(probs_ok, 8 * b + 2 * k + 2)
                            if k % 2 == 0:
                                need(pe, pv_ok, 2 * b + k // 2)
                            if k == 0:
                                pe.wait_ge(v_ok, b + 1)
                                pe.wait_ge(v_fill, 2)
                            for kt in range(QT):
                                for j in range(4):
                                    mm = nc.tensor.matmul(pv_bank[32 * j:32 * j + VW, k % 2, :],
                                                          v_aug[:, v, kt, 4 * k + j, :],
                                                          probs[:, (2 * k + j // 2) % 4, j % 2, kt, :],
                                                          start=(kt == 0), stop=(kt == QT - 1))
                            mm.then_inc(pv_ps, 1)
                        elif what == "max":
                            if k == 0:
                                pe.wait_ge(stack_in, 16 * 4 * (b + 1))
                            need(pe, max_ok, 16 * b + k - 1)
                            for qt in range(QT):
                                mm = nc.tensor.matmul(s_bank[:, k % 2, qt, :],
                                                      q_stack[0:DATA, v, k // 2, qt * P:(qt + 1) * P],
                                                      k_stack[0:DATA, v, k, :], start=True, stop=True)
                            mm.then_inc(s_ps, 1)
                        elif what == "mT":
                            pe.wait_ge(nmax_ok, 2 * (2 * b + k + 1))
                            pe.wait_ge(v_fill, 2)
                            for qt in range(QT):
                                mm = nc.tensor.transpose(misc_bf[0:24, qt * P:(qt + 1) * P],
                                                         nmax_parts[:, k, qt].rearrange("p r c j -> p (r c j)"),
                                                         m.ident_bf[:])
                            mm.then_inc(misc_ps, 1)
                        elif what == "xnT":
                            pe.wait_ge(norm.xn_ok, QT * (b + 1))
                            for qt in range(QT):
                                mm = nc.tensor.transpose(misc[:, qt * P:(qt + 1) * P], m.xn[:, v, qt, :], m.ident[:])
                            mm.then_inc(misc_ps, 1)
                        elif what == "qk":
                            for qt in range(QT):
                                mm = nc.tensor.matmul(misc[:, qt * 2 * D:(qt + 1) * 2 * D], m.xnT[:, qt * P:(qt + 1) * P],
                                                      m.w_qkv_a[:, 0:2 * D], start=True, stop=True)
                            mm.then_inc(misc_ps, 1)
                        elif what == "v":
                            for qt in range(QT):
                                mm = nc.tensor.matmul(misc[:, qt * D:(qt + 1) * D], m.xnT[:, qt * P:(qt + 1) * P],
                                                      m.w_qkv_a[:, 2 * D:], start=True, stop=True)
                            mm.then_inc(misc_ps, 1)
                        elif what == "qkT":
                            pe.wait_ge(qk_ok, b + 1)
                            for i in range(2):
                                for qt in range(QT):
                                    mm = nc.tensor.transpose(misc[:, i * SEQ + qt * P:i * SEQ + (qt + 1) * P],
                                                             m.qk[:, qt, i * D:(i + 1) * D], m.ident[:])
                            mm.then_inc(misc_ps, 1)
                        elif what == "ctx":
                            pe.wait_ge(pv_ok, 2 * b + k + 1)
                            for qt in range(QT):
                                for g in range(2):
                                    mm = nc.tensor.transpose(misc[:, (2 * qt + g) * P:(2 * qt + g + 1) * P],
                                                             ctxT_raw[:, k, g, qt * P:(qt + 1) * P], m.ident[:])
                            mm.then_inc(misc_ps, 1)
                        elif what == "ctxT":
                            for qt in range(QT):
                                mm = nc.tensor.transpose(misc[:, qt * P:(qt + 1) * P], ctx_tok[:, qt, :], m.ident[:])
                            mm.then_inc(misc_ps, 1)
                        elif what == "proj":
                            for qt in range(QT):
                                mm = nc.tensor.matmul(misc[:, qt * D:(qt + 1) * D], ctxT[:, qt * P:(qt + 1) * P],
                                                      m.w_o[:], start=True, stop=True)
                            mm.then_inc(misc_ps, 1)
                        elif what == "xnT2":
                            pe.wait_ge(norm2.xn_ok, QT * (b + 1))
                            for qt in range(QT):
                                mm = nc.tensor.transpose(misc[:, qt * P:(qt + 1) * P], m.xn2[:, v, qt, :], m.ident[:])
                            mm.then_inc(misc_ps, 1)
                        elif what == "conv":
                            pe.wait_ge(misc_read, turn(s, "xnT2") + 1)
                            pe.wait_ge(v_fill, 2)
                            nc.tensor.matmul(misc[0:NL, 0:SEQ], m.w_conv[:], m.xnT2[:, v, :],
                                             start=True, stop=True).then_inc(misc_ps, 1)

                steps(pe, step)

            @block.scalar
            def _(act):
                def step(s, u):
                    for what, lag, k in ORDER_A:
                        b, v = s - lag, (u - lag) % RING
                        if not live(b):
                            continue
                        if (what, k) in MISC_A and what != "ctx" and what != "proj":
                            settle(act, m, misc_ps, turn(s, what, k) + 1)
                        if what == "st":
                            act.wait_ge(st_ps, 8 * b + k + 1)
                            need(act, pv_ps, 4 * b + k // 2 - 1)
                            nc.scalar.activation(probs[:, k % 4].rearrange("p a b c -> p (a b c)"),
                                                 st_bank[:, k % 2].rearrange("p a b c -> p (a b c)"), ACT.Exp,
                                                 scale=HD ** -0.5).then_inc(probs_ok, 1)
                        elif what == "pv" and k % 2 == 1:
                            act.wait_ge(pv_ps, 4 * b + k + 1)
                            nc.scalar.copy(ctxT_raw[:, k // 2], pv_bank[:]).then_inc(pv_ok, 1)
                        elif what == "mT":
                            need(act, mT_out, 16 * (2 * b + k - 1))
                            nc.scalar.copy(nmaxT[:, k], misc_bf[0:24, 0:SEQ]).then_inc(misc_read, 1)
                        elif what == "xnT":
                            nc.scalar.copy(m.xnT[:], misc[:, 0:SEQ]).then_inc(misc_read, 1)
                        elif what == "qk":
                            nc.scalar.copy(m.qk_raw[:].rearrange("p a b -> p (a b)"), misc).then_inc(misc_read, 1)
                        elif what == "v":
                            need(act, v_ok, b)
                            nc.scalar.copy(m.v_raw[:].rearrange("p a b -> p (a b)"), misc[:, 0:QT * D]).then_inc(misc_read, 1)
                        elif what == "qkT":
                            need(act, parts_ok, b)
                            nc.scalar.copy(m.qkT[:], misc).then_inc(misc_read, 1)
                        elif what == "ctxT":
                            nc.scalar.copy(ctxT[:], misc[:, 0:SEQ]).then_inc(misc_read, 1)
                        elif what == "xnT2":
                            need(act, kept, 32 * b)
                            nc.scalar.copy(m.xnT2[:, v, :], misc[:, 0:SEQ]).then_inc(misc_read, 1)
                        elif what == "conv":
                            nc.scalar.activation(m.gate_in[:, bass.ds(b * SEQ, SEQ)], misc[0:NL, 0:SEQ], ACT.Identity,
                                                 bias=m.norm_gate[:, 0:1]).then_inc(misc_read, 1)

                steps(act, step)

            @block.vector
            def _(dve):
                nc.vector.memset(k_stack[:], 0.0).then_inc(k_clear, 1)
                nc.vector.memset(v_aug[:], 0.0).then_inc(v_fill, 1)
                dve.wait_ge(v_fill, 1)
                nc.vector.memset(v_aug[:, :, :, :, HD:HD + 1], 1.0).then_inc(v_fill, 1)
                dve.wait_ge(m.x_first, 16)
                norm_stats(nc, dve, m, norm, m.ln_st, m.ln_mv, 0)
                norm_scale(nc, dve, m, norm, m.ln_mv, m.ln_rstd, m.xn[:, 0], 0)

                def step(s, u):
                    if isinstance(s, int) and s == FIRST_LOOPED - 2:
                        dve.wait_ge(m.x_all, 16)
                    for what, lag, k in ORDER_A:
                        b, v = s - lag, (u - lag) % RING
                        if not live(b):
                            continue
                        if what == "max":
                            dve.wait_ge(s_ps, 16 * b + k + 1)
                            if k % 8 == 0:
                                need(dve, nmax_ok, 2 * (2 * b + k // 8 - 1))
                            nc.vector.tensor_reduce(nmax[:, k // 8, :, k % 2, k // 2 % 4], s_bank[:, k % 2], AX.X,
                                                    ALU.max, negate=True).then_inc(max_ok, 1)
                        elif what == "ctx":
                            dve.wait_ge(misc_ps, turn(s, "ctx", k) + 1)
                            heads = misc.rearrange("p (a h c) -> p a h c", a=QT, c=VW)
                            nc.vector.reciprocal(z_inv[:], heads[:, :, :, HD]).then_inc(z_ok, 1)
                            dve.wait_ge(z_ok, 2 * b + k + 1)
                            nc.vector.tensor_tensor(
                                ctx_tok[:, :, k * D // 2:(k + 1) * D // 2].rearrange("p a (h d) -> p a h d", d=HD),
                                heads[:, :, :, 0:HD], z_inv[:].unsqueeze(3).broadcast_to([P, QT, 8, HD]),
                                ALU.mult).then_inc(misc_read, 1)
                        elif what == "proj":
                            dve.wait_ge(misc_ps, turn(s, "proj") + 1)
                            dve.wait_ge(xb_ok, b + 1)
                            nc.vector.tensor_tensor(m.x[:, bass.ds(b * QT, QT), :],
                                                    misc[:, 0:QT * D].rearrange("p (a b) -> p a b", a=QT), xb[:],
                                                    ALU.add).then_inc(misc_read, 1)
                            settle(dve, m, misc_read, turn(s, "proj") + 1)
                            norm_stats(nc, dve, m, norm2, m.ln2_st, m.ln2_mv, b)
                        elif what == "scale2":
                            need(dve, kept, 32 * b)
                            norm_scale(nc, dve, m, norm2, m.ln2_mv, m.ln2_rstd, m.xn2[:, v], b)
                        elif what == "ln":
                            norm_stats(nc, dve, m, norm, m.ln_st, m.ln_mv, b)
                        elif what == "scale":
                            norm_scale(nc, dve, m, norm, m.ln_mv, m.ln_rstd, m.xn[:, v], b)
                        elif what == "conv":
                            settle(dve, m, misc_read, turn(s, "conv") + 1)
                            nc.vector.bn_stats(m.bn_parts[:, b, :], m.gate_in[:, bass.ds(b * SEQ, SEQ)]).then_inc(bn_ok, 1)

                steps(dve, step)

            @block.gpsimd
            def _(pool):
                pool.wait_ge(m.consts, m.n_consts)
                norm_rstd(nc, pool, m, norm, m.ln_mv, m.ln_rstd, 0)

                def cut_maxima(b, k):
                    settle(pool, m, max_ok, 16 * b + 8 * k + 8)
                    links = 6 * (2 * b + k)
                    for i, src in enumerate((nmax, nmax_rest)):
                        for qt in range(QT):
                            nc.gpsimd.tensor_copy(nmax_parts[:, k, qt, :, i, :], src[:, k, qt]).then_inc(cut_max, 1)
                        pool.wait_ge(cut_max, links + 4 * i + 2)
                        for qt in range(QT):
                            dst, done = ((nmax_rest[:, k, qt], cut_max) if i == 0 else
                                         (nmax_parts[:, k, qt, :, 2, :], nmax_ok))
                            nc.gpsimd.tensor_tensor(dst, src[:, k, qt], nmax_parts[:, k, qt, :, i, :],
                                                    ALU.subtract).then_inc(done, 1)
                        if i == 0:
                            settle(pool, m, cut_max, links + 4)

                def step(s, u):
                    for what, lag, k in ORDER_A:
                        b, v = s - lag, (u - lag) % RING
                        if not live(b):
                            continue
                        if what == "ln":
                            norm_rstd(nc, pool, m, norm, m.ln_mv, m.ln_rstd, b)
                        elif what == "proj":
                            norm_rstd(nc, pool, m, norm2, m.ln2_mv, m.ln2_rstd, b)
                        elif what == "ctxT":
                            nc.gpsimd.tensor_tensor(xb[:], m.x[:, bass.ds(b * QT, QT), :],
                                                    m.b_o[:].unsqueeze(1).broadcast_to([P, QT, D]),
                                                    ALU.add).then_inc(xb_ok, 1)
                        elif what == "mT":
                            cut_maxima(b, k)
                        elif what == "qk":
                            pool.wait_ge(misc_read, turn(s, "qk") + 1)
                            add_bias(nc, pool, m, m.b_qkv_a, chain, b)
                            rows = m.qk[:].rearrange("p a (q r) -> p a q r", r=D // 2)
                            turned = m.rot[:].rearrange("p a (q r) -> p a q r", r=D // 2)
                            for qt in range(QT):
                                both = rows[:, qt, :, 2 * NPAIR:6 * NPAIR]
                                pairs = both.rearrange("p q (c e t) -> p q c e t", c=2, e=2)
                                term = turned[:, qt, :, 2 * NPAIR:6 * NPAIR]
                                terms = term.rearrange("p q (c e t) -> p q c e t", c=2, e=2)
                                cos = m.rope_a[:, qt, 0, :].unsqueeze(1).broadcast_to([P, 4, 32])
                                sin = m.rope_a[:, qt, 1, :].rearrange("p (c e t) -> p c e t", c=2, e=2)
                                for e in range(2):
                                    nc.gpsimd.tensor_tensor(terms[:, :, :, e, :], pairs[:, :, :, 1 - e, :],
                                                            sin[:, :, e, :].unsqueeze(1).broadcast_to([P, 4, 2, NPAIR]),
                                                            ALU.mult).then_inc(chain, 1)
                                pool.wait_ge(chain, 8 * b + 3 + 4 * qt)
                                nc.gpsimd.tensor_tensor(both, both, cos, ALU.mult).then_inc(chain, 1)
                                pool.wait_ge(chain, 8 * b + 4 + 4 * qt)
                                nc.gpsimd.tensor_tensor(both, both, term, ALU.add)\
                                    .then_inc(qk_ok if qt == QT - 1 else chain, 1)
                        elif what == "v":
                            pool.wait_ge(misc_read, turn(s, "v") + 1)
                            pool.wait_ge(v_fill, 2)
                            need(pool, pv_ps, 4 * (b - 2))
                            nc.gpsimd.tensor_tensor(v_aug[:, v, :, :, 0:HD], m.v_raw[:].rearrange("p a (h d) -> p a h d", d=HD),
                                                    m.b_qkv_a[:, 2 * D:].rearrange("p (h d) -> p h d", d=HD).unsqueeze(1)
                                                    .broadcast_to([P, QT, NH, HD]), ALU.add).then_inc(v_ok, 1)
                        elif what == "qkT":
                            pool.wait_ge(misc_read, turn(s, "qkT") + 1)
                            settle(pool, m, stack_out, 16 * 12 * b)
                            nc.gpsimd.tensor_copy(parts[:, 0], m.qkT[:]).then_inc(cut, 1)
                            pool.wait_ge(cut, 3 * b + 1)
                            nc.gpsimd.tensor_tensor(rest[:], m.qkT[:], parts[:, 0], ALU.subtract).then_inc(cut, 1)
                            settle(pool, m, cut, 3 * b + 2)
                            nc.gpsimd.tensor_copy(parts[:, 1], rest[:]).then_inc(cut, 1)
                            pool.wait_ge(cut, 3 * b + 3)
                            nc.gpsimd.tensor_tensor(parts[:, 2], rest[:], parts[:, 1], ALU.subtract).then_inc(parts_ok, 1)

                steps(pool, step)

            @block.sync
            def _(sp):
                sp.wait_ge(k_clear, 1)
                for r in range(RING):
                    sp.dma_start(k_stack[DATA:DATA + MAXROWS, r], t["k_ones"]).then_inc(k_ones, 16)

                def step(s, u):
                    for what, lag, k in ORDER_A:
                        b, v = s - lag, (u - lag) % RING
                        if not live(b):
                            continue
                        if what == "mT":
                            settle(sp, m, misc_read, turn(s, "mT", k) + 1)
                            settle(sp, m, mT_in, 16 * (2 * b + k))
                            sp.dma_start(m.nmax_hbm[k], nmaxT[:, k]).then_inc(mT_out, 16)
                            settle(sp, m, mT_out, 16 * (2 * b + k + 1))
                            sp.dma_start(q_stack[DATA:DATA + MAXROWS, v, 4 * k:4 * k + 4, :],
                                         m.nmax_hbm[k].rearrange("(r t) n -> r t n", t=4)).then_inc(mT_in, 16)
                        elif what == "qkT":
                            settle(sp, m, parts_ok, b + 1)
                            for i in range(2):
                                for par in range(2):
                                    half = parts[par * 64:(par + 1) * 64, :, i * SEQ:(i + 1) * SEQ]
                                    dst = m.stack_hbm[i, par].rearrange("s r n -> r s n")
                                    for at, n, part in ((0, 3, 0), (3, 2, 1), (5, 1, 2)):
                                        src = half[:, 0:n] if i == 0 else half[:, part:part + 1].broadcast_to([64, n, SEQ])
                                        sp.dma_start(dst[:, at:at + n], src).then_inc(stack_out, 16)
                            settle(sp, m, stack_out, 16 * 12 * (b + 1))
                            for i in range(2):
                                for par in range(2):
                                    src = m.stack_hbm[i, par].rearrange("s (d t) n -> (s d) t n", t=NPAIR)
                                    dst = (q_stack[par * ROWS:(par + 1) * ROWS, v] if i == 0 else
                                           k_stack[par * ROWS:(par + 1) * ROWS, v]
                                           .rearrange("p (t r) n -> p r t n", r=2)[:, par])
                                    sp.dma_start(dst, src).then_inc(stack_in, 16)
                        elif what == "conv":
                            settle(sp, m, kept, 32 * b)
                            settle(sp, m, misc_read, turn(s, "conv") + 1)
                            sp.dma_start(m.xn_hbm[0, b], m.xn2[:, v].rearrange("p a b -> p (a b)")).then_inc(kept, 16)
                            sp.dma_start(m.xnT_hbm[0, b], m.xnT2[:, v, :]).then_inc(kept, 16)

                steps(sp, step)
                sp.wait_ge(kept, 32 * NSEQ)



def gate_norm(nc, m, n):
    with ExitStack() as ctx:
        mv = ctx.enter_context(nc.sbuf_tensor(f"gn{n}_mv", [NL, 2], F32))
        w = ctx.enter_context(nc.sbuf_tensor(f"gn{n}_w", [NL, 4], F32))
        mean_ok = ctx.enter_context(nc.semaphore(f"gn{n}_mean_ok"))
        link = ctx.enter_context(nc.semaphore(f"gn{n}_link"))
        with nc.Block() as block:
            @block.vector
            def _(dve):
                nc.vector.bn_aggr(mv[:], m.bn_parts[:].rearrange("p a b -> p (a b)")).then_inc(mean_ok, 1)

            @block.gpsimd
            def _(pool):
                pool.wait_ge(mean_ok, 1)
                nc.gpsimd.tensor_scalar(w[:, 0:1], mv[:, 1:2], EPS, None, ALU.add).then_inc(link, 1)
                pool.wait_ge(link, 1)
                nc.gpsimd.tensor_tensor(w[:, 0:1], w[:, 0:1], m.neg_half[0:NL, 0:1], ALU.pow).then_inc(link, 1)
                pool.wait_ge(link, 2)
                nc.gpsimd.tensor_tensor(w[:, 1:2], w[:, 0:1], m.norm_gate[:, 1:2], ALU.mult).then_inc(link, 1)
                pool.wait_ge(link, 3)
                nc.gpsimd.tensor_tensor(w[:, 2:3], mv[:, 0:1], w[:, 1:2], ALU.mult).then_inc(link, 1)
                pool.wait_ge(link, 4)
                nc.gpsimd.tensor_tensor(w[:, 3:4], m.norm_gate[:, 2:3], w[:, 2:3], ALU.subtract).then_inc(link, 1)

            @block.scalar
            def _(act):
                act.wait_ge(link, 5)
                for i in range(4):
                    piece = m.gate_in[:, i * NSEQ * SEQ // 4:(i + 1) * NSEQ * SEQ // 4]
                    nc.scalar.activation(piece, piece, ACT.Gelu, bias=w[:, 3:4], scale=w[:, 1:2])



ORDER_F = [
    ("load", -1, 0), ("logits", 0, 0), ("full", 0, 0), ("probs", 3, 0), ("gates", 1, 0),
    ("top", 0, 0), ("top", 0, 1), ("xnT", 2, 0), ("xgT", 1, 0), ("probsT", 3, 0),
    ("top", 0, 2), ("top", 0, 3), ("exps", 0, 0), ("qk", 2, 0), ("top", 0, 4), ("o", 1, 0),
    ("pv", 3, 0), ("top", 0, 5), ("v", 2, 0), ("top", 0, 6), ("top", 0, 7), ("exps", 0, 1), ("scale", 1, 0),
    ("top", 0, 8), ("scale2", 3, 0), ("xnT2", 3, 0), ("qkT", 2, 0), ("top", 0, 9), ("top", 0, 10),
    ("top", 0, 11), ("exps", 0, 2), ("s", 2, 0), ("top", 0, 12), ("conv", 3, 0), ("top", 0, 13),
    ("top", 0, 14), ("top", 0, 15), ("exps", 0, 3),
]
ATTENTION = ("probs", "xnT", "probsT", "qk", "pv", "v", "scale", "scale2", "xnT2", "qkT", "s", "conv")
GATE_BANK = [("xgT", 0), ("o", 0)]
PROJ_BANK = [("xnT", 0), ("qk", 0), ("v", 0), ("qkT", 0)]
ATT_BANK = [("probsT", 0), ("pv", 0), ("s", 0)]
TAIL_BANK = [("xnT2", 0), ("conv", 0)]
LOGIT_BANK = [("logits", 0)]
FULL_BANK = [("full", 0)]


def feed_forward(nc, m, n):
    with_attention = n == 0
    order = [e for e in ORDER_F if with_attention or e[0] not in ATTENTION]
    with ExitStack() as ctx:
        def sb(name, shape, dt=F32):
            return ctx.enter_context(nc.sbuf_tensor(f"f{n}_{name}", shape, dt))

        def psum(name, shape):
            return ctx.enter_context(nc.psum_tensor(f"f{n}_{name}", shape, F32))

        def sem(name):
            return ctx.enter_context(nc.semaphore(f"f{n}_{name}"))

        xn_f = sb("xn_f", [P, RING, QT, D])
        xnT_f = sb("xnT_f", [P, RING, SEQ])
        xa = sb("xa", [NL + 1, RING, SEQ])
        logit = sb("logit", [P, QT, 2 * D])
        left = sb("left", [P, QT, 2 * D])
        top8 = sb("top8", [P, NGATE, ROUNDS, 8])
        neg_top = sb("neg_top", [P, NGATE])
        e_all = sb("e_all", [P, QT, 2 * D])
        e_left = sb("e_left", [P, QT, 2 * D])
        z = sb("z", [P, NGATE])
        z_left = sb("z_left", [P, NGATE])
        z_inv = sb("z_inv", [P, NGATE])
        gates = sb("gates", [P, QT, 2 * D])
        full_s = sb("full_s", [P, RING, QT, D])
        gated = sb("gated", [P, QT, D])
        xg = sb("xg", [P, QT, D])
        xgT = sb("xgT", [P, SEQ])
        xb = sb("xb", [P, QT, D])
        logit_bank = psum("logit_bank", [P, QT * 2 * D])
        full_bank = psum("full_bank", [P, QT * D])
        gate_bank = psum("gate_bank", [P, SEQ])

        logit_ps, logit_read = sem("logit_ps"), sem("logit_read")
        full_ps, full_read = sem("full_ps"), sem("full_read")
        gate_ps, gate_read = sem("gate_ps"), sem("gate_read")
        loaded = sem("loaded")
        ones_ok = sem("ones_ok")
        top_ok = sem("top_ok")
        neg_ok = sem("neg_ok")
        exps_ok = sem("exps_ok")
        z_ok = sem("z_ok")
        gates_ok = sem("gates_ok")
        gated_ok = sem("gated_ok")
        xb_ok = sem("xb_ok")
        x_ok = sem("x_ok")
        turn = {k: counter(order, bank) for k, bank in (("logit", LOGIT_BANK), ("full", FULL_BANK), ("gate", GATE_BANK))}

        if with_attention:
            nmax = sb("nmax", [P, QT])
            nmax_s = sb("nmax_s", [P, QT])
            v_b = sb("v_b", [P, RING, QT, D])
            prob = sb("prob", [P, QT, SEQ])
            row_sum = sb("row_sum", [P, QT])
            row_inv = sb("row_inv", [P, QT])
            probT = sb("probT", [P, QT * SEQ])
            proj_bank = psum("proj_bank", [P, QT * 2 * D])
            att_bank = psum("att_bank", [P, QT * SEQ])
            tail_bank = psum("tail_bank", [P, SEQ])
            proj_ps, proj_read = sem("proj_ps"), sem("proj_read")
            att_ps, att_read = sem("att_ps"), sem("att_read")
            tail_ps, tail_read = sem("tail_ps"), sem("tail_read")
            norm, norm2 = Norm(ctx, nc, f"f{n}_ln"), Norm(ctx, nc, f"f{n}_ln2")
            chain = sem("chain")
            qk_ok = sem("qk_ok")
            v_ok = sem("v_ok")
            max_ok = sem("max_ok")
            nmax_ok = sem("nmax_ok")
            row_ok = sem("row_ok")
            x3_ok = sem("x3_ok")
            bn_ok = sem("bn_ok")
            kept = sem("kept")
            turn.update({k: counter(order, bank) for k, bank in (("proj", PROJ_BANK), ("att", ATT_BANK), ("tail", TAIL_BANK))})
        else:
            stored = sem("stored")

        def row(tensor, g):
            return tensor[:, g // 2, (g % 2) * D:(g % 2 + 1) * D]

        with nc.Block() as block:
            @block.tensor
            def _(pe):
                pe.wait_ge(ones_ok, 1)

                def step(s, u):
                    for what, lag, k in order:
                        b, v = s - lag, (u - lag) % RING
                        if not live(b):
                            continue
                        if what == "logits":
                            pe.wait_ge(loaded, 48 * (b + 1))
                            need(pe, logit_read, turn["logit"](s, what))
                            for qt in range(QT):
                                mm = nc.tensor.matmul(logit_bank[:, qt * 2 * D:(qt + 1) * 2 * D],
                                                      xa[:, v, qt * P:(qt + 1) * P], m.w_gate[:], start=True, stop=True)
                            mm.then_inc(logit_ps, 1)
                        elif what == "full":
                            need(pe, full_read, turn["full"](s, what))
                            for qt in range(QT):
                                mm = nc.tensor.matmul(full_bank[:, qt * D:(qt + 1) * D],
                                                      xnT_f[:, v, qt * P:(qt + 1) * P], m.w_ffn[:], start=True, stop=True)
                            mm.then_inc(full_ps, 1)
                        elif what == "xgT":
                            pe.wait_ge(gated_ok, NGATE * (b + 1))
                            need(pe, gate_read, turn["gate"](s, what))
                            for qt in range(QT):
                                mm = nc.tensor.transpose(gate_bank[:, qt * P:(qt + 1) * P], xg[:, qt, :], m.ident[:])
                            mm.then_inc(gate_ps, 1)
                        elif what == "o":
                            pe.wait_ge(gate_read, turn["gate"](s, what))
                            for qt in range(QT):
                                mm = nc.tensor.matmul(gate_bank[:, qt * D:(qt + 1) * D], xgT[:, qt * P:(qt + 1) * P],
                                                      m.w_ffn[:], start=True, stop=True)
                            mm.then_inc(gate_ps, 1)
                        elif what == "xnT":
                            pe.wait_ge(norm.xn_ok, QT * (b + 1))
                            need(pe, proj_read, turn["proj"](s, what))
                            for qt in range(QT):
                                mm = nc.tensor.transpose(proj_bank[:, qt * P:(qt + 1) * P], m.xn[:, v, qt, :], m.ident[:])
                            mm.then_inc(proj_ps, 1)
                        elif what == "qk":
                            pe.wait_ge(proj_read, turn["proj"](s, what))
                            for qt in range(QT):
                                mm = nc.tensor.matmul(proj_bank[:, qt * 2 * D:(qt + 1) * 2 * D],
                                                      m.xnT[:, qt * P:(qt + 1) * P], m.w_qkv_b[:, 0:2 * D], start=True, stop=True)
                            mm.then_inc(proj_ps, 1)
                        elif what == "v":
                            pe.wait_ge(proj_read, turn["proj"](s, what))
                            for qt in range(QT):
                                mm = nc.tensor.matmul(proj_bank[:, qt * D:(qt + 1) * D],
                                                      m.xnT[:, qt * P:(qt + 1) * P], m.w_qkv_b[:, 2 * D:], start=True, stop=True)
                            mm.then_inc(proj_ps, 1)
                        elif what == "qkT":
                            pe.wait_ge(qk_ok, b + 1)
                            pe.wait_ge(proj_read, turn["proj"](s, what))
                            for i in range(2):
                                for qt in range(QT):
                                    mm = nc.tensor.transpose(proj_bank[:, i * SEQ + qt * P:i * SEQ + (qt + 1) * P],
                                                             m.qk[:, qt, i * D:(i + 1) * D], m.ident[:])
                            mm.then_inc(proj_ps, 1)
                        elif what == "s":
                            pe.wait_ge(proj_read, turn["proj"](s, "qkT") + 1)
                            need(pe, att_read, turn["att"](s, what))
                            for qt in range(QT):
                                mm = nc.tensor.matmul(att_bank[:, qt * SEQ:(qt + 1) * SEQ], m.qkT[:, qt * P:(qt + 1) * P],
                                                      m.qkT[:, SEQ:2 * SEQ], start=True, stop=True)
                            mm.then_inc(att_ps, 1)
                        elif what == "probsT":
                            pe.wait_ge(att_read, turn["att"](s, what))
                            for kt in range(QT):
                                for qt in range(QT):
                                    mm = nc.tensor.transpose(att_bank[:, kt * SEQ + qt * P:kt * SEQ + (qt + 1) * P],
                                                             prob[:, qt, kt * P:(kt + 1) * P], m.ident[:])
                            mm.then_inc(att_ps, 1)
                        elif what == "pv":
                            pe.wait_ge(att_read, turn["att"](s, what))
                            pe.wait_ge(v_ok, b + 1)
                            for qt in range(QT):
                                for kt in range(QT):
                                    mm = nc.tensor.matmul(att_bank[:, qt * D:(qt + 1) * D],
                                                          probT[:, kt * SEQ + qt * P:kt * SEQ + (qt + 1) * P],
                                                          v_b[:, v, kt, :], start=(kt == 0), stop=(kt == QT - 1))
                            mm.then_inc(att_ps, 1)
                        elif what == "xnT2":
                            pe.wait_ge(norm2.xn_ok, QT * (b + 1))
                            need(pe, tail_read, turn["tail"](s, what))
                            for qt in range(QT):
                                mm = nc.tensor.transpose(tail_bank[:, qt * P:(qt + 1) * P], m.xn2[:, v, qt, :], m.ident[:])
                            mm.then_inc(tail_ps, 1)
                        elif what == "conv":
                            pe.wait_ge(tail_read, turn["tail"](s, what))
                            pe.wait_ge(ones_ok, 1)
                            nc.tensor.matmul(tail_bank[0:NL, :], m.w_conv[:], m.xnT2[:, v, :],
                                             start=True, stop=True).then_inc(tail_ps, 1)

                steps(pe, step)

            @block.scalar
            def _(act):
                def step(s, u):
                    for what, lag, k in order:
                        b, v = s - lag, (u - lag) % RING
                        if not live(b):
                            continue
                        if what == "logits":
                            act.wait_ge(logit_ps, turn["logit"](s, what) + 1)
                            need(act, exps_ok, NGATE * b)
                            nc.scalar.copy(logit[:].rearrange("p a b -> p (a b)"), logit_bank[:]).then_inc(logit_read, 1)
                        elif what == "full":
                            act.wait_ge(full_ps, turn["full"](s, what) + 1)
                            nc.scalar.copy(full_s[:, v].rearrange("p a b -> p (a b)"), full_bank[:]).then_inc(full_read, 1)
                        elif what == "exps":
                            act.wait_ge(neg_ok, NGATE * b + k + 1)
                            need(act, gates_ok, b)
                            nc.scalar.activation(row(e_all, k), row(logit, k), ACT.Exp, bias=neg_top[:, k:k + 1],
                                                 accum_out=z[:, k:k + 1])
                            act.wait_ge(top_ok, 8 * (NGATE * b + k + 1))
                            nc.scalar.activation(row(e_left, k), row(left, k), ACT.Exp, bias=neg_top[:, k:k + 1])\
                                .then_inc(exps_ok, 1)
                        elif what == "xgT":
                            act.wait_ge(gate_ps, turn["gate"](s, what) + 1)
                            nc.scalar.copy(xgT[:], gate_bank[:]).then_inc(gate_read, 1)
                        elif what == "xnT":
                            act.wait_ge(proj_ps, turn["proj"](s, what) + 1)
                            nc.scalar.copy(m.xnT[:], proj_bank[:, 0:SEQ]).then_inc(proj_read, 1)
                        elif what == "qk":
                            act.wait_ge(proj_ps, turn["proj"](s, what) + 1)
                            nc.scalar.copy(m.qk_raw[:].rearrange("p a b -> p (a b)"), proj_bank[:]).then_inc(proj_read, 1)
                        elif what == "v":
                            act.wait_ge(proj_ps, turn["proj"](s, what) + 1)
                            need(act, v_ok, b)
                            nc.scalar.copy(m.v_raw[:].rearrange("p a b -> p (a b)"), proj_bank[:, 0:QT * D]).then_inc(proj_read, 1)
                        elif what == "qkT":
                            act.wait_ge(proj_ps, turn["proj"](s, what) + 1)
                            nc.scalar.copy(m.qkT[:], proj_bank[:]).then_inc(proj_read, 1)
                        elif what == "probs":
                            act.wait_ge(nmax_ok, b + 1)
                            need(act, row_ok, b)
                            for qt in range(QT):
                                e = nc.scalar.activation(prob[:, qt, :], att_bank[:, qt * SEQ:(qt + 1) * SEQ], ACT.Exp,
                                                         bias=nmax_s[:, qt:qt + 1], scale=D ** -0.5,
                                                         accum_out=row_sum[:, qt:qt + 1])
                            e.then_inc(att_read, 1)
                        elif what == "probsT":
                            act.wait_ge(att_ps, turn["att"](s, what) + 1)
                            nc.scalar.copy(probT[:], att_bank[:]).then_inc(att_read, 1)
                        elif what == "xnT2":
                            act.wait_ge(tail_ps, turn["tail"](s, what) + 1)
                            need(act, kept, 32 * b)
                            nc.scalar.copy(m.xnT2[:, v, :], tail_bank[:]).then_inc(tail_read, 1)
                        elif what == "conv":
                            settle(act, m, tail_ps, turn["tail"](s, what) + 1)
                            need(act, loaded, 48 * (b + 1))
                            nc.scalar.activation(m.gate_in[:, bass.ds(b * SEQ, SEQ)], tail_bank[0:NL, :], ACT.Identity,
                                                 bias=m.norm_gate[:, 0:1]).then_inc(tail_read, 1)

                steps(act, step)

            @block.vector
            def _(dve):
                nc.vector.memset(xa[NL:NL + 1], 1.0).then_inc(ones_ok, 1)

                def step(s, u):
                    for what, lag, k in order:
                        b, v = s - lag, (u - lag) % RING
                        if not live(b):
                            continue
                        if what == "top":
                            g, r = k // ROUNDS, k % ROUNDS
                            links = 8 * NGATE * b + 2 * k
                            if k == 0:
                                dve.wait_ge(logit_read, turn["logit"](s, "logits") + 1)
                            if r == 0:
                                need(dve, exps_ok, NGATE * (b - 1) + g + 1)
                            src = row(logit if r == 0 else left, g)
                            settle(dve, m, top_ok, links)
                            nc.vector.max(top8[:, g, r, :], src).then_inc(top_ok, 1)
                            settle(dve, m, top_ok, links + 1)
                            nc.vector.match_replace(row(left, g), top8[:, g, r, :], src, LOWEST).then_inc(top_ok, 1)
                        elif what == "gates":
                            dve.wait_ge(exps_ok, NGATE * (b + 1))
                            nc.vector.reciprocal(z_inv[:], z[:]).then_inc(z_ok, 1)
                            dve.wait_ge(z_ok, b + 1)
                            dve.wait_ge(gates_ok, b + 1)
                            for qt in range(QT):
                                for i, (dst, other) in enumerate(((gated, full_s), (xg, xn_f))):
                                    g = 2 * qt + i
                                    nc.vector.scalar_tensor_tensor(out=dst[:, qt, :], in0=row(gates, g),
                                                                   scalar=z_inv[:, g:g + 1], in1=other[:, v, qt, :],
                                                                   op0=ALU.mult, op1=ALU.mult).then_inc(gated_ok, 1)
                        elif what == "o":
                            dve.wait_ge(gate_ps, turn["gate"](s, what) + 1)
                            dve.wait_ge(xb_ok, 2 * (b + 1))
                            nc.vector.tensor_tensor(m.x[:, bass.ds(b * QT, QT), :],
                                                    gate_bank[:].rearrange("p (a b) -> p a b", a=QT), xb[:],
                                                    ALU.add).then_inc(gate_read, 1)
                            if with_attention:
                                settle(dve, m, gate_read, turn["gate"](s, what) + 1)
                                norm_stats(nc, dve, m, norm, m.ln_st, m.ln_mv, b)
                        elif what == "scale":
                            norm_scale(nc, dve, m, norm, m.ln_mv, m.ln_rstd, m.xn[:, v], b)
                        elif what == "s":
                            dve.wait_ge(att_ps, turn["att"](s, what) + 1)
                            nc.vector.tensor_reduce(nmax[:], att_bank[:].rearrange("p (a b) -> p a b", a=QT), AX.X, ALU.max,
                                                    negate=True).then_inc(max_ok, 1)
                        elif what == "pv":
                            dve.wait_ge(att_ps, turn["att"](s, what) + 1)
                            nc.vector.reciprocal(row_inv[:], row_sum[:]).then_inc(row_ok, 1)
                            dve.wait_ge(row_ok, b + 1)
                            for qt in range(QT):
                                x = m.x[:, b * QT + qt, :]
                                nc.vector.scalar_tensor_tensor(out=x, in0=att_bank[:, qt * D:(qt + 1) * D],
                                                               scalar=row_inv[:, qt:qt + 1], in1=x, op0=ALU.mult,
                                                               op1=ALU.add).then_inc(x3_ok if qt < QT - 1 else att_read, 1)
                            settle(dve, m, x3_ok, b + 1)
                            dve.wait_ge(att_read, turn["att"](s, what) + 1)
                            norm_stats(nc, dve, m, norm2, m.ln2_st, m.ln2_mv, b)
                        elif what == "scale2":
                            need(dve, kept, 32 * b)
                            norm_scale(nc, dve, m, norm2, m.ln2_mv, m.ln2_rstd, m.xn2[:, v], b)
                        elif what == "conv":
                            settle(dve, m, tail_read, turn["tail"](s, what) + 1)
                            nc.vector.bn_stats(m.bn_parts[:, b, :], m.gate_in[:, bass.ds(b * SEQ, SEQ)]).then_inc(bn_ok, 1)

                steps(dve, step)

            @block.gpsimd
            def _(pool):
                def step(s, u):
                    for what, lag, k in order:
                        b, v = s - lag, (u - lag) % RING
                        if not live(b):
                            continue
                        if what == "gates":
                            pool.wait_ge(exps_ok, NGATE * (b + 1))
                            need(pool, gated_ok, NGATE * b)
                            nc.gpsimd.tensor_tensor(gates[:], e_all[:], e_left[:], ALU.subtract).then_inc(gates_ok, 1)
                            need(pool, gate_read, turn["gate"](s, "xgT"))
                            nc.gpsimd.tensor_tensor(xb[:], m.x[:, bass.ds(b * QT, QT), :],
                                                    m.b_ffn[:].unsqueeze(1).broadcast_to([P, QT, D]),
                                                    ALU.add).then_inc(xb_ok, 1)
                        elif what == "xgT":
                            pool.wait_ge(gated_ok, NGATE * (b + 1))
                            pool.wait_ge(xb_ok, 2 * b + 1)
                            nc.gpsimd.tensor_tensor(xb[:], xb[:], gated[:], ALU.add).then_inc(xb_ok, 1)
                        elif what == "top" and k % ROUNDS == 0:
                            g = k // ROUNDS
                            settle(pool, m, exps_ok, NGATE * (b - 1) + g + 1)
                            settle(pool, m, top_ok, 8 * NGATE * b + 2 * k + 1)
                            nc.gpsimd.tensor_scalar(neg_top[:, g:g + 1], top8[:, g, 0, 0:1], -1.0, None,
                                                    ALU.mult).then_inc(neg_ok, 1)
                        elif what == "o" and with_attention:
                            norm_rstd(nc, pool, m, norm, m.ln_mv, m.ln_rstd, b)
                        elif what == "pv":
                            norm_rstd(nc, pool, m, norm2, m.ln2_mv, m.ln2_rstd, b)
                        elif what == "qk":
                            pool.wait_ge(proj_read, turn["proj"](s, what) + 1)
                            add_bias(nc, pool, m, m.b_qkv_b, chain, b)
                            for qt in range(QT):
                                both = m.qk[:, qt, :].rearrange("p (q r) -> p q r", q=2)
                                term = m.rot[:, qt, :].rearrange("p (q r) -> p q r", q=2)
                                pairs = m.qk[:, qt, :].rearrange("p (q f e) -> p q f e", q=2, e=2)
                                terms = m.rot[:, qt, :].rearrange("p (q f e) -> p q f e", q=2, e=2)
                                sin = m.rope_b[:, qt, 1, :].rearrange("p (f e) -> p f e", e=2)
                                for e in range(2):
                                    nc.gpsimd.tensor_tensor(terms[:, :, :, e], pairs[:, :, :, 1 - e],
                                                            sin[:, :, e].unsqueeze(1).broadcast_to([P, 2, D // 2]),
                                                            ALU.mult).then_inc(chain, 1)
                                pool.wait_ge(chain, 8 * b + 3 + 4 * qt)
                                nc.gpsimd.tensor_tensor(both, both, m.rope_b[:, qt, 0, :].unsqueeze(1).broadcast_to([P, 2, D]),
                                                        ALU.mult).then_inc(chain, 1)
                                pool.wait_ge(chain, 8 * b + 4 + 4 * qt)
                                nc.gpsimd.tensor_tensor(both, both, term, ALU.add)\
                                    .then_inc(qk_ok if qt == QT - 1 else chain, 1)
                        elif what == "v":
                            pool.wait_ge(proj_read, turn["proj"](s, what) + 1)
                            nc.gpsimd.tensor_tensor(v_b[:, v], m.v_raw[:],
                                                    m.b_qkv_b[:, 2 * D:].unsqueeze(1).broadcast_to([P, QT, D]),
                                                    ALU.add).then_inc(v_ok, 1)
                        elif what == "s":
                            settle(pool, m, att_read, turn["att"](s, what))
                            settle(pool, m, max_ok, b + 1)
                            nc.gpsimd.tensor_scalar(nmax_s[:], nmax[:], D ** -0.5, None, ALU.mult).then_inc(nmax_ok, 1)

                steps(pool, step)

            @block.sync
            def _(sp):
                def load(b, v):
                    settle(sp, m, loaded, 48 * b)
                    settle(sp, m, gated_ok, NGATE * (b - 2))
                    sp.dma_start(xa[0:NL, v, :], m.gate_in[:, bass.ds(b * SEQ, SEQ)]).then_inc(loaded, 16)
                    sp.dma_start(xnT_f[:, v, :], m.xnT_hbm[n, b]).then_inc(loaded, 16)
                    sp.dma_start(xn_f[:, v].rearrange("p a b -> p (a b)"), m.xn_hbm[n, b]).then_inc(loaded, 16)

                load(0, 0)

                def step(s, u):
                    for what, lag, k in order:
                        b, v = s - lag, (u - lag) % RING
                        if not live(b):
                            continue
                        if what == "load":
                            load(b, v)
                        elif what == "conv":
                            settle(sp, m, kept, 32 * b)
                            settle(sp, m, tail_read, turn["tail"](s, what) + 1)
                            sp.dma_start(m.xn_hbm[1, b], m.xn2[:, v].rearrange("p a b -> p (a b)")).then_inc(kept, 16)
                            sp.dma_start(m.xnT_hbm[1, b], m.xnT2[:, v, :]).then_inc(kept, 16)
                        elif what == "o" and not with_attention:
                            settle(sp, m, gate_read, turn["gate"](s, what) + 1)
                            sp.dma_start(m.out_dram[:, b], m.x[:, bass.ds(b * QT, QT), :]).then_inc(stored, 16)

                steps(sp, step)
                if with_attention:
                    sp.wait_ge(kept, 32 * NSEQ)
                else:
                    sp.wait_ge(stored, 16 * NSEQ)


def kernel(**inputs):
    import ml_dtypes as _ml
    import numpy as _np
    import concourse.bacc as _bacc
    from concourse.bass_utils import run_bass_kernel_spmd as _run

    f32 = _np.float32

    def got(name):
        return _np.ascontiguousarray(inputs["L0_" + name])

    cols = _np.array([(2 * pair + par) * HD + d for par in range(2) for d in range(HD) for pair in range(NPAIR)])
    n = _np.arange(SEQ)
    rope_a = _np.zeros((SEQ, 2, 2, 2, NPAIR), f32)
    for c, pos in enumerate((n // 16, n % 16)):
        angle = pos.astype(f32)
        for e in range(2):
            rope_a[:, 0, c, e, :] = _np.cos(angle)[:, None]
            rope_a[:, 1, c, e, :] = (_np.sin(angle) if e else -_np.sin(angle))[:, None]
    inv = (f32(1.0) / f32(10000.0) ** (_np.arange(0, D, 2, dtype=f32) / f32(D))).astype(f32)
    angle = n.astype(f32)[:, None] * inv[None, :]
    rope_b = _np.zeros((SEQ, 2, D // 2, 2), f32)
    for e in range(2):
        rope_b[:, 0, :, e] = _np.cos(angle)
        rope_b[:, 1, :, e] = _np.sin(angle) if e else -_np.sin(angle)

    def tiles(a):
        return _np.ascontiguousarray(a.reshape(QT, P, 2, -1).transpose(1, 0, 2, 3))

    w_conv = _np.zeros((D, NL), f32)
    w_gate = _np.zeros((NL + 1, 2 * D), f32)
    for i, gate in enumerate(("so", "si")):
        conv = got(f"ffn_{gate}_conv_w")
        for g in range(NG):
            w_conv[4 * g:4 * g + 4, i * NG + g] = conv[g]
        w_gate[i * NG:(i + 1) * NG, i * D:(i + 1) * D] = got(f"ffn_{gate}_lin_w").T
        w_gate[NL, i * D:(i + 1) * D] = got(f"ffn_{gate}_lin_b")
    norm_gate = _np.stack([_np.concatenate([got(f"ffn_so_{k}"), got(f"ffn_si_{k}")])
                           for k in ("conv_b", "gamma", "beta")], axis=1)
    k_ones = _np.zeros((2, 3, NPAIR, 2, SEQ), f32)
    for par in range(2):
        k_ones[par, :, :, par, :] = 1.0
    arrays = {
        "x": got("attn_a_hidden_states"),
        "ident": _np.eye(P, dtype=f32),
        "ident_bf": _np.eye(P, dtype=f32).astype(_ml.bfloat16),
        "k_ones": k_ones.reshape(MAXROWS, NH, SEQ).astype(_ml.bfloat16),
        "rope_a": tiles(rope_a.reshape(SEQ, 2, 32)),
        "rope_b": tiles(rope_b.reshape(SEQ, 2, D)),
        "w_qkv_a": _np.concatenate([got("attn_a_Wq")[:, cols], got("attn_a_Wk")[:, cols], got("attn_a_Wv")], axis=1),
        "b_qkv_a": _np.concatenate([got("attn_a_bq")[cols], got("attn_a_bk")[cols], got("attn_a_bv")]),
        "w_o": got("attn_a_Wo"),
        "b_o": got("attn_a_bo"),
        "w_qkv_b": _np.concatenate([got("attn_b_wq_w").T, got("attn_b_wk_w").T, got("attn_b_wv_w").T], axis=1),
        "b_qkv_b": _np.concatenate([got("attn_b_wq_b"), got("attn_b_wk_b"), got("attn_b_wv_b")]),
        "w_conv": w_conv,
        "norm_gate": norm_gate,
        "w_gate": w_gate,
        "w_ffn": got("ffn_weight"),
        "b_ffn": got("ffn_bias"),
    }
    arrays = {k: _np.ascontiguousarray(a) for k, a in arrays.items()}
    nc = _bacc.Bacc("TRN2", target_bir_lowering=False, num_devices=1)
    t = {k: nc.dram_tensor("in_" + k, a.shape, mybir.dt.from_np(a.dtype), kind="ExternalInput").ap()
         for k, a in arrays.items()}
    out = nc.dram_tensor("out_0", (NSEQ, SEQ, D), F32, kind="ExternalOutput").ap()
    program(nc, t, out)
    r = _run(nc, [{"in_" + k: a for k, a in arrays.items()}], core_ids=[0])
    return r.results[0]["out_0"]
```

```python
from contextlib import ExitStack

import concourse.bass as bass
from concourse import mybir

F32 = mybir.dt.float32
BF16 = mybir.dt.bfloat16
ALU = mybir.AluOpType
ACT = mybir.ActivationFunctionType
AX = mybir.AxisListType

P = 128
NSEQ, SEQ, D = 32, 256, 128
QT = SEQ // P
NH, HD = 16, 8
NPAIR = NH // 2
NSLOT = 6
ROWS = NSLOT * HD
DATA = 2 * ROWS
MAXROWS = 6
VW = 32
HW = VW // 2
NG = D // 4
NL = 2 * NG
ROUNDS = 4
NGATE = QT * 2
EPS = 1e-5
LOWEST = -3.0e38
RING = 3
FIRST_LOOPED, LOOP_TRIPS = 5, 8
STEPS = NSEQ + 4


def steps(eng, step):
    for s in range(FIRST_LOOPED):
        step(s, s % RING)
    with eng.Fori(0, LOOP_TRIPS) as trip:
        for r in range(RING):
            step(trip * RING + (FIRST_LOOPED + r), (FIRST_LOOPED + r) % RING)
    for s in range(FIRST_LOOPED + LOOP_TRIPS * RING, STEPS):
        step(s, s % RING)


def live(b):
    return not isinstance(b, int) or 0 <= b < NSEQ


def need(eng, sem, value):
    if isinstance(value, int) and value <= 0:
        return
    eng.wait_ge(sem, value)


def settle(eng, m, sem, value):
    if isinstance(value, int):
        need(eng, sem, value)
        return
    register = eng.compute_val(value)
    eng.wait_ge(m.fills, 1)
    eng.wait_ge(sem, register)


def counter(order, users):
    mine = [e for e in order if (e[0], e[2]) in users]

    def turn(s, what, k=0):
        place = [(e[0], e[2]) for e in mine].index((what, k))
        if isinstance(s, int):
            return (sum(live(i - e[1]) for i in range(s) for e in mine)
                    + sum(live(s - e[1]) for e in mine[:place]))
        start = sum(live(i - e[1]) for i in range(FIRST_LOOPED) for e in mine)
        return (s - FIRST_LOOPED) * len(mine) + (start + place)

    return turn


class Model:
    pass


def program(nc, t, out):
    with ExitStack() as ctx:
        m = Model()

        def sb(name, shape, dt=F32):
            return ctx.enter_context(nc.sbuf_tensor(name, shape, dt))

        def dram(name, shape, dt=F32):
            return nc.dram_tensor(name, shape, dt).ap()

        m.x = sb("x", [P, NSEQ * QT, D])
        m.gate_in = sb("gate_in", [NL, NSEQ * SEQ])
        m.bn_parts = sb("bn_parts", [NL, NSEQ, 6])
        m.ident = sb("ident", [P, P])
        m.ident_bf = sb("ident_bf", [P, P], BF16)
        m.w_qkv_a = sb("w_qkv_a", [P, 5 * D])
        m.b_qk_a = sb("b_qk_a", [P, 4])
        m.b_v_a = sb("b_v_a", [P, D])
        m.w_o = sb("w_o", [P, D])
        m.b_o = sb("b_o", [P, D])
        m.rope_a = sb("rope_a", [P, 2, SEQ])
        m.w_qkv_b = sb("w_qkv_b", [P, 5 * D])
        m.b_qk_b = sb("b_qk_b", [P, 4])
        m.b_v_b = sb("b_v_b", [P, D])
        m.rope_b = sb("rope_b", [P, 2, SEQ])
        m.w_conv = sb("w_conv", [P, NL])
        m.norm_gate = sb("norm_gate", [NL, 3])
        m.w_gate = sb("w_gate", [NL + 1, 2 * D])
        m.w_ffn = sb("w_ffn", [P, D])
        m.b_ffn = sb("b_ffn", [P, D])
        m.neg_half = sb("neg_half", [P, QT])

        m.ln_st = sb("ln_st", [P, QT, 6])
        m.ln_mv = sb("ln_mv", [P, QT, 2])
        m.ln_rstd = sb("ln_rstd", [P, QT])
        m.ln2_st = sb("ln2_st", [P, QT, 6])
        m.ln2_mv = sb("ln2_mv", [P, QT, 2])
        m.ln2_rstd = sb("ln2_rstd", [P, QT])
        m.xn = sb("xn", [P, RING, QT, D])
        m.xn2 = sb("xn2", [P, RING, QT, D])
        m.xnT = sb("xnT", [P, SEQ])
        m.xnT2 = sb("xnT2", [P, RING, SEQ])
        m.rope_terms = sb("rope_terms", [P, 2, 2 * SEQ])
        m.qkT = sb("qkT", [P, 2 * SEQ])

        m.stack_hbm = dram("stack_hbm", [2, 2, NSLOT, HD * NPAIR, SEQ], BF16)
        m.xn_hbm = dram("xn_hbm", [2, NSEQ, P, QT * D])
        m.xnT_hbm = dram("xnT_hbm", [2, NSEQ, P, SEQ])

        m.consts = ctx.enter_context(nc.semaphore("consts"))
        m.x_first = ctx.enter_context(nc.semaphore("x_first"))
        m.x_all = ctx.enter_context(nc.semaphore("x_all"))
        m.fills = ctx.enter_context(nc.semaphore("fills"))

        tables = [(m.ident, "ident"), (m.ident_bf, "ident_bf"), (m.w_qkv_a, "w_qkv_a"), (m.w_o, "w_o"),
                  (m.rope_a, "rope_a"), (m.w_qkv_b, "w_qkv_b"), (m.rope_b, "rope_b"), (m.w_conv, "w_conv"),
                  (m.norm_gate, "norm_gate"), (m.w_gate, "w_gate"), (m.w_ffn, "w_ffn"),
                  (m.b_qk_a, "b_qk_a"), (m.b_qk_b, "b_qk_b")]
        rows = [(m.b_v_a, "b_v_a"), (m.b_o, "b_o"), (m.b_v_b, "b_v_b"), (m.b_ffn, "b_ffn")]
        m.n_consts = 16 * (len(tables) + len(rows))
        x_dram = t["x"].rearrange("b (q p) d -> p (b q) d", p=P)
        m.out_dram = out.rearrange("b (q p) d -> p b q d", p=P)

        with nc.Block() as block:
            @block.sync
            def _(sp):
                sp.dma_start(m.x[:, 0:8, :], x_dram[:, 0:8, :]).then_inc(m.x_first, 16)
                for dst, name in tables:
                    sp.dma_start(dst[:], t[name]).then_inc(m.consts, 16)
                for dst, name in rows:
                    sp.dma_start(dst[:], t[name].partition_broadcast(P)).then_inc(m.consts, 16)
                sp.dma_start(m.x[:, 8:, :], x_dram[:, 8:, :]).then_inc(m.x_all, 16)

            @block.vector
            def _(dve):
                nc.vector.memset(m.neg_half[:], -0.5).then_inc(m.fills, 1)

        attention_a(nc, m, t)
        for n in range(2):
            gate_norm(nc, m, n)
            feed_forward(nc, m, n)



class Norm:

    def __init__(self, ctx, nc, name):
        self.parts_ok = ctx.enter_context(nc.semaphore(name + "_parts_ok"))
        self.stats_ok = ctx.enter_context(nc.semaphore(name + "_stats_ok"))
        self.eps_ok = ctx.enter_context(nc.semaphore(name + "_eps_ok"))
        self.rstd_ok = ctx.enter_context(nc.semaphore(name + "_rstd_ok"))
        self.xn_ok = ctx.enter_context(nc.semaphore(name + "_xn_ok"))


def norm_stats(nc, dve, m, sems, st, mv, b):
    settle(dve, m, sems.xn_ok, QT * b)
    for qt in range(QT):
        nc.vector.bn_stats(st[:, qt, :], m.x[:, b * QT + qt, :]).then_inc(sems.parts_ok, 1)
    for qt in range(QT):
        settle(dve, m, sems.parts_ok, QT * b + QT)
        nc.vector.bn_aggr(mv[:, qt, :], st[:, qt, :]).then_inc(sems.stats_ok, 1)


def norm_rstd(nc, pool, m, sems, mv, rstd, b):
    settle(pool, m, sems.stats_ok, QT * (b + 1))
    nc.gpsimd.tensor_scalar(rstd[:], mv[:, :, 1], EPS, None, ALU.add).then_inc(sems.eps_ok, 1)
    pool.wait_ge(sems.eps_ok, b + 1)
    nc.gpsimd.tensor_tensor(rstd[:], rstd[:], m.neg_half[:], ALU.pow).then_inc(sems.rstd_ok, 1)


def norm_scale(nc, dve, m, sems, mv, rstd, dst, b):
    dve.wait_ge(sems.rstd_ok, b + 1)
    for qt in range(QT):
        nc.vector.tensor_scalar(dst[:, qt, :], m.x[:, b * QT + qt, :], mv[:, qt, 0:1], rstd[:, qt:qt + 1],
                                ALU.subtract, ALU.mult).then_inc(sems.xn_ok, 1)


def project(nc, m, w, i, bank):
    for q in range(2):
        mm = nc.tensor.matmul(bank[:, q * SEQ:(q + 1) * SEQ], w[:, (2 * i + q) * D:(2 * i + q + 1) * D], m.xnT[:],
                              start=True, stop=True)
    return mm


def rope_term(nc, m, bias, table, i, bank, sem, last):
    for q in range(2):
        nc.vector.scalar_tensor_tensor(out=m.rope_terms[:, i, q * SEQ:(q + 1) * SEQ], in0=bank[:, q * SEQ:(q + 1) * SEQ],
                                       scalar=bias[:, 2 * i + q:2 * i + q + 1], in1=table[:, i, :],
                                       op0=ALU.add, op1=ALU.mult).then_inc(last if q else sem, 1)



ORDER_A = [
    ("st", 3, 4), ("max", 2, 8), ("proj", 4, 0), ("max", 2, 9), ("xnT", 0, 0), ("cut_max", 2, 0),
    ("st", 3, 5), ("max", 2, 10), ("pv", 3, 1), ("main", 0, 0), ("max", 2, 11), ("rstd2", 4, 0),
    ("st", 3, 6), ("mT", 2, 0), ("max", 2, 12), ("rot", 0, 0), ("max", 2, 13), ("scale2", 4, 0), ("cut", 0, 0),
    ("st", 3, 7), ("max", 2, 14), ("pv", 3, 2), ("xnT2", 4, 0), ("max", 2, 15), ("cut_max", 2, 1),
    ("st", 2, 0), ("max", 1, 0), ("conv", 4, 0), ("max", 1, 1), ("cut", 0, 1), ("ln", -1, 0),
    ("st", 2, 1), ("max", 1, 2), ("pv", 3, 3), ("max", 1, 3), ("rstd", -1, 0),
    ("st", 2, 2), ("max", 1, 4), ("v", 0, 0), ("ctx", 3, 0), ("max", 1, 5), ("scale", -1, 0),
    ("st", 2, 3), ("max", 1, 6), ("mT", 2, 1), ("pv", 2, 0), ("ctxT", 3, 0), ("max", 1, 7),
]
MISC_A = [("proj", 0), ("xnT", 0), ("main", 0), ("mT", 0), ("rot", 0), ("xnT2", 0), ("conv", 0),
          ("v", 0), ("ctx", 0), ("mT", 1), ("ctxT", 0)]
EVACUATED_BY_ACT = ("xnT", "mT", "xnT2", "conv", "ctxT")


def attention_a(nc, m, t):
    with ExitStack() as ctx:
        def sb(name, shape, dt=F32):
            return ctx.enter_context(nc.sbuf_tensor(name, shape, dt))

        def psum(name, shape):
            return ctx.enter_context(nc.psum_tensor(name, shape, F32))

        def sem(name):
            return ctx.enter_context(nc.semaphore("a_" + name))

        rest = sb("rest", [P, 2 * SEQ])
        parts = sb("parts", [P, 3, 2 * SEQ], BF16)
        q_stack = sb("q_stack", [P, RING, NPAIR, SEQ], BF16)
        k_stack = sb("k_stack", [P, RING, NH, SEQ], BF16)
        v_aug = sb("v_aug", [P, RING, QT, NPAIR, 2, VW + HW])
        nmax = sb("nmax", [P, 2, QT, 4, 2])
        nmax_rest = sb("nmax_rest", [P, 2, QT, 4, 2])
        nmax_parts = sb("nmax_parts", [P, 2, QT, 4, 2, 3], BF16)
        probs = sb("probs", [P, 4, 2, QT, SEQ])
        ctxT_raw = sb("ctxT_raw", [P, 2, SEQ])
        z_inv = sb("z_inv", [P, QT, NH])
        ctx_tok = sb("ctx_tok", [P, QT, D])
        ctxT = sb("ctxT", [P, SEQ])
        xb = sb("xb", [P, QT, D])
        st_bank = psum("st_bank", [P, 2, 2, QT, SEQ])
        s_bank = psum("s_bank", [P, 2, QT, SEQ])
        pv_bank = psum("pv_bank", [P, 2, SEQ])
        misc_bank = psum("misc_bank", [P, 2 * SEQ])
        misc = misc_bank[:]
        misc_bf = misc.bitcast(BF16)
        turn = counter(ORDER_A, MISC_A)

        misc_ps = sem("misc_ps")
        misc_read = sem("misc_read")
        norm, norm2 = Norm(ctx, nc, "a_ln"), Norm(ctx, nc, "a_ln2")
        term_ok = sem("term_ok")
        qk_ok = sem("qk_ok")
        v_ok = sem("v_ok")
        cut = sem("cut")
        parts_ok = sem("parts_ok")
        q_out = sem("q_out")
        k_out = sem("k_out")
        stack_in = sem("stack_in")
        k_clear = sem("k_clear")
        k_ones = sem("k_ones")
        v_fill = sem("v_fill")
        s_ps = sem("s_ps")
        max_ok = sem("max_ok")
        cut_max = sem("cut_max")
        nmax_ok = sem("nmax_ok")
        st_ps = sem("st_ps")
        probs_ok = sem("probs_ok")
        pv_ps = sem("pv_ps")
        pv_ok = sem("pv_ok")
        z_ok = sem("z_ok")
        xb_ok = sem("xb_ok")
        g_ok = sem("g_ok")
        bn_ok = sem("bn_ok")
        kept = sem("kept")

        with nc.Block() as block:
            @block.tensor
            def _(pe):
                pe.wait_ge(m.consts, m.n_consts)
                pe.wait_ge(k_ones, 16 * RING)
                pe.wait_ge(v_fill, 2)

                def step(s, u):
                    for what, lag, k in ORDER_A:
                        b, v = s - lag, (u - lag) % RING
                        if not live(b):
                            continue
                        if (what, k) in MISC_A:
                            n = turn(s, what, k)
                            need(pe, misc_read, n)
                        if what == "st":
                            if k % 4 == 0:
                                pe.wait_ge(misc_read, turn(s if k == 0 else s - 1, "mT", k // 4) + 1)
                            if k == 0:
                                pe.wait_ge(stack_in, 16 * 4 * (b + 1))
                            need(pe, probs_ok, 8 * b + k - 1)
                            for par in range(2):
                                for kt in range(QT):
                                    mm = nc.tensor.matmul(
                                        st_bank[:, k % 2, par, kt, :],
                                        k_stack[0:DATA + MAXROWS, v, 2 * k + par, kt * P:(kt + 1) * P],
                                        q_stack[0:DATA + MAXROWS, v, k, :], start=True, stop=True)
                            mm.then_inc(st_ps, 1)
                        elif what == "pv":
                            pe.wait_ge(probs_ok, 8 * b + 2 * k + 2)
                            if k == 0:
                                need(pe, pv_ok, b)
                                pe.wait_ge(v_ok, b + 1)
                                pe.wait_ge(v_fill, 2)
                            for pair in (2 * k, 2 * k + 1):
                                j = pair % 4
                                for par in range(2):
                                    for kt in range(QT):
                                        mm = nc.tensor.matmul(
                                            pv_bank[VW * j:VW * (j + 1), pair // 4, :],
                                            v_aug[:, v, kt, pair].rearrange("p a b -> p (a b)")[:, VW * par:VW * (par + 1)],
                                            probs[:, pair % 4, par, kt, :],
                                            start=(par == 0 and kt == 0), stop=(par == 1 and kt == QT - 1))
                            mm.then_inc(pv_ps, 1)
                        elif what == "max":
                            if k == 0:
                                pe.wait_ge(stack_in, 16 * 4 * (b + 1))
                            need(pe, max_ok, 16 * b + k - 1)
                            for qt in range(QT):
                                mm = nc.tensor.matmul(s_bank[:, k % 2, qt, :],
                                                      q_stack[0:DATA, v, k // 2, qt * P:(qt + 1) * P],
                                                      k_stack[0:DATA, v, k, :], start=True, stop=True)
                            mm.then_inc(s_ps, 1)
                        elif what == "mT":
                            pe.wait_ge(nmax_ok, 2 * b + k + 1)
                            pe.wait_ge(v_fill, 2)
                            for j in range(4):
                                for qt in range(QT):
                                    mm = nc.tensor.transpose(
                                        misc_bf[DATA:DATA + MAXROWS, j * SEQ + qt * P:j * SEQ + (qt + 1) * P],
                                        nmax_parts[:, k, qt, j].rearrange("p a b -> p (a b)"), m.ident_bf[:])
                            mm.then_inc(misc_ps, 1)
                        elif what == "xnT":
                            pe.wait_ge(norm.xn_ok, QT * (b + 1))
                            for qt in range(QT):
                                mm = nc.tensor.transpose(misc[:, qt * P:(qt + 1) * P], m.xn[:, v, qt, :], m.ident[:])
                            mm.then_inc(misc_ps, 1)
                        elif what in ("main", "rot"):
                            pe.wait_ge(misc_read, turn(s, "xnT") + 1)
                            project(nc, m, m.w_qkv_a, int(what == "rot"), misc).then_inc(misc_ps, 1)
                        elif what == "v":
                            for qt in range(QT):
                                mm = nc.tensor.matmul(misc[:, qt * D:(qt + 1) * D], m.xnT[:, qt * P:(qt + 1) * P],
                                                      m.w_qkv_a[:, 4 * D:], start=True, stop=True)
                            mm.then_inc(misc_ps, 1)
                        elif what == "ctx":
                            pe.wait_ge(pv_ok, b + 1)
                            for qt in range(QT):
                                for g in range(2):
                                    mm = nc.tensor.transpose(misc[:, (2 * qt + g) * P:(2 * qt + g + 1) * P],
                                                             ctxT_raw[:, g, qt * P:(qt + 1) * P], m.ident[:])
                            mm.then_inc(misc_ps, 1)
                        elif what == "ctxT":
                            pe.wait_ge(misc_read, turn(s, "ctx") + 1)
                            for qt in range(QT):
                                mm = nc.tensor.transpose(misc[:, qt * P:(qt + 1) * P], ctx_tok[:, qt, :], m.ident[:])
                            mm.then_inc(misc_ps, 1)
                        elif what == "proj":
                            for qt in range(QT):
                                mm = nc.tensor.matmul(misc[:, qt * D:(qt + 1) * D], ctxT[:, qt * P:(qt + 1) * P],
                                                      m.w_o[:], start=True, stop=True)
                            mm.then_inc(misc_ps, 1)
                        elif what == "xnT2":
                            pe.wait_ge(norm2.xn_ok, QT * (b + 1))
                            for qt in range(QT):
                                mm = nc.tensor.transpose(misc[:, qt * P:(qt + 1) * P], m.xn2[:, v, qt, :], m.ident[:])
                            mm.then_inc(misc_ps, 1)
                        elif what == "conv":
                            pe.wait_ge(misc_read, turn(s, "xnT2") + 1)
                            pe.wait_ge(v_fill, 2)
                            nc.tensor.matmul(misc[0:NL, 0:SEQ], m.w_conv[:], m.xnT2[:, v, :],
                                             start=True, stop=True).then_inc(misc_ps, 1)

                steps(pe, step)

            @block.scalar
            def _(act):
                def step(s, u):
                    for what, lag, k in ORDER_A:
                        b, v = s - lag, (u - lag) % RING
                        if not live(b):
                            continue
                        if what in EVACUATED_BY_ACT:
                            settle(act, m, misc_ps, turn(s, what, k) + 1)
                        if what == "st":
                            act.wait_ge(st_ps, 8 * b + k + 1)
                            need(act, pv_ps, 4 * b + k // 2 - 1)
                            nc.scalar.activation(probs[:, k % 4].rearrange("p a b c -> p (a b c)"),
                                                 st_bank[:, k % 2].rearrange("p a b c -> p (a b c)"), ACT.Exp,
                                                 scale=HD ** -0.5).then_inc(probs_ok, 1)
                        elif what == "pv" and k == 3:
                            act.wait_ge(pv_ps, 4 * (b + 1))
                            nc.scalar.copy(ctxT_raw[:], pv_bank[:]).then_inc(pv_ok, 1)
                        elif what == "mT":
                            nc.scalar.copy(q_stack[DATA:DATA + MAXROWS, v, 4 * k:4 * k + 4, :].rearrange("p a b -> p (a b)"),
                                           misc_bf[DATA:DATA + MAXROWS, :]).then_inc(misc_read, 1)
                        elif what == "xnT":
                            nc.scalar.copy(m.xnT[:], misc[:, 0:SEQ]).then_inc(misc_read, 1)
                        elif what == "ctxT":
                            nc.scalar.copy(ctxT[:], misc[:, 0:SEQ]).then_inc(misc_read, 1)
                        elif what == "xnT2":
                            need(act, kept, 32 * b)
                            nc.scalar.copy(m.xnT2[:, v, :], misc[:, 0:SEQ]).then_inc(misc_read, 1)
                        elif what == "conv":
                            nc.scalar.activation(m.gate_in[:, bass.ds(b * SEQ, SEQ)], misc[0:NL, 0:SEQ], ACT.Identity,
                                                 bias=m.norm_gate[:, 0:1]).then_inc(misc_read, 1)

                steps(act, step)

            @block.vector
            def _(dve):
                nc.vector.memset(k_stack[:], 0.0).then_inc(k_clear, 1)
                nc.vector.memset(v_aug[:], 0.0).then_inc(v_fill, 1)
                dve.wait_ge(v_fill, 1)
                nc.vector.memset(v_aug[:, :, :, :, :, HD:HD + 1].rearrange("p r a t b c -> p (r a t b) c"), 1.0).then_inc(v_fill, 1)
                dve.wait_ge(m.x_first, 16)
                norm_stats(nc, dve, m, norm, m.ln_st, m.ln_mv, 0)
                norm_scale(nc, dve, m, norm, m.ln_mv, m.ln_rstd, m.xn[:, 0], 0)

                def step(s, u):
                    if isinstance(s, int) and s == FIRST_LOOPED - 2:
                        dve.wait_ge(m.x_all, 16)
                    for what, lag, k in ORDER_A:
                        b, v = s - lag, (u - lag) % RING
                        if not live(b):
                            continue
                        if what == "max":
                            dve.wait_ge(s_ps, 16 * b + k + 1)
                            if k % 8 == 0:
                                need(dve, nmax_ok, 2 * b + k // 8 - 1)
                            nc.vector.tensor_reduce(nmax[:, k // 8, :, k // 2 % 4, k % 2], s_bank[:, k % 2], AX.X,
                                                    ALU.max, negate=True).then_inc(max_ok, 1)
                        elif what == "main":
                            dve.wait_ge(misc_ps, turn(s, what) + 1)
                            need(dve, qk_ok, 2 * b)
                            rope_term(nc, m, m.b_qk_a, m.rope_a, 0, misc, term_ok, misc_read)
                        elif what == "rot":
                            dve.wait_ge(misc_ps, turn(s, what) + 1)
                            rope_term(nc, m, m.b_qk_a, m.rope_a, 1, misc, term_ok, misc_read)
                        elif what == "v":
                            dve.wait_ge(misc_ps, turn(s, what) + 1)
                            need(dve, pv_ps, 4 * (b - 2))
                            for qt in range(QT):
                                nc.vector.tensor_tensor(
                                    v_aug[:, v, qt, :, :, 0:HD],
                                    misc[:, qt * D:(qt + 1) * D].rearrange("p (t r d) -> p t r d", r=2, d=HD),
                                    m.b_v_a[:].rearrange("p (t r d) -> p t r d", r=2, d=HD),
                                    ALU.add).then_inc(v_ok if qt < QT - 1 else misc_read, 1)
                        elif what == "ctx":
                            dve.wait_ge(misc_ps, turn(s, "ctx") + 1)
                            heads = misc.rearrange("p (a h c) -> p a h c", a=QT, c=HW)
                            nc.vector.reciprocal(z_inv[:], heads[:, :, :, HD]).then_inc(z_ok, 1)
                            dve.wait_ge(z_ok, b + 1)
                            nc.vector.tensor_tensor(
                                ctx_tok[:].rearrange("p a (h d) -> p a h d", d=HD),
                                heads[:, :, :, 0:HD], z_inv[:].unsqueeze(3).broadcast_to([P, QT, NH, HD]),
                                ALU.mult).then_inc(misc_read, 1)
                        elif what == "proj":
                            dve.wait_ge(misc_ps, turn(s, "proj") + 1)
                            dve.wait_ge(xb_ok, b + 1)
                            nc.vector.tensor_tensor(m.x[:, bass.ds(b * QT, QT), :],
                                                    misc[:, 0:QT * D].rearrange("p (a b) -> p a b", a=QT), xb[:],
                                                    ALU.add).then_inc(misc_read, 1)
                            settle(dve, m, misc_read, turn(s, "proj") + 1)
                            norm_stats(nc, dve, m, norm2, m.ln2_st, m.ln2_mv, b)
                        elif what == "scale2":
                            need(dve, kept, 32 * b)
                            norm_scale(nc, dve, m, norm2, m.ln2_mv, m.ln2_rstd, m.xn2[:, v], b)
                        elif what == "ln":
                            norm_stats(nc, dve, m, norm, m.ln_st, m.ln_mv, b)
                        elif what == "scale":
                            norm_scale(nc, dve, m, norm, m.ln_mv, m.ln_rstd, m.xn[:, v], b)
                        elif what == "conv":
                            settle(dve, m, misc_read, turn(s, "conv") + 1)
                            nc.vector.bn_stats(m.bn_parts[:, b, :], m.gate_in[:, bass.ds(b * SEQ, SEQ)]).then_inc(bn_ok, 1)

                steps(dve, step)

            @block.gpsimd
            def _(pool):
                pool.wait_ge(m.consts, m.n_consts)
                norm_rstd(nc, pool, m, norm, m.ln_mv, m.ln_rstd, 0)

                def step(s, u):
                    for what, lag, k in ORDER_A:
                        b, v = s - lag, (u - lag) % RING
                        if not live(b):
                            continue
                        if what == "rstd":
                            norm_rstd(nc, pool, m, norm, m.ln_mv, m.ln_rstd, b)
                        elif what == "rstd2":
                            norm_rstd(nc, pool, m, norm2, m.ln2_mv, m.ln2_rstd, b)
                        elif what == "ctxT":
                            nc.gpsimd.tensor_tensor(xb[:], m.x[:, bass.ds(b * QT, QT), :],
                                                    m.b_o[:].unsqueeze(1).broadcast_to([P, QT, D]),
                                                    ALU.add).then_inc(xb_ok, 1)
                        elif what == "cut_max":
                            whole = nmax[:, k].rearrange("p a t r -> p (a t r)")
                            left = nmax_rest[:, k].rearrange("p a t r -> p (a t r)")
                            part = nmax_parts[:, k].rearrange("p a t r c -> p (a t r) c")
                            links = 3 * (2 * b + k)
                            settle(pool, m, max_ok, 16 * b + 8 * k + 8)
                            nc.gpsimd.tensor_copy(part[:, :, 0], whole).then_inc(cut_max, 1)
                            pool.wait_ge(cut_max, links + 1)
                            nc.gpsimd.tensor_tensor(left, whole, part[:, :, 0], ALU.subtract).then_inc(cut_max, 1)
                            settle(pool, m, cut_max, links + 2)
                            nc.gpsimd.tensor_copy(part[:, :, 1], left).then_inc(cut_max, 1)
                            pool.wait_ge(cut_max, links + 3)
                            nc.gpsimd.tensor_tensor(part[:, :, 2], left, part[:, :, 1], ALU.subtract).then_inc(nmax_ok, 1)
                        elif what == "cut":
                            cols = slice(k * SEQ, (k + 1) * SEQ)
                            links = 3 * (2 * b + k)
                            pool.wait_ge(misc_read, turn(s, "rot") + 1)
                            nc.gpsimd.tensor_tensor(m.qkT[:, cols], m.rope_terms[:, 0, cols], m.rope_terms[:, 1, cols],
                                                    ALU.add).then_inc(qk_ok, 1)
                            settle(pool, m, k_out if k else q_out, 16 * 6 * b)
                            settle(pool, m, qk_ok, 2 * b + k + 1)
                            nc.gpsimd.tensor_copy(parts[:, 0, cols], m.qkT[:, cols]).then_inc(cut, 1)
                            pool.wait_ge(cut, links + 1)
                            nc.gpsimd.tensor_tensor(rest[:, cols], m.qkT[:, cols], parts[:, 0, cols],
                                                    ALU.subtract).then_inc(cut, 1)
                            settle(pool, m, cut, links + 2)
                            nc.gpsimd.tensor_copy(parts[:, 1, cols], rest[:, cols]).then_inc(cut, 1)
                            pool.wait_ge(cut, links + 3)
                            nc.gpsimd.tensor_tensor(parts[:, 2, cols], rest[:, cols], parts[:, 1, cols],
                                                    ALU.subtract).then_inc(parts_ok, 1)

                steps(pool, step)

            @block.sync
            def _(sp):
                sp.wait_ge(k_clear, 1)
                for r in range(RING):
                    sp.dma_start(k_stack[DATA:DATA + MAXROWS, r], t["k_ones"]).then_inc(k_ones, 16)

                def step(s, u):
                    for what, lag, k in ORDER_A:
                        b, v = s - lag, (u - lag) % RING
                        if not live(b):
                            continue
                        if what == "cut":
                            settle(sp, m, stack_in, 16 * 4 * b)
                            settle(sp, m, parts_ok, 2 * b + k + 1)
                            for par in range(2):
                                half = parts[par * 64:(par + 1) * 64, :, k * SEQ:(k + 1) * SEQ]
                                dst = m.stack_hbm[k, par].rearrange("s r n -> r s n")
                                for at, n, part in ((0, 3, 0), (3, 2, 1), (5, 1, 2)):
                                    src = half[:, 0:n] if k == 0 else half[:, part:part + 1].broadcast_to([64, n, SEQ])
                                    sp.dma_start(dst[:, at:at + n], src).then_inc(k_out if k else q_out, 16)
                            if k == 0:
                                continue
                            settle(sp, m, probs_ok, 8 * (b - 2))
                            for i in range(2):
                                settle(sp, m, k_out if i else q_out, 16 * 6 * (b + 1))
                                for par in range(2):
                                    src = m.stack_hbm[i, par].rearrange("s (d t) n -> (s d) t n", t=NPAIR)
                                    dst = (q_stack[par * ROWS:(par + 1) * ROWS, v] if i == 0 else
                                           k_stack[par * ROWS:(par + 1) * ROWS, v]
                                           .rearrange("p (t r) n -> p r t n", r=2)[:, par])
                                    sp.dma_start(dst, src).then_inc(stack_in, 16)
                        elif what == "conv":
                            settle(sp, m, kept, 32 * b)
                            settle(sp, m, misc_read, turn(s, "conv") + 1)
                            sp.dma_start(m.xn_hbm[0, b], m.xn2[:, v].rearrange("p a b -> p (a b)")).then_inc(kept, 16)
                            sp.dma_start(m.xnT_hbm[0, b], m.xnT2[:, v, :]).then_inc(kept, 16)

                steps(sp, step)
                sp.wait_ge(kept, 32 * NSEQ)



def gate_norm(nc, m, n):
    with ExitStack() as ctx:
        mv = ctx.enter_context(nc.sbuf_tensor(f"gn{n}_mv", [NL, 2], F32))
        w = ctx.enter_context(nc.sbuf_tensor(f"gn{n}_w", [NL, 4], F32))
        mean_ok = ctx.enter_context(nc.semaphore(f"gn{n}_mean_ok"))
        link = ctx.enter_context(nc.semaphore(f"gn{n}_link"))
        with nc.Block() as block:
            @block.vector
            def _(dve):
                nc.vector.bn_aggr(mv[:], m.bn_parts[:].rearrange("p a b -> p (a b)")).then_inc(mean_ok, 1)

            @block.gpsimd
            def _(pool):
                pool.wait_ge(mean_ok, 1)
                nc.gpsimd.tensor_scalar(w[:, 0:1], mv[:, 1:2], EPS, None, ALU.add).then_inc(link, 1)
                pool.wait_ge(link, 1)
                nc.gpsimd.tensor_tensor(w[:, 0:1], w[:, 0:1], m.neg_half[0:NL, 0:1], ALU.pow).then_inc(link, 1)
                pool.wait_ge(link, 2)
                nc.gpsimd.tensor_tensor(w[:, 1:2], w[:, 0:1], m.norm_gate[:, 1:2], ALU.mult).then_inc(link, 1)
                pool.wait_ge(link, 3)
                nc.gpsimd.tensor_tensor(w[:, 2:3], mv[:, 0:1], w[:, 1:2], ALU.mult).then_inc(link, 1)
                pool.wait_ge(link, 4)
                nc.gpsimd.tensor_tensor(w[:, 3:4], m.norm_gate[:, 2:3], w[:, 2:3], ALU.subtract).then_inc(link, 1)

            @block.scalar
            def _(act):
                act.wait_ge(link, 5)
                for i in range(4):
                    piece = m.gate_in[:, i * NSEQ * SEQ // 4:(i + 1) * NSEQ * SEQ // 4]
                    nc.scalar.activation(piece, piece, ACT.Gelu, bias=w[:, 3:4], scale=w[:, 1:2])



ORDER_F = [
    ("xnT", 3, 0), ("logits", 0, 0), ("probs", 4, 0), ("left", 2, 0), ("top", 1, 0), ("main", 3, 0), ("probsT", 4, 0),
    ("rot", 3, 0), ("full", 0, 0), ("gates", 2, 0), ("all", 1, 0), ("xgT", 2, 0), ("top", 1, 1), ("pv", 4, 0),
    ("o", 2, 0), ("rstd2", 4, 0), ("load", -1, 0), ("v", 3, 0), ("rstd", 2, 0), ("top", 1, 2), ("scale2", 4, 0),
    ("xnT2", 4, 0), ("s", 3, 0), ("scale", 2, 0), ("conv", 4, 0), ("top", 1, 3),
]
ORDER_LAST = [
    ("left", 2, 0), ("logits", 0, 0), ("full", 0, 0), ("top", 1, 0), ("all", 1, 0),
    ("top", 1, 1), ("gates", 2, 0), ("xgT", 2, 0), ("load", -1, 0), ("top", 1, 2), ("o", 2, 0), ("top", 1, 3),
]
GATE_BANK = [("xgT", 0), ("o", 0)]
PROJ_BANK = [("xnT", 0), ("main", 0), ("rot", 0), ("v", 0)]
ATT_BANK = [("probsT", 0), ("pv", 0), ("s", 0)]
TAIL_BANK = [("xnT2", 0), ("conv", 0)]
LOGIT_BANK = [("logits", 0)]
FULL_BANK = [("full", 0)]


def feed_forward(nc, m, n):
    with_attention = n == 0
    order = ORDER_F if with_attention else ORDER_LAST
    with ExitStack() as ctx:
        def sb(name, shape, dt=F32):
            return ctx.enter_context(nc.sbuf_tensor(f"f{n}_{name}", shape, dt))

        def psum(name, shape):
            return ctx.enter_context(nc.psum_tensor(f"f{n}_{name}", shape, F32))

        def sem(name):
            return ctx.enter_context(nc.semaphore(f"f{n}_{name}"))

        xn_f = sb("xn_f", [P, RING, QT, D])
        xnT_f = sb("xnT_f", [P, RING, SEQ])
        xa = sb("xa", [NL + 1, RING, SEQ])
        logit = sb("logit", [P, RING, QT, 2 * D])
        left = sb("left", [P, RING, QT, 2 * D])
        top8 = sb("top8", [P, NGATE, ROUNDS, 8])
        neg_top = sb("neg_top", [P, RING, NGATE])
        e_all = sb("e_all", [P, QT, 2 * D])
        e_left = sb("e_left", [P, QT, 2 * D])
        z = sb("z", [P, RING, NGATE])
        z_inv = sb("z_inv", [P, NGATE])
        gates = sb("gates", [P, QT, 2 * D])
        full_s = sb("full_s", [P, RING, QT, D])
        gated = sb("gated", [P, QT, D])
        xg = sb("xg", [P, QT, D])
        xgT = sb("xgT", [P, SEQ])
        xb = sb("xb", [P, QT, D])
        logit_bank = psum("logit_bank", [P, QT * 2 * D])
        full_bank = psum("full_bank", [P, QT * D])
        gate_bank = psum("gate_bank", [P, SEQ])

        logit_ps, logit_read = sem("logit_ps"), sem("logit_read")
        full_ps, full_read = sem("full_ps"), sem("full_read")
        gate_ps, gate_read = sem("gate_ps"), sem("gate_read")
        loaded = sem("loaded")
        ones_ok = sem("ones_ok")
        top_ok = sem("top_ok")
        neg_ok = sem("neg_ok")
        exps_ok = sem("exps_ok")
        z_ok = sem("z_ok")
        gates_ok = sem("gates_ok")
        gated_ok = sem("gated_ok")
        xb_ok = sem("xb_ok")
        turn = {k: counter(order, bank) for k, bank in (("logit", LOGIT_BANK), ("full", FULL_BANK), ("gate", GATE_BANK))}

        if with_attention:
            nmax = sb("nmax", [P, QT])
            nmax_s = sb("nmax_s", [P, QT])
            v_b = sb("v_b", [P, RING, QT, D])
            prob = sb("prob", [P, QT, SEQ])
            row_sum = sb("row_sum", [P, QT])
            row_inv = sb("row_inv", [P, QT])
            probT = sb("probT", [P, QT * SEQ])
            proj_bank = psum("proj_bank", [P, QT * 2 * D])
            att_bank = psum("att_bank", [P, QT * SEQ])
            tail_bank = psum("tail_bank", [P, SEQ])
            proj_ps, proj_read = sem("proj_ps"), sem("proj_read")
            att_ps, att_read = sem("att_ps"), sem("att_read")
            tail_ps, tail_read = sem("tail_ps"), sem("tail_read")
            norm, norm2 = Norm(ctx, nc, f"f{n}_ln"), Norm(ctx, nc, f"f{n}_ln2")
            term_ok = sem("term_ok")
            qk_ok = sem("qk_ok")
            max_ok = sem("max_ok")
            nmax_ok = sem("nmax_ok")
            row_ok = sem("row_ok")
            x3_ok = sem("x3_ok")
            bn_ok = sem("bn_ok")
            kept = sem("kept")
            turn.update({k: counter(order, bank) for k, bank in (("proj", PROJ_BANK), ("att", ATT_BANK), ("tail", TAIL_BANK))})
        else:
            stored = sem("stored")

        def row(tensor, g):
            return tensor[:, g // 2, (g % 2) * D:(g % 2 + 1) * D]

        with nc.Block() as block:
            @block.tensor
            def _(pe):
                pe.wait_ge(ones_ok, 1)

                def step(s, u):
                    for what, lag, k in order:
                        b, v = s - lag, (u - lag) % RING
                        if not live(b):
                            continue
                        if what == "logits":
                            pe.wait_ge(loaded, 48 * (b + 1))
                            need(pe, logit_read, turn["logit"](s, what))
                            for qt in range(QT):
                                mm = nc.tensor.matmul(logit_bank[:, qt * 2 * D:(qt + 1) * 2 * D],
                                                      xa[:, v, qt * P:(qt + 1) * P], m.w_gate[:], start=True, stop=True)
                            mm.then_inc(logit_ps, 1)
                        elif what == "full":
                            need(pe, full_read, turn["full"](s, what))
                            for qt in range(QT):
                                mm = nc.tensor.matmul(full_bank[:, qt * D:(qt + 1) * D],
                                                      xnT_f[:, v, qt * P:(qt + 1) * P], m.w_ffn[:], start=True, stop=True)
                            mm.then_inc(full_ps, 1)
                        elif what == "xgT":
                            pe.wait_ge(gated_ok, NGATE * (b + 1))
                            need(pe, gate_read, turn["gate"](s, what))
                            for qt in range(QT):
                                mm = nc.tensor.transpose(gate_bank[:, qt * P:(qt + 1) * P], xg[:, qt, :], m.ident[:])
                            mm.then_inc(gate_ps, 1)
                        elif what == "o":
                            pe.wait_ge(gate_read, turn["gate"](s, what))
                            for qt in range(QT):
                                mm = nc.tensor.matmul(gate_bank[:, qt * D:(qt + 1) * D], xgT[:, qt * P:(qt + 1) * P],
                                                      m.w_ffn[:], start=True, stop=True)
                            mm.then_inc(gate_ps, 1)
                        elif what == "xnT":
                            pe.wait_ge(norm.xn_ok, QT * (b + 1))
                            need(pe, proj_read, turn["proj"](s, what))
                            for qt in range(QT):
                                mm = nc.tensor.transpose(proj_bank[:, qt * P:(qt + 1) * P], m.xn[:, v, qt, :], m.ident[:])
                            mm.then_inc(proj_ps, 1)
                        elif what in ("main", "rot"):
                            pe.wait_ge(proj_read, turn["proj"](s, what))
                            project(nc, m, m.w_qkv_b, int(what == "rot"), proj_bank).then_inc(proj_ps, 1)
                        elif what == "v":
                            pe.wait_ge(proj_read, turn["proj"](s, what))
                            for qt in range(QT):
                                mm = nc.tensor.matmul(proj_bank[:, qt * D:(qt + 1) * D],
                                                      m.xnT[:, qt * P:(qt + 1) * P], m.w_qkv_b[:, 4 * D:], start=True, stop=True)
                            mm.then_inc(proj_ps, 1)
                        elif what == "s":
                            pe.wait_ge(qk_ok, b + 1)
                            need(pe, att_read, turn["att"](s, what))
                            for qt in range(QT):
                                mm = nc.tensor.matmul(att_bank[:, qt * SEQ:(qt + 1) * SEQ], m.qkT[:, qt * P:(qt + 1) * P],
                                                      m.qkT[:, SEQ:2 * SEQ], start=True, stop=True)
                            mm.then_inc(att_ps, 1)
                        elif what == "probsT":
                            pe.wait_ge(att_read, turn["att"](s, what))
                            for kt in range(QT):
                                for qt in range(QT):
                                    mm = nc.tensor.transpose(att_bank[:, kt * SEQ + qt * P:kt * SEQ + (qt + 1) * P],
                                                             prob[:, qt, kt * P:(kt + 1) * P], m.ident[:])
                            mm.then_inc(att_ps, 1)
                        elif what == "pv":
                            pe.wait_ge(att_read, turn["att"](s, what))
                            pe.wait_ge(proj_read, turn["proj"](s - 1, "v") + 1)
                            for qt in range(QT):
                                for kt in range(QT):
                                    mm = nc.tensor.matmul(att_bank[:, qt * D:(qt + 1) * D],
                                                          probT[:, kt * SEQ + qt * P:kt * SEQ + (qt + 1) * P],
                                                          v_b[:, v, kt, :], start=(kt == 0), stop=(kt == QT - 1))
                            mm.then_inc(att_ps, 1)
                        elif what == "xnT2":
                            pe.wait_ge(norm2.xn_ok, QT * (b + 1))
                            need(pe, tail_read, turn["tail"](s, what))
                            for qt in range(QT):
                                mm = nc.tensor.transpose(tail_bank[:, qt * P:(qt + 1) * P], m.xn2[:, v, qt, :], m.ident[:])
                            mm.then_inc(tail_ps, 1)
                        elif what == "conv":
                            pe.wait_ge(tail_read, turn["tail"](s, what))
                            pe.wait_ge(ones_ok, 1)
                            nc.tensor.matmul(tail_bank[0:NL, :], m.w_conv[:], m.xnT2[:, v, :],
                                             start=True, stop=True).then_inc(tail_ps, 1)

                steps(pe, step)

            @block.scalar
            def _(act):
                def step(s, u):
                    for what, lag, k in order:
                        b, v = s - lag, (u - lag) % RING
                        if not live(b):
                            continue
                        if what == "logits":
                            act.wait_ge(logit_ps, turn["logit"](s, what) + 1)
                            nc.scalar.copy(logit[:, v].rearrange("p a b -> p (a b)"), logit_bank[:]).then_inc(logit_read, 1)
                        elif what == "full":
                            act.wait_ge(full_ps, turn["full"](s, what) + 1)
                            nc.scalar.copy(full_s[:, v].rearrange("p a b -> p (a b)"), full_bank[:]).then_inc(full_read, 1)
                        elif what == "all":
                            act.wait_ge(neg_ok, b + 1)
                            need(act, gates_ok, b)
                            for g in range(NGATE):
                                nc.scalar.activation(row(e_all, g), row(logit[:, v], g), ACT.Exp,
                                                     bias=neg_top[:, v, g:g + 1], accum_out=z[:, v, g:g + 1])
                        elif what == "left":
                            act.wait_ge(top_ok, 8 * ROUNDS * (b + 1))
                            for g in range(NGATE):
                                e = nc.scalar.activation(row(e_left, g), row(left[:, v], g), ACT.Exp,
                                                         bias=neg_top[:, v, g:g + 1])
                            e.then_inc(exps_ok, 1)
                        elif what == "xgT":
                            act.wait_ge(gate_ps, turn["gate"](s, what) + 1)
                            nc.scalar.copy(xgT[:], gate_bank[:]).then_inc(gate_read, 1)
                        elif what == "xnT":
                            act.wait_ge(proj_ps, turn["proj"](s, what) + 1)
                            nc.scalar.copy(m.xnT[:], proj_bank[:, 0:SEQ]).then_inc(proj_read, 1)
                        elif what == "probs":
                            act.wait_ge(nmax_ok, b + 1)
                            need(act, row_ok, b)
                            for qt in range(QT):
                                e = nc.scalar.activation(prob[:, qt, :], att_bank[:, qt * SEQ:(qt + 1) * SEQ], ACT.Exp,
                                                         bias=nmax_s[:, qt:qt + 1], scale=D ** -0.5,
                                                         accum_out=row_sum[:, qt:qt + 1])
                            e.then_inc(att_read, 1)
                        elif what == "probsT":
                            act.wait_ge(att_ps, turn["att"](s, what) + 1)
                            nc.scalar.copy(probT[:], att_bank[:]).then_inc(att_read, 1)
                        elif what == "xnT2":
                            act.wait_ge(tail_ps, turn["tail"](s, what) + 1)
                            need(act, kept, 32 * b)
                            nc.scalar.copy(m.xnT2[:, v, :], tail_bank[:]).then_inc(tail_read, 1)
                        elif what == "conv":
                            settle(act, m, tail_ps, turn["tail"](s, what) + 1)
                            need(act, loaded, 48 * (b + 1))
                            nc.scalar.activation(m.gate_in[:, bass.ds(b * SEQ, SEQ)], tail_bank[0:NL, :], ACT.Identity,
                                                 bias=m.norm_gate[:, 0:1]).then_inc(tail_read, 1)

                steps(act, step)

            @block.vector
            def _(dve):
                nc.vector.memset(xa[NL:NL + 1], 1.0).then_inc(ones_ok, 1)

                def step(s, u):
                    for what, lag, k in order:
                        b, v = s - lag, (u - lag) % RING
                        if not live(b):
                            continue
                        if what == "top":
                            links = 8 * (ROUNDS * b + k)
                            if k == 0:
                                dve.wait_ge(logit_read, b + 1)
                                need(dve, neg_ok, b)
                            src = (logit if k == 0 else left)[:, v]
                            for g in range(NGATE):
                                if g % 2 == 0:
                                    settle(dve, m, top_ok, links - 4 + g + 2)
                                nc.vector.max(top8[:, g, k, :], row(src, g)).then_inc(top_ok, 1)
                            for g in range(NGATE):
                                if g % 2 == 0:
                                    settle(dve, m, top_ok, links + g + 2)
                                nc.vector.match_replace(row(left[:, v], g), top8[:, g, k, :], row(src, g), LOWEST)\
                                    .then_inc(top_ok, 1)
                        elif what == "gates":
                            dve.wait_ge(exps_ok, b + 1)
                            nc.vector.reciprocal(z_inv[:], z[:, v]).then_inc(z_ok, 1)
                            dve.wait_ge(z_ok, b + 1)
                            dve.wait_ge(gates_ok, b + 1)
                            for qt in range(QT):
                                for i, (dst, other) in enumerate(((gated, full_s), (xg, xn_f))):
                                    g = 2 * qt + i
                                    nc.vector.scalar_tensor_tensor(out=dst[:, qt, :], in0=row(gates, g),
                                                                   scalar=z_inv[:, g:g + 1], in1=other[:, v, qt, :],
                                                                   op0=ALU.mult, op1=ALU.mult).then_inc(gated_ok, 1)
                        elif what == "o":
                            dve.wait_ge(gate_ps, turn["gate"](s, what) + 1)
                            dve.wait_ge(xb_ok, 2 * (b + 1))
                            nc.vector.tensor_tensor(m.x[:, bass.ds(b * QT, QT), :],
                                                    gate_bank[:].rearrange("p (a b) -> p a b", a=QT), xb[:],
                                                    ALU.add).then_inc(gate_read, 1)
                            if with_attention:
                                settle(dve, m, gate_read, turn["gate"](s, what) + 1)
                                norm_stats(nc, dve, m, norm, m.ln_st, m.ln_mv, b)
                        elif what == "scale":
                            norm_scale(nc, dve, m, norm, m.ln_mv, m.ln_rstd, m.xn[:, v], b)
                        elif what == "main":
                            dve.wait_ge(proj_ps, turn["proj"](s, what) + 1)
                            need(dve, qk_ok, b)
                            rope_term(nc, m, m.b_qk_b, m.rope_b, 0, proj_bank, term_ok, proj_read)
                        elif what == "rot":
                            dve.wait_ge(proj_ps, turn["proj"](s, what) + 1)
                            rope_term(nc, m, m.b_qk_b, m.rope_b, 1, proj_bank, term_ok, proj_read)
                        elif what == "v":
                            dve.wait_ge(proj_ps, turn["proj"](s, what) + 1)
                            nc.vector.tensor_tensor(v_b[:, v], proj_bank[:, 0:QT * D].rearrange("p (a b) -> p a b", a=QT),
                                                    m.b_v_b[:].unsqueeze(1).broadcast_to([P, QT, D]),
                                                    ALU.add).then_inc(proj_read, 1)
                        elif what == "s":
                            dve.wait_ge(att_ps, turn["att"](s, what) + 1)
                            nc.vector.tensor_reduce(nmax[:], att_bank[:].rearrange("p (a b) -> p a b", a=QT), AX.X, ALU.max,
                                                    negate=True).then_inc(max_ok, 1)
                        elif what == "pv":
                            dve.wait_ge(att_ps, turn["att"](s, what) + 1)
                            nc.vector.reciprocal(row_inv[:], row_sum[:]).then_inc(row_ok, 1)
                            dve.wait_ge(row_ok, b + 1)
                            for qt in range(QT):
                                x = m.x[:, b * QT + qt, :]
                                nc.vector.scalar_tensor_tensor(out=x, in0=att_bank[:, qt * D:(qt + 1) * D],
                                                               scalar=row_inv[:, qt:qt + 1], in1=x, op0=ALU.mult,
                                                               op1=ALU.add).then_inc(x3_ok if qt < QT - 1 else att_read, 1)
                            settle(dve, m, x3_ok, b + 1)
                            dve.wait_ge(att_read, turn["att"](s, what) + 1)
                            norm_stats(nc, dve, m, norm2, m.ln2_st, m.ln2_mv, b)
                        elif what == "scale2":
                            need(dve, kept, 32 * b)
                            norm_scale(nc, dve, m, norm2, m.ln2_mv, m.ln2_rstd, m.xn2[:, v], b)
                        elif what == "conv":
                            settle(dve, m, tail_read, turn["tail"](s, what) + 1)
                            nc.vector.bn_stats(m.bn_parts[:, b, :], m.gate_in[:, bass.ds(b * SEQ, SEQ)]).then_inc(bn_ok, 1)

                steps(dve, step)

            @block.gpsimd
            def _(pool):
                def step(s, u):
                    for what, lag, k in order:
                        b, v = s - lag, (u - lag) % RING
                        if not live(b):
                            continue
                        if what == "left":
                            pool.wait_ge(exps_ok, b + 1)
                            need(pool, gated_ok, NGATE * b)
                            nc.gpsimd.tensor_tensor(gates[:], e_all[:], e_left[:], ALU.subtract).then_inc(gates_ok, 1)
                            need(pool, gate_read, turn["gate"](s, "xgT"))
                            nc.gpsimd.tensor_tensor(xb[:], m.x[:, bass.ds(b * QT, QT), :],
                                                    m.b_ffn[:].unsqueeze(1).broadcast_to([P, QT, D]),
                                                    ALU.add).then_inc(xb_ok, 1)
                        elif what == "xgT":
                            pool.wait_ge(gated_ok, NGATE * (b + 1))
                            pool.wait_ge(xb_ok, 2 * b + 1)
                            nc.gpsimd.tensor_tensor(xb[:], xb[:], gated[:], ALU.add).then_inc(xb_ok, 1)
                        elif what == "all":
                            settle(pool, m, exps_ok, b - 2)
                            settle(pool, m, top_ok, 8 * ROUNDS * b + NGATE)
                            nc.gpsimd.tensor_scalar(neg_top[:, v], top8[:, :, 0, 0], -1.0, None,
                                                    ALU.mult).then_inc(neg_ok, 1)
                        elif what == "rstd":
                            norm_rstd(nc, pool, m, norm, m.ln_mv, m.ln_rstd, b)
                        elif what == "rstd2":
                            norm_rstd(nc, pool, m, norm2, m.ln2_mv, m.ln2_rstd, b)
                        elif what == "rot":
                            pool.wait_ge(proj_read, turn["proj"](s, what) + 1)
                            nc.gpsimd.tensor_tensor(m.qkT[:], m.rope_terms[:, 0], m.rope_terms[:, 1],
                                                    ALU.add).then_inc(qk_ok, 1)
                        elif what == "s":
                            settle(pool, m, att_read, turn["att"](s, what))
                            settle(pool, m, max_ok, b + 1)
                            nc.gpsimd.tensor_scalar(nmax_s[:], nmax[:], D ** -0.5, None, ALU.mult).then_inc(nmax_ok, 1)

                steps(pool, step)

            @block.sync
            def _(sp):
                def load(b, v):
                    settle(sp, m, loaded, 48 * b)
                    settle(sp, m, gated_ok, NGATE * (b - 2))
                    sp.dma_start(xa[0:NL, v, :], m.gate_in[:, bass.ds(b * SEQ, SEQ)]).then_inc(loaded, 16)
                    sp.dma_start(xnT_f[:, v, :], m.xnT_hbm[n, b]).then_inc(loaded, 16)
                    sp.dma_start(xn_f[:, v].rearrange("p a b -> p (a b)"), m.xn_hbm[n, b]).then_inc(loaded, 16)

                load(0, 0)

                def step(s, u):
                    for what, lag, k in order:
                        b, v = s - lag, (u - lag) % RING
                        if not live(b):
                            continue
                        if what == "load":
                            load(b, v)
                        elif what == "conv":
                            settle(sp, m, kept, 32 * b)
                            settle(sp, m, tail_read, turn["tail"](s, what) + 1)
                            sp.dma_start(m.xn_hbm[1, b], m.xn2[:, v].rearrange("p a b -> p (a b)")).then_inc(kept, 16)
                            sp.dma_start(m.xnT_hbm[1, b], m.xnT2[:, v, :]).then_inc(kept, 16)
                        elif what == "o" and not with_attention:
                            settle(sp, m, gate_read, turn["gate"](s, what) + 1)
                            sp.dma_start(m.out_dram[:, b], m.x[:, bass.ds(b * QT, QT), :]).then_inc(stored, 16)

                steps(sp, step)
                if with_attention:
                    sp.wait_ge(kept, 32 * NSEQ)
                else:
                    sp.wait_ge(stored, 16 * NSEQ)


def kernel(**inputs):
    import ml_dtypes as _ml
    import numpy as _np
    import concourse.bacc as _bacc
    from concourse.bass_utils import run_bass_kernel_spmd as _run

    f32 = _np.float32

    def got(name):
        return _np.ascontiguousarray(inputs["L0_" + name])

    order = [(par, d, pair) for par in range(2) for d in range(HD) for pair in range(NPAIR)]

    def column(par, d, pair):
        return (2 * pair + par) * HD + d

    cols = _np.array([column(*o) for o in order])
    partners = _np.array([column(par, d ^ 1 if 2 <= d < 6 else d, pair) for par, d, pair in order])
    n = _np.arange(SEQ)
    rope_a = _np.zeros((P, 2, SEQ), f32)
    for c, (par, d, pair) in enumerate(order):
        if 2 <= d < 6:
            angle = (n // 16 if d < 4 else n % 16).astype(f32)
            rope_a[c, 0], rope_a[c, 1] = _np.cos(angle), _np.sin(angle) if d % 2 else -_np.sin(angle)
        else:
            rope_a[c, 0] = 1.0
    inv = (f32(1.0) / f32(10000.0) ** (_np.arange(0, D, 2, dtype=f32) / f32(D))).astype(f32)
    angle = n.astype(f32)[:, None] * inv[None, :]
    rope_b = _np.zeros((D // 2, 2, 2, SEQ), f32)
    for e in range(2):
        rope_b[:, e, 0] = _np.cos(angle).T
        rope_b[:, e, 1] = (_np.sin(angle) if e else -_np.sin(angle)).T
    turned = _np.arange(D) ^ 1

    def weights(wq, wk, wv, take, partner):
        return _np.concatenate([wq[:, take], wk[:, take], wq[:, partner], wk[:, partner], wv], axis=1)

    def biases(bq, bk, take, partner):
        return _np.stack([bq[take], bk[take], bq[partner], bk[partner]], axis=1)

    w_conv = _np.zeros((D, NL), f32)
    w_gate = _np.zeros((NL + 1, 2 * D), f32)
    for i, gate in enumerate(("so", "si")):
        conv = got(f"ffn_{gate}_conv_w")
        for g in range(NG):
            w_conv[4 * g:4 * g + 4, i * NG + g] = conv[g]
        w_gate[i * NG:(i + 1) * NG, i * D:(i + 1) * D] = got(f"ffn_{gate}_lin_w").T
        w_gate[NL, i * D:(i + 1) * D] = got(f"ffn_{gate}_lin_b")
    norm_gate = _np.stack([_np.concatenate([got(f"ffn_so_{k}"), got(f"ffn_si_{k}")])
                           for k in ("conv_b", "gamma", "beta")], axis=1)
    k_ones = _np.zeros((2, 3, NPAIR, 2, SEQ), f32)
    for par in range(2):
        k_ones[par, :, :, par, :] = 1.0
    arrays = {
        "x": got("attn_a_hidden_states"),
        "ident": _np.eye(P, dtype=f32),
        "ident_bf": _np.eye(P, dtype=f32).astype(_ml.bfloat16),
        "k_ones": k_ones.reshape(MAXROWS, NH, SEQ).astype(_ml.bfloat16),
        "rope_a": rope_a,
        "rope_b": rope_b.reshape(D, 2, SEQ),
        "w_qkv_a": weights(got("attn_a_Wq"), got("attn_a_Wk"), got("attn_a_Wv"), cols, partners),
        "b_qk_a": biases(got("attn_a_bq"), got("attn_a_bk"), cols, partners),
        "b_v_a": got("attn_a_bv"),
        "w_o": got("attn_a_Wo"),
        "b_o": got("attn_a_bo"),
        "w_qkv_b": weights(got("attn_b_wq_w").T, got("attn_b_wk_w").T, got("attn_b_wv_w").T, _np.arange(D), turned),
        "b_qk_b": biases(got("attn_b_wq_b"), got("attn_b_wk_b"), _np.arange(D), turned),
        "b_v_b": got("attn_b_wv_b"),
        "w_conv": w_conv,
        "norm_gate": norm_gate,
        "w_gate": w_gate,
        "w_ffn": got("ffn_weight"),
        "b_ffn": got("ffn_bias"),
    }
    arrays = {k: _np.ascontiguousarray(a) for k, a in arrays.items()}
    nc = _bacc.Bacc("TRN2", target_bir_lowering=False, num_devices=1)
    t = {k: nc.dram_tensor("in_" + k, a.shape, mybir.dt.from_np(a.dtype), kind="ExternalInput").ap()
         for k, a in arrays.items()}
    out = nc.dram_tensor("out_0", (NSEQ, SEQ, D), F32, kind="ExternalOutput").ap()
    program(nc, t, out)
    r = _run(nc, [{"in_" + k: a for k, a in arrays.items()}], core_ids=[0])
    return r.results[0]["out_0"]
```

```python
from contextlib import ExitStack

import concourse.bass as bass
from concourse import mybir

F32 = mybir.dt.float32
BF16 = mybir.dt.bfloat16
ALU = mybir.AluOpType
ACT = mybir.ActivationFunctionType
AX = mybir.AxisListType

P = 128
NSEQ, SEQ, D = 32, 256, 128
QT = SEQ // P
NH, HD = 16, 8
NPAIR = NH // 2
NSLOT = 6
ROWS = NSLOT * HD
DATA = 2 * ROWS
MAXROWS = 6
VW = 32
HW = VW // 2
NG = D // 4
NL = 2 * NG
ROUNDS = 4
NGATE = QT * 2
EPS = 1e-5
LOWEST = -3.0e38
RING = 3
FIRST_LOOPED, LOOP_TRIPS = 5, 8
STEPS = NSEQ + 4


def steps(eng, step):
    for s in range(FIRST_LOOPED):
        step(s, s % RING)
    with eng.Fori(0, LOOP_TRIPS) as trip:
        for r in range(RING):
            step(trip * RING + (FIRST_LOOPED + r), (FIRST_LOOPED + r) % RING)
    for s in range(FIRST_LOOPED + LOOP_TRIPS * RING, STEPS):
        step(s, s % RING)


def live(b):
    return not isinstance(b, int) or 0 <= b < NSEQ


def need(eng, sem, value):
    if isinstance(value, int) and value <= 0:
        return
    eng.wait_ge(sem, value)


def settle(eng, m, sem, value):
    if isinstance(value, int):
        need(eng, sem, value)
        return
    register = eng.compute_val(value)
    eng.wait_ge(m.fills, 1)
    eng.wait_ge(sem, register)


def counter(order, users):
    mine = [e for e in order if (e[0], e[2]) in users]

    def turn(s, what, k=0):
        place = [(e[0], e[2]) for e in mine].index((what, k))
        if isinstance(s, int):
            return (sum(live(i - e[1]) for i in range(s) for e in mine)
                    + sum(live(s - e[1]) for e in mine[:place]))
        start = sum(live(i - e[1]) for i in range(FIRST_LOOPED) for e in mine)
        return (s - FIRST_LOOPED) * len(mine) + (start + place)

    return turn


class Model:
    pass


def program(nc, t, out):
    with ExitStack() as ctx:
        m = Model()

        def sb(name, shape, dt=F32):
            return ctx.enter_context(nc.sbuf_tensor(name, shape, dt))

        def dram(name, shape, dt=F32):
            return nc.dram_tensor(name, shape, dt).ap()

        m.x = sb("x", [P, NSEQ * QT, D])
        m.gate_in = sb("gate_in", [NL, NSEQ * SEQ])
        m.bn_parts = sb("bn_parts", [NL, NSEQ, 6])
        m.ident = sb("ident", [P, P])
        m.ident_bf = sb("ident_bf", [P, P], BF16)
        m.w_qkv_a = sb("w_qkv_a", [P, 5 * D])
        m.b_qk_a = sb("b_qk_a", [P, 4])
        m.b_v_a = sb("b_v_a", [P, D])
        m.w_o = sb("w_o", [P, D])
        m.b_o = sb("b_o", [P, D])
        m.rope_a = sb("rope_a", [P, 2, SEQ])
        m.w_qkv_b = sb("w_qkv_b", [P, 5 * D])
        m.b_qk_b = sb("b_qk_b", [P, 4])
        m.b_v_b = sb("b_v_b", [P, D])
        m.rope_b = sb("rope_b", [P, 2, SEQ])
        m.w_conv = sb("w_conv", [P, NL])
        m.norm_gate = sb("norm_gate", [NL, 3])
        m.w_gate = sb("w_gate", [NL + 1, 2 * D])
        m.w_ffn = sb("w_ffn", [P, D])
        m.b_ffn = sb("b_ffn", [P, D])
        m.neg_half = sb("neg_half", [P, QT])

        m.ln_st = sb("ln_st", [P, QT, 6])
        m.ln_mv = sb("ln_mv", [P, QT, 2])
        m.ln_rstd = sb("ln_rstd", [P, QT])
        m.ln2_st = sb("ln2_st", [P, QT, 6])
        m.ln2_mv = sb("ln2_mv", [P, QT, 2])
        m.ln2_rstd = sb("ln2_rstd", [P, QT])
        m.xn = sb("xn", [P, RING, QT, D])
        m.xn2 = sb("xn2", [P, RING, QT, D])
        m.xnT = sb("xnT", [P, SEQ])
        m.xnT2 = sb("xnT2", [P, RING, SEQ])
        m.rope_terms = sb("rope_terms", [P, 2, 2 * SEQ])
        m.qkT = sb("qkT", [P, 2 * SEQ])

        m.stack_hbm = dram("stack_hbm", [2, 2, NSLOT, HD * NPAIR, SEQ], BF16)
        m.xn_hbm = dram("xn_hbm", [2, NSEQ, P, QT * D])
        m.xnT_hbm = dram("xnT_hbm", [2, NSEQ, P, SEQ])

        m.consts_first = ctx.enter_context(nc.semaphore("consts_first"))
        m.consts = ctx.enter_context(nc.semaphore("consts"))
        m.x_first = ctx.enter_context(nc.semaphore("x_first"))
        m.x_all = ctx.enter_context(nc.semaphore("x_all"))
        m.fills = ctx.enter_context(nc.semaphore("fills"))

        first = [(m.ident, "ident"), (m.w_qkv_a, "w_qkv_a"), (m.rope_a, "rope_a"), (m.b_qk_a, "b_qk_a"),
                 (m.ident_bf, "ident_bf")]
        tables = [(m.w_o, "w_o"), (m.w_conv, "w_conv"), (m.norm_gate, "norm_gate"), (m.w_gate, "w_gate"),
                  (m.w_ffn, "w_ffn"), (m.w_qkv_b, "w_qkv_b"), (m.rope_b, "rope_b"), (m.b_qk_b, "b_qk_b")]
        rows = [(m.b_o, "b_o"), (m.b_v_b, "b_v_b"), (m.b_ffn, "b_ffn")]
        m.n_first = 16 * (len(first) + 1)
        m.n_consts = 16 * (len(tables) + len(rows))
        x_dram = t["x"].rearrange("b (q p) d -> p (b q) d", p=P)
        m.out_dram = out.rearrange("b (q p) d -> p b q d", p=P)

        with nc.Block() as block:
            @block.sync
            def _(sp):
                sp.dma_start(m.x[:, 0:8, :], x_dram[:, 0:8, :]).then_inc(m.x_first, 16)
                for dst, name in first:
                    sp.dma_start(dst[:], t[name]).then_inc(m.consts_first, 16)
                sp.dma_start(m.b_v_a[:], t["b_v_a"].partition_broadcast(P)).then_inc(m.consts_first, 16)
                for dst, name in tables:
                    sp.dma_start(dst[:], t[name]).then_inc(m.consts, 16)
                for dst, name in rows:
                    sp.dma_start(dst[:], t[name].partition_broadcast(P)).then_inc(m.consts, 16)
                sp.dma_start(m.x[:, 8:, :], x_dram[:, 8:, :]).then_inc(m.x_all, 16)

            @block.vector
            def _(dve):
                nc.vector.memset(m.neg_half[:], -0.5).then_inc(m.fills, 1)

        attention_a(nc, m, t)
        for n in range(2):
            feed_forward(nc, m, n)



class Norm:

    def __init__(self, ctx, nc, name):
        self.parts_ok = ctx.enter_context(nc.semaphore(name + "_parts_ok"))
        self.stats_ok = ctx.enter_context(nc.semaphore(name + "_stats_ok"))
        self.eps_ok = ctx.enter_context(nc.semaphore(name + "_eps_ok"))
        self.rstd_ok = ctx.enter_context(nc.semaphore(name + "_rstd_ok"))
        self.xn_ok = ctx.enter_context(nc.semaphore(name + "_xn_ok"))


def norm_stats(nc, dve, m, sems, st, mv, b):
    settle(dve, m, sems.xn_ok, QT * b)
    for qt in range(QT):
        nc.vector.bn_stats(st[:, qt, :], m.x[:, b * QT + qt, :]).then_inc(sems.parts_ok, 1)
    for qt in range(QT):
        settle(dve, m, sems.parts_ok, QT * b + QT)
        nc.vector.bn_aggr(mv[:, qt, :], st[:, qt, :]).then_inc(sems.stats_ok, 1)


def norm_rstd(nc, pool, m, sems, mv, rstd, b):
    settle(pool, m, sems.stats_ok, QT * (b + 1))
    nc.gpsimd.tensor_scalar(rstd[:], mv[:, :, 1], EPS, None, ALU.add).then_inc(sems.eps_ok, 1)
    pool.wait_ge(sems.eps_ok, b + 1)
    nc.gpsimd.tensor_tensor(rstd[:], rstd[:], m.neg_half[:], ALU.pow).then_inc(sems.rstd_ok, 1)


def norm_rstd_shift(nc, pool, m, sems, mv, rstd, shift, b):
    settle(pool, m, sems.stats_ok, QT * (b + 1))
    nc.gpsimd.tensor_scalar(rstd[:], mv[:, :, 1], EPS, None, ALU.add).then_inc(sems.eps_ok, 1)
    nc.gpsimd.tensor_scalar(shift[:], mv[:, :, 0], -1.0, None, ALU.mult).then_inc(sems.eps_ok, 1)
    pool.wait_ge(sems.eps_ok, 3 * b + 1)
    nc.gpsimd.tensor_tensor(rstd[:], rstd[:], m.neg_half[:], ALU.pow).then_inc(sems.eps_ok, 1)
    pool.wait_ge(sems.eps_ok, 3 * (b + 1))
    nc.gpsimd.tensor_tensor(shift[:], shift[:], rstd[:], ALU.mult).then_inc(sems.rstd_ok, 1)


def norm_apply(nc, act, m, sems, rstd, shift, dst, b):
    settle(act, m, sems.rstd_ok, b + 1)
    for qt in range(QT):
        nc.scalar.activation(dst[:, qt, :], m.x[:, b * QT + qt, :], ACT.Identity, bias=shift[:, qt:qt + 1],
                             scale=rstd[:, qt:qt + 1]).then_inc(sems.xn_ok, 1)


def norm_scale(nc, dve, m, sems, mv, rstd, dst, b):
    dve.wait_ge(sems.rstd_ok, b + 1)
    for qt in range(QT):
        nc.vector.tensor_scalar(dst[:, qt, :], m.x[:, b * QT + qt, :], mv[:, qt, 0:1], rstd[:, qt:qt + 1],
                                ALU.subtract, ALU.mult).then_inc(sems.xn_ok, 1)


def project(nc, m, w, i, bank):
    for q in range(2):
        mm = nc.tensor.matmul(bank[:, q * SEQ:(q + 1) * SEQ], w[:, (2 * i + q) * D:(2 * i + q + 1) * D], m.xnT[:],
                              start=True, stop=True)
    return mm


def rope_term(nc, m, bias, table, i, bank, sem, last):
    for q in range(2):
        nc.vector.scalar_tensor_tensor(out=m.rope_terms[:, i, q * SEQ:(q + 1) * SEQ], in0=bank[:, q * SEQ:(q + 1) * SEQ],
                                       scalar=bias[:, 2 * i + q:2 * i + q + 1], in1=table[:, i, :],
                                       op0=ALU.add, op1=ALU.mult).then_inc(last if q else sem, 1)



ORDER_A = [
    ("proj", 4, 0), ("st", 3, 4), ("v", 1, 0), ("read_proj", 4, 0), ("read_v", 1, 0), ("max", 2, 8), ("st", 3, 5),
    ("max", 2, 9), ("cut_max", 2, 0), ("xnT", 0, 0), ("read_xnT", 0, 0), ("pv", 3, 1), ("max", 2, 10),
    ("max", 2, 11), ("rstd2", 4, 0), ("main", 0, 0), ("read_main", 0, 0), ("max", 2, 12), ("max", 2, 13),
    ("st", 3, 6), ("mT", 2, 0), ("read_mT", 2, 0), ("rot", 0, 0), ("read_rot", 0, 0), ("max", 2, 14),
    ("scale2", 4, 0), ("cut", 0, 0), ("st", 3, 7), ("ln", -1, 0), ("pv", 3, 2), ("max", 2, 15), ("st", 2, 0),
    ("xnT2", 4, 0), ("read_xnT2", 4, 0), ("cut_max", 2, 1), ("st", 2, 1), ("rstd", -1, 0), ("max", 1, 0),
    ("cut", 0, 1), ("max", 1, 1), ("pv", 3, 3), ("read_pv", 3, 0), ("max", 1, 2), ("max", 1, 3), ("st", 2, 2),
    ("mT", 2, 1), ("read_mT", 2, 1), ("max", 1, 4), ("max", 1, 5), ("ctx", 3, 0), ("st", 2, 3), ("read_ctx", 3, 0),
    ("pv", 2, 0), ("max", 1, 6), ("ctxT", 3, 0), ("scale", -1, 0), ("conv", 4, 0), ("read_ctxT", 3, 0),
    ("xb", 3, 0), ("read_conv", 4, 0), ("keep", 4, 0), ("max", 1, 7), ("bn", 4, 0),
]
DVE_BANK = [("proj", 0), ("v", 0), ("main", 0), ("rot", 0), ("ctx", 0)]
ACT_BANK = [("xnT", 0), ("mT", 0), ("xnT2", 0), ("mT", 1), ("ctxT", 0), ("conv", 0)]


def attention_a(nc, m, t):
    with ExitStack() as ctx:
        def sb(name, shape, dt=F32):
            return ctx.enter_context(nc.sbuf_tensor(name, shape, dt))

        def psum(name, shape):
            return ctx.enter_context(nc.psum_tensor(name, shape, F32))

        def sem(name):
            return ctx.enter_context(nc.semaphore("a_" + name))

        rest = sb("rest", [P, 2 * SEQ])
        parts = sb("parts", [P, 3, 2 * SEQ], BF16)
        q_stack = sb("q_stack", [P, RING, NPAIR, SEQ], BF16)
        k_stack = sb("k_stack", [P, RING, NH, SEQ], BF16)
        v_aug = sb("v_aug", [P, RING, QT, NPAIR, 2, VW + HW])
        nmax = sb("nmax", [P, 2, QT, 4, 2])
        nmax_rest = sb("nmax_rest", [P, 2, QT, 4, 2])
        nmax_parts = sb("nmax_parts", [P, 2, QT, 4, 2, 3], BF16)
        probs = sb("probs", [P, 4, 2, QT, SEQ])
        ctxT_raw = sb("ctxT_raw", [P, 2, SEQ])
        z_inv = sb("z_inv", [P, QT, NH])
        ctx_tok = sb("ctx_tok", [P, QT, D])
        ctxT = sb("ctxT", [P, SEQ])
        xb = sb("xb", [P, QT, D])
        st_bank = psum("st_bank", [P, RING, QT, SEQ])
        s_bank = psum("s_bank", [P, 2, QT, SEQ])
        pv_bank = psum("pv_bank", [P, 2, SEQ])
        dve_bank = psum("dve_bank", [P, 2 * SEQ])[:]
        act_bank = psum("act_bank", [P, 2 * SEQ])[:]
        act_bank_bf = act_bank.bitcast(BF16)
        dve_turn, act_turn = counter(ORDER_A, DVE_BANK), counter(ORDER_A, ACT_BANK)

        dve_ps, dve_read = sem("dve_ps"), sem("dve_read")
        act_ps, act_read = sem("act_ps"), sem("act_read")
        norm, norm2 = Norm(ctx, nc, "a_ln"), Norm(ctx, nc, "a_ln2")
        term_ok = sem("term_ok")
        qk_ok = sem("qk_ok")
        cut = sem("cut")
        parts_ok = sem("parts_ok")
        q_out = sem("q_out")
        k_out = sem("k_out")
        stack_in = sem("stack_in")
        k_clear = sem("k_clear")
        k_ones = sem("k_ones")
        v_fill = sem("v_fill")
        s_ps = sem("s_ps")
        max_ok = sem("max_ok")
        cut_max = sem("cut_max")
        nmax_ok = sem("nmax_ok")
        st_ps = sem("st_ps")
        probs_ok = sem("probs_ok")
        pv_ps = sem("pv_ps")
        pv_ok = sem("pv_ok")
        z_ok = sem("z_ok")
        xb_ok = sem("xb_ok")
        bn_ok = sem("bn_ok")
        kept = sem("kept")

        with nc.Block() as block:
            @block.tensor
            def _(pe):
                pe.wait_ge(m.consts_first, m.n_first)

                def step(s, u):
                    if isinstance(s, int) and s == 1:
                        pe.wait_ge(m.consts, m.n_consts)
                        pe.wait_ge(k_ones, 16 * RING)
                        pe.wait_ge(v_fill, 2)
                    for what, lag, k in ORDER_A:
                        b, v = s - lag, (u - lag) % RING
                        if not live(b):
                            continue
                        if (what, k) in DVE_BANK:
                            need(pe, dve_read, dve_turn(s, what, k))
                        if (what, k) in ACT_BANK:
                            need(pe, act_read, act_turn(s, what, k))
                        if what == "st":
                            if k % 4 == 0:
                                pe.wait_ge(act_read, act_turn(s if k == 0 else s - 1, "mT", k // 4) + 1)
                            if k == 0:
                                pe.wait_ge(stack_in, 16 * 4 * (b + 1))
                            for par in range(2):
                                h = 2 * k + par
                                need(pe, probs_ok, NH * b + h - 2)
                                for kt in range(QT):
                                    mm = nc.tensor.matmul(
                                        st_bank[:, (h + v) % RING, kt, :],
                                        k_stack[0:DATA + MAXROWS, v, h, kt * P:(kt + 1) * P],
                                        q_stack[0:DATA + MAXROWS, v, k, :], start=True, stop=True)
                                mm.then_inc(st_ps, 1)
                        elif what == "pv":
                            pe.wait_ge(probs_ok, NH * b + 4 * k + 4)
                            if k == 0:
                                need(pe, pv_ok, b)
                                pe.wait_ge(dve_read, dve_turn(s - 1, "v") + 1)
                                pe.wait_ge(v_fill, 2)
                            for pair in (2 * k, 2 * k + 1):
                                j = pair % 4
                                for par in range(2):
                                    for kt in range(QT):
                                        mm = nc.tensor.matmul(
                                            pv_bank[VW * j:VW * (j + 1), pair // 4, :],
                                            v_aug[:, v, kt, pair].rearrange("p a b -> p (a b)")[:, VW * par:VW * (par + 1)],
                                            probs[:, pair % 4, par, kt, :],
                                            start=(par == 0 and kt == 0), stop=(par == 1 and kt == QT - 1))
                            mm.then_inc(pv_ps, 1)
                        elif what == "max":
                            if k == 0:
                                pe.wait_ge(stack_in, 16 * 4 * (b + 1))
                            need(pe, max_ok, 16 * b + k - 1)
                            for qt in range(QT):
                                mm = nc.tensor.matmul(s_bank[:, k % 2, qt, :],
                                                      q_stack[0:DATA, v, k // 2, qt * P:(qt + 1) * P],
                                                      k_stack[0:DATA, v, k, :], start=True, stop=True)
                            mm.then_inc(s_ps, 1)
                        elif what == "mT":
                            pe.wait_ge(nmax_ok, 2 * b + k + 1)
                            pe.wait_ge(v_fill, 2)
                            for j in range(4):
                                for qt in range(QT):
                                    mm = nc.tensor.transpose(
                                        act_bank_bf[DATA:DATA + MAXROWS, j * SEQ + qt * P:j * SEQ + (qt + 1) * P],
                                        nmax_parts[:, k, qt, j].rearrange("p a b -> p (a b)"), m.ident_bf[:])
                            mm.then_inc(act_ps, 1)
                        elif what == "xnT":
                            pe.wait_ge(norm.xn_ok, QT * (b + 1))
                            for qt in range(QT):
                                mm = nc.tensor.transpose(act_bank[:, qt * P:(qt + 1) * P], m.xn[:, v, qt, :], m.ident[:])
                            mm.then_inc(act_ps, 1)
                        elif what in ("main", "rot"):
                            pe.wait_ge(act_read, act_turn(s, "xnT") + 1)
                            project(nc, m, m.w_qkv_a, int(what == "rot"), dve_bank).then_inc(dve_ps, 1)
                        elif what == "v":
                            for qt in range(QT):
                                mm = nc.tensor.matmul(dve_bank[:, SEQ + qt * D:SEQ + (qt + 1) * D], m.xnT[:, qt * P:(qt + 1) * P],
                                                      m.w_qkv_a[:, 4 * D:], start=True, stop=True)
                            mm.then_inc(dve_ps, 1)
                        elif what == "ctx":
                            pe.wait_ge(pv_ok, b + 1)
                            for qt in range(QT):
                                for g in range(2):
                                    mm = nc.tensor.transpose(dve_bank[:, (2 * qt + g) * P:(2 * qt + g + 1) * P],
                                                             ctxT_raw[:, g, qt * P:(qt + 1) * P], m.ident[:])
                            mm.then_inc(dve_ps, 1)
                        elif what == "ctxT":
                            pe.wait_ge(dve_read, dve_turn(s, "ctx") + 1)
                            for qt in range(QT):
                                mm = nc.tensor.transpose(act_bank[:, qt * P:(qt + 1) * P], ctx_tok[:, qt, :], m.ident[:])
                            mm.then_inc(act_ps, 1)
                        elif what == "proj":
                            pe.wait_ge(act_read, act_turn(s - 1, "ctxT") + 1)
                            for qt in range(QT):
                                mm = nc.tensor.matmul(dve_bank[:, qt * D:(qt + 1) * D], ctxT[:, qt * P:(qt + 1) * P],
                                                      m.w_o[:], start=True, stop=True)
                            mm.then_inc(dve_ps, 1)
                        elif what == "xnT2":
                            pe.wait_ge(norm2.xn_ok, QT * (b + 1))
                            for qt in range(QT):
                                mm = nc.tensor.transpose(act_bank[:, qt * P:(qt + 1) * P], m.xn2[:, v, qt, :], m.ident[:])
                            mm.then_inc(act_ps, 1)
                        elif what == "conv":
                            pe.wait_ge(act_read, act_turn(s, "xnT2") + 1)
                            pe.wait_ge(v_fill, 2)
                            nc.tensor.matmul(act_bank[0:NL, SEQ:2 * SEQ], m.w_conv[:], m.xnT2[:, v, :],
                                             start=True, stop=True).then_inc(act_ps, 1)

                steps(pe, step)

            @block.scalar
            def _(act):
                def step(s, u):
                    for what, lag, k in ORDER_A:
                        b, v, source = s - lag, (u - lag) % RING, what.removeprefix("read_")
                        if not live(b):
                            continue
                        if source != what and (source, k) in ACT_BANK:
                            settle(act, m, act_ps, act_turn(s, source, k) + 1)
                        if what == "st":
                            need(act, pv_ps, 4 * b + k // 2 - 1)
                            for par in range(2):
                                h = 2 * k + par
                                act.wait_ge(st_ps, NH * b + h + 1)
                                nc.scalar.activation(probs[:, k % 4, par].rearrange("p b c -> p (b c)"),
                                                     st_bank[:, (h + v) % RING].rearrange("p b c -> p (b c)"), ACT.Exp,
                                                     scale=HD ** -0.5).then_inc(probs_ok, 1)
                        elif what == "read_pv":
                            act.wait_ge(pv_ps, 4 * (b + 1))
                            nc.scalar.copy(ctxT_raw[:], pv_bank[:]).then_inc(pv_ok, 1)
                        elif what == "read_mT":
                            nc.scalar.copy(q_stack[DATA:DATA + MAXROWS, v, 4 * k:4 * k + 4, :].rearrange("p a b -> p (a b)"),
                                           act_bank_bf[DATA:DATA + MAXROWS, :]).then_inc(act_read, 1)
                        elif what == "read_xnT":
                            nc.scalar.copy(m.xnT[:], act_bank[:, 0:SEQ]).then_inc(act_read, 1)
                        elif what == "read_ctxT":
                            nc.scalar.copy(ctxT[:], act_bank[:, 0:SEQ]).then_inc(act_read, 1)
                        elif what == "read_xnT2":
                            need(act, kept, 32 * b)
                            nc.scalar.copy(m.xnT2[:, v, :], act_bank[:, 0:SEQ]).then_inc(act_read, 1)
                        elif what == "read_conv":
                            nc.scalar.activation(m.gate_in[:, bass.ds(b * SEQ, SEQ)], act_bank[0:NL, SEQ:2 * SEQ], ACT.Identity,
                                                 bias=m.norm_gate[:, 0:1]).then_inc(act_read, 1)

                steps(act, step)

            @block.vector
            def _(dve):
                dve.wait_ge(m.x_first, 16)
                norm_stats(nc, dve, m, norm, m.ln_st, m.ln_mv, 0)
                norm_scale(nc, dve, m, norm, m.ln_mv, m.ln_rstd, m.xn[:, 0], 0)
                nc.vector.memset(v_aug[:], 0.0).then_inc(v_fill, 1)
                dve.wait_ge(v_fill, 1)
                nc.vector.memset(v_aug[:, :, :, :, :, HD:HD + 1].rearrange("p r a t b c -> p (r a t b) c"), 1.0).then_inc(v_fill, 1)

                def step(s, u):
                    if isinstance(s, int) and s == FIRST_LOOPED - 2:
                        dve.wait_ge(m.x_all, 16)
                    for what, lag, k in ORDER_A:
                        b, v, source = s - lag, (u - lag) % RING, what.removeprefix("read_")
                        if not live(b):
                            continue
                        if what == "max":
                            dve.wait_ge(s_ps, 16 * b + k + 1)
                            if k % 8 == 0:
                                need(dve, nmax_ok, 2 * b + k // 8 - 1)
                            nc.vector.tensor_reduce(nmax[:, k // 8, :, k // 2 % 4, k % 2], s_bank[:, k % 2], AX.X,
                                                    ALU.max, negate=True).then_inc(max_ok, 1)
                        elif what == "read_main":
                            dve.wait_ge(dve_ps, dve_turn(s, source) + 1)
                            need(dve, qk_ok, 2 * b)
                            rope_term(nc, m, m.b_qk_a, m.rope_a, 0, dve_bank, term_ok, dve_read)
                        elif what == "read_rot":
                            dve.wait_ge(dve_ps, dve_turn(s, source) + 1)
                            rope_term(nc, m, m.b_qk_a, m.rope_a, 1, dve_bank, term_ok, dve_read)
                        elif what == "read_v":
                            dve.wait_ge(dve_ps, dve_turn(s, source) + 1)
                            need(dve, pv_ps, 4 * (b - 2))
                            for qt in range(QT):
                                e = nc.vector.tensor_tensor(
                                    v_aug[:, v, qt, :, :, 0:HD],
                                    dve_bank[:, SEQ + qt * D:SEQ + (qt + 1) * D].rearrange("p (t r d) -> p t r d", r=2, d=HD),
                                    m.b_v_a[:].rearrange("p (t r d) -> p t r d", r=2, d=HD),
                                    ALU.add)
                            e.then_inc(dve_read, 1)
                        elif what == "read_ctx":
                            dve.wait_ge(dve_ps, dve_turn(s, "ctx") + 1)
                            heads = dve_bank.rearrange("p (a h c) -> p a h c", a=QT, c=HW)
                            nc.vector.reciprocal(z_inv[:], heads[:, :, :, HD]).then_inc(z_ok, 1)
                            dve.wait_ge(z_ok, b + 1)
                            nc.vector.tensor_tensor(
                                ctx_tok[:].rearrange("p a (h d) -> p a h d", d=HD),
                                heads[:, :, :, 0:HD], z_inv[:].unsqueeze(3).broadcast_to([P, QT, NH, HD]),
                                ALU.mult).then_inc(dve_read, 1)
                        elif what == "read_proj":
                            dve.wait_ge(dve_ps, dve_turn(s, "proj") + 1)
                            dve.wait_ge(xb_ok, b + 1)
                            nc.vector.tensor_tensor(m.x[:, bass.ds(b * QT, QT), :],
                                                    dve_bank[:, 0:QT * D].rearrange("p (a b) -> p a b", a=QT), xb[:],
                                                    ALU.add).then_inc(dve_read, 1)
                            settle(dve, m, dve_read, dve_turn(s, "proj") + 1)
                            norm_stats(nc, dve, m, norm2, m.ln2_st, m.ln2_mv, b)
                        elif what == "scale2":
                            need(dve, kept, 32 * b)
                            norm_scale(nc, dve, m, norm2, m.ln2_mv, m.ln2_rstd, m.xn2[:, v], b)
                        elif what == "ln":
                            norm_stats(nc, dve, m, norm, m.ln_st, m.ln_mv, b)
                        elif what == "scale":
                            norm_scale(nc, dve, m, norm, m.ln_mv, m.ln_rstd, m.xn[:, v], b)
                        elif what == "bn":
                            settle(dve, m, act_read, act_turn(s, "conv") + 1)
                            nc.vector.bn_stats(m.bn_parts[:, b, :], m.gate_in[:, bass.ds(b * SEQ, SEQ)]).then_inc(bn_ok, 1)

                steps(dve, step)

            @block.gpsimd
            def _(pool):
                norm_rstd(nc, pool, m, norm, m.ln_mv, m.ln_rstd, 0)
                nc.gpsimd.memset(k_stack[:], 0.0).then_inc(k_clear, 1)

                def step(s, u):
                    if isinstance(s, int) and s == 1:
                        pool.wait_ge(m.consts, m.n_consts)
                    for what, lag, k in ORDER_A:
                        b, v = s - lag, (u - lag) % RING
                        if not live(b):
                            continue
                        if what == "rstd":
                            norm_rstd(nc, pool, m, norm, m.ln_mv, m.ln_rstd, b)
                        elif what == "rstd2":
                            norm_rstd(nc, pool, m, norm2, m.ln2_mv, m.ln2_rstd, b)
                        elif what == "xb":
                            nc.gpsimd.tensor_tensor(xb[:], m.x[:, bass.ds(b * QT, QT), :],
                                                    m.b_o[:].unsqueeze(1).broadcast_to([P, QT, D]),
                                                    ALU.add).then_inc(xb_ok, 1)
                        elif what == "cut_max":
                            whole = nmax[:, k].rearrange("p a t r -> p (a t r)")
                            left = nmax_rest[:, k].rearrange("p a t r -> p (a t r)")
                            part = nmax_parts[:, k].rearrange("p a t r c -> p (a t r) c")
                            links = 3 * (2 * b + k)
                            settle(pool, m, max_ok, 16 * b + 8 * k + 8)
                            nc.gpsimd.tensor_copy(part[:, :, 0], whole).then_inc(cut_max, 1)
                            pool.wait_ge(cut_max, links + 1)
                            nc.gpsimd.tensor_tensor(left, whole, part[:, :, 0], ALU.subtract).then_inc(cut_max, 1)
                            settle(pool, m, cut_max, links + 2)
                            nc.gpsimd.tensor_copy(part[:, :, 1], left).then_inc(cut_max, 1)
                            pool.wait_ge(cut_max, links + 3)
                            nc.gpsimd.tensor_tensor(part[:, :, 2], left, part[:, :, 1], ALU.subtract).then_inc(nmax_ok, 1)
                        elif what == "cut":
                            cols = slice(k * SEQ, (k + 1) * SEQ)
                            links = 3 * (2 * b + k)
                            pool.wait_ge(dve_read, dve_turn(s, "rot") + 1)
                            nc.gpsimd.tensor_tensor(m.qkT[:, cols], m.rope_terms[:, 0, cols], m.rope_terms[:, 1, cols],
                                                    ALU.add).then_inc(qk_ok, 1)
                            settle(pool, m, k_out if k else q_out, 16 * 6 * b)
                            settle(pool, m, qk_ok, 2 * b + k + 1)
                            nc.gpsimd.tensor_copy(parts[:, 0, cols], m.qkT[:, cols]).then_inc(cut, 1)
                            pool.wait_ge(cut, links + 1)
                            nc.gpsimd.tensor_tensor(rest[:, cols], m.qkT[:, cols], parts[:, 0, cols],
                                                    ALU.subtract).then_inc(cut, 1)
                            settle(pool, m, cut, links + 2)
                            nc.gpsimd.tensor_copy(parts[:, 1, cols], rest[:, cols]).then_inc(cut, 1)
                            pool.wait_ge(cut, links + 3)
                            nc.gpsimd.tensor_tensor(parts[:, 2, cols], rest[:, cols], parts[:, 1, cols],
                                                    ALU.subtract).then_inc(parts_ok, 1)

                steps(pool, step)

            @block.sync
            def _(sp):
                sp.wait_ge(k_clear, 1)
                for r in range(RING):
                    sp.dma_start(k_stack[DATA:DATA + MAXROWS, r], t["k_ones"]).then_inc(k_ones, 16)

                def step(s, u):
                    for what, lag, k in ORDER_A:
                        b, v = s - lag, (u - lag) % RING
                        if not live(b):
                            continue
                        if what == "cut":
                            settle(sp, m, stack_in, 16 * 4 * b)
                            settle(sp, m, parts_ok, 2 * b + k + 1)
                            for par in range(2):
                                half = parts[par * 64:(par + 1) * 64, :, k * SEQ:(k + 1) * SEQ]
                                dst = m.stack_hbm[k, par].rearrange("s r n -> r s n")
                                for at, n, part in ((0, 3, 0), (3, 2, 1), (5, 1, 2)):
                                    src = half[:, 0:n] if k == 0 else half[:, part:part + 1].broadcast_to([64, n, SEQ])
                                    sp.dma_start(dst[:, at:at + n], src).then_inc(k_out if k else q_out, 16)
                            if k == 0:
                                continue
                            settle(sp, m, probs_ok, NH * (b - 2))
                            for i in range(2):
                                settle(sp, m, k_out if i else q_out, 16 * 6 * (b + 1))
                                for par in range(2):
                                    src = m.stack_hbm[i, par].rearrange("s (d t) n -> (s d) t n", t=NPAIR)
                                    dst = (q_stack[par * ROWS:(par + 1) * ROWS, v] if i == 0 else
                                           k_stack[par * ROWS:(par + 1) * ROWS, v]
                                           .rearrange("p (t r) n -> p r t n", r=2)[:, par])
                                    sp.dma_start(dst, src).then_inc(stack_in, 16)
                        elif what == "keep":
                            settle(sp, m, kept, 32 * b)
                            settle(sp, m, act_read, act_turn(s, "conv") + 1)
                            sp.dma_start(m.xn_hbm[0, b], m.xn2[:, v].rearrange("p a b -> p (a b)")).then_inc(kept, 16)
                            sp.dma_start(m.xnT_hbm[0, b], m.xnT2[:, v, :]).then_inc(kept, 16)

                steps(sp, step)
                sp.wait_ge(kept, 32 * NSEQ)



class GateNorm:

    PIECES = 4

    def __init__(self, ctx, nc, n):
        self.mv = ctx.enter_context(nc.sbuf_tensor(f"gn{n}_mv", [NL, 2], F32))
        self.w = ctx.enter_context(nc.sbuf_tensor(f"gn{n}_w", [NL, 4], F32))
        self.mean_ok = ctx.enter_context(nc.semaphore(f"gn{n}_mean_ok"))
        self.link = ctx.enter_context(nc.semaphore(f"gn{n}_link"))
        self.gelu_ok = ctx.enter_context(nc.semaphore(f"gn{n}_gelu_ok"))

    def statistics(self, nc, m):
        nc.vector.bn_aggr(self.mv[:], m.bn_parts[:].rearrange("p a b -> p (a b)")).then_inc(self.mean_ok, 1)

    def scale_and_shift(self, nc, pool, m):
        mv, w, link = self.mv, self.w, self.link
        pool.wait_ge(self.mean_ok, 1)
        nc.gpsimd.tensor_scalar(w[:, 0:1], mv[:, 1:2], EPS, None, ALU.add).then_inc(link, 1)
        pool.wait_ge(link, 1)
        nc.gpsimd.tensor_tensor(w[:, 0:1], w[:, 0:1], m.neg_half[0:NL, 0:1], ALU.pow).then_inc(link, 1)
        pool.wait_ge(link, 2)
        nc.gpsimd.tensor_tensor(w[:, 1:2], w[:, 0:1], m.norm_gate[:, 1:2], ALU.mult).then_inc(link, 1)
        pool.wait_ge(link, 3)
        nc.gpsimd.tensor_tensor(w[:, 2:3], mv[:, 0:1], w[:, 1:2], ALU.mult).then_inc(link, 1)
        pool.wait_ge(link, 4)
        nc.gpsimd.tensor_tensor(w[:, 3:4], m.norm_gate[:, 2:3], w[:, 2:3], ALU.subtract).then_inc(link, 1)

    def gelu(self, nc, act, m):
        act.wait_ge(self.link, 5)
        for i in range(self.PIECES):
            piece = m.gate_in[:, i * NSEQ * SEQ // self.PIECES:(i + 1) * NSEQ * SEQ // self.PIECES]
            nc.scalar.activation(piece, piece, ACT.Gelu, bias=self.w[:, 3:4], scale=self.w[:, 1:2]).then_inc(self.gelu_ok, 1)



ORDER_F = [
    ("xnT", 3, 0), ("read_xnT", 3, 0), ("probs", 4, 0), ("logits", 0, 0), ("left", 2, 0), ("top", 1, 0),
    ("main", 3, 0), ("read_main", 3, 0), ("probsT", 4, 0), ("read_logits", 0, 0), ("read_probsT", 4, 0),
    ("rot", 3, 0), ("full", 0, 0), ("gates", 2, 0), ("read_rot", 3, 0), ("all", 1, 0), ("read_full", 0, 0),
    ("cos", 3, 0), ("xgT", 2, 0), ("read_xgT", 2, 0), ("xb", 2, 0), ("top", 1, 1), ("pv", 4, 0), ("read_pv", 4, 0),
    ("sum", 3, 0), ("o", 2, 0), ("read_o", 2, 0), ("stats", 2, 0), ("rstd2", 4, 0), ("load", -1, 0), ("v", 3, 0),
    ("s", 3, 0), ("rstd", 2, 0), ("read_v", 3, 0), ("v_bias", 3, 0), ("scale2", 4, 0), ("xnT2", 4, 0),
    ("top", 1, 2), ("read_xnT2", 4, 0), ("read_s", 3, 0), ("conv", 4, 0), ("scale", 2, 0), ("nmax", 3, 0),
    ("read_conv", 4, 0), ("top", 1, 3), ("bn", 4, 0), ("keep", 4, 0),
]
ORDER_LAST = [
    ("logits", 0, 0), ("left", 2, 0), ("read_logits", 0, 0), ("full", 0, 0), ("read_full", 0, 0), ("top", 1, 0),
    ("all", 1, 0), ("top", 1, 1), ("gates", 2, 0), ("xgT", 2, 0), ("read_xgT", 2, 0), ("xb", 2, 0), ("top", 1, 2),
    ("o", 2, 0), ("top", 1, 3), ("load", -1, 0), ("read_o", 2, 0), ("add", 2, 0), ("store", 2, 0),
]
GATE_BANK = [("xgT", 0), ("o", 0)]
PROJ_BANK = [("xnT", 0), ("main", 0), ("rot", 0), ("v", 0)]
ATT_BANK = [("probsT", 0), ("pv", 0), ("s", 0)]
TAIL_BANK = [("xnT2", 0), ("conv", 0)]
LOGIT_BANK = [("logits", 0)]
FULL_BANK = [("full", 0)]


def feed_forward(nc, m, n):
    with_attention = n == 0
    order = ORDER_F if with_attention else ORDER_LAST
    with ExitStack() as ctx:
        def sb(name, shape, dt=F32):
            return ctx.enter_context(nc.sbuf_tensor(f"f{n}_{name}", shape, dt))

        def psum(name, shape):
            return ctx.enter_context(nc.psum_tensor(f"f{n}_{name}", shape, F32))

        def sem(name):
            return ctx.enter_context(nc.semaphore(f"f{n}_{name}"))

        xn_f = sb("xn_f", [P, RING, QT, D])
        xnT_f = sb("xnT_f", [P, RING, SEQ])
        xa = sb("xa", [NL + 1, RING, SEQ])
        logit = sb("logit", [P, RING, QT, 2 * D])
        left = sb("left", [P, RING, QT, 2 * D])
        top8 = sb("top8", [P, NGATE, ROUNDS, 8])
        neg_top = sb("neg_top", [P, RING, NGATE])
        e_all = sb("e_all", [P, QT, 2 * D])
        e_left = sb("e_left", [P, QT, 2 * D])
        z = sb("z", [P, RING, NGATE])
        z_inv = sb("z_inv", [P, NGATE])
        gates = sb("gates", [P, QT, 2 * D])
        full_s = sb("full_s", [P, RING, QT, D])
        gated = sb("gated", [P, QT, D])
        xg = sb("xg", [P, QT, D])
        xgT = sb("xgT", [P, SEQ])
        xb = sb("xb", [P, QT, D])
        o_raw = sb("o_raw", [P, QT, D])
        logit_bank = psum("logit_bank", [P, QT * 2 * D])
        full_bank = psum("full_bank", [P, 2 * SEQ])[:, 0:SEQ]
        gate_bank = psum("gate_bank", [P, 2 * SEQ])[:, 0:SEQ]

        logit_ps, logit_read = sem("logit_ps"), sem("logit_read")
        full_ps, full_read = sem("full_ps"), sem("full_read")
        gate_ps, gate_read = sem("gate_ps"), sem("gate_read")
        loaded = sem("loaded")
        ones_ok = sem("ones_ok")
        top_ok = sem("top_ok")
        neg_ok = sem("neg_ok")
        exps_ok = sem("exps_ok")
        z_ok = sem("z_ok")
        gates_ok = sem("gates_ok")
        gated_ok = sem("gated_ok")
        xb_ok = sem("xb_ok")
        x_ok = sem("x_ok")
        turn = {k: counter(order, bank) for k, bank in (("logit", LOGIT_BANK), ("full", FULL_BANK), ("gate", GATE_BANK))}

        if with_attention:
            nmax = sb("nmax", [P, QT])
            nmax_s = sb("nmax_s", [P, QT])
            v_b = sb("v_b", [P, RING, QT, D])
            v_raw = sb("v_raw", [P, QT, D])
            shift, shift2 = sb("shift", [P, QT]), sb("shift2", [P, QT])
            prob = sb("prob", [P, QT, SEQ])
            row_sum = sb("row_sum", [P, QT])
            row_inv = sb("row_inv", [P, QT])
            probT = sb("probT", [P, QT * SEQ])
            proj_bank = psum("proj_bank", [P, QT * 2 * D])
            att_bank = psum("att_bank", [P, QT * SEQ])
            tail_bank = psum("tail_bank", [P, 2 * SEQ])[:, 0:SEQ]
            proj_ps, proj_read = sem("proj_ps"), sem("proj_read")
            att_ps, att_read = sem("att_ps"), sem("att_read")
            tail_ps, tail_read = sem("tail_ps"), sem("tail_read")
            norm, norm2 = Norm(ctx, nc, f"f{n}_ln"), Norm(ctx, nc, f"f{n}_ln2")
            term_ok = sem("term_ok")
            qk_ok = sem("qk_ok")
            max_ok = sem("max_ok")
            nmax_ok = sem("nmax_ok")
            v_ok = sem("v_ok")
            row_ok = sem("row_ok")
            x3_ok = sem("x3_ok")
            bn_ok = sem("bn_ok")
            kept = sem("kept")
            turn.update({k: counter(order, bank) for k, bank in (("proj", PROJ_BANK), ("att", ATT_BANK), ("tail", TAIL_BANK))})
        else:
            stored = sem("stored")

        def row(tensor, g):
            return tensor[:, g // 2, (g % 2) * D:(g % 2 + 1) * D]

        def halves(tensor):
            return tensor.rearrange("p (q n) -> p q n", q=2)

        gates_norm = GateNorm(ctx, nc, n)

        with nc.Block() as block:
            @block.tensor
            def _(pe):
                pe.wait_ge(ones_ok, 1)

                def step(s, u):
                    for what, lag, k in order:
                        b, v = s - lag, (u - lag) % RING
                        if not live(b):
                            continue
                        if what == "logits":
                            pe.wait_ge(loaded, 48 * (b + 1))
                            need(pe, logit_read, turn["logit"](s, what))
                            for qt in range(QT):
                                mm = nc.tensor.matmul(logit_bank[:, qt * 2 * D:(qt + 1) * 2 * D],
                                                      xa[:, v, qt * P:(qt + 1) * P], m.w_gate[:], start=True, stop=True)
                            mm.then_inc(logit_ps, 1)
                        elif what == "full":
                            need(pe, full_read, turn["full"](s, what))
                            for qt in range(QT):
                                mm = nc.tensor.matmul(full_bank[:, qt * D:(qt + 1) * D],
                                                      xnT_f[:, v, qt * P:(qt + 1) * P], m.w_ffn[:], start=True, stop=True)
                            mm.then_inc(full_ps, 1)
                        elif what == "xgT":
                            pe.wait_ge(gated_ok, NGATE * (b + 1))
                            need(pe, gate_read, turn["gate"](s, what))
                            for qt in range(QT):
                                mm = nc.tensor.transpose(gate_bank[:, qt * P:(qt + 1) * P], xg[:, qt, :], m.ident[:])
                            mm.then_inc(gate_ps, 1)
                        elif what == "o":
                            pe.wait_ge(gate_read, turn["gate"](s, what))
                            for qt in range(QT):
                                mm = nc.tensor.matmul(gate_bank[:, qt * D:(qt + 1) * D], xgT[:, qt * P:(qt + 1) * P],
                                                      m.w_ffn[:], start=True, stop=True)
                            mm.then_inc(gate_ps, 1)
                        elif what == "xnT":
                            pe.wait_ge(norm.xn_ok, QT * (b + 1))
                            need(pe, proj_read, turn["proj"](s, what))
                            for qt in range(QT):
                                mm = nc.tensor.transpose(proj_bank[:, qt * P:(qt + 1) * P], m.xn[:, v, qt, :], m.ident[:])
                            mm.then_inc(proj_ps, 1)
                        elif what in ("main", "rot"):
                            pe.wait_ge(proj_read, turn["proj"](s, what))
                            project(nc, m, m.w_qkv_b, int(what == "rot"), proj_bank).then_inc(proj_ps, 1)
                        elif what == "v":
                            pe.wait_ge(proj_read, turn["proj"](s, what))
                            for qt in range(QT):
                                mm = nc.tensor.matmul(proj_bank[:, qt * D:(qt + 1) * D],
                                                      m.xnT[:, qt * P:(qt + 1) * P], m.w_qkv_b[:, 4 * D:], start=True, stop=True)
                            mm.then_inc(proj_ps, 1)
                        elif what == "s":
                            pe.wait_ge(qk_ok, b + 1)
                            need(pe, att_read, turn["att"](s, what))
                            for qt in range(QT):
                                mm = nc.tensor.matmul(att_bank[:, qt * SEQ:(qt + 1) * SEQ], m.qkT[:, qt * P:(qt + 1) * P],
                                                      m.qkT[:, SEQ:2 * SEQ], start=True, stop=True)
                            mm.then_inc(att_ps, 1)
                        elif what == "probsT":
                            pe.wait_ge(att_read, turn["att"](s, what))
                            for kt in range(QT):
                                for qt in range(QT):
                                    mm = nc.tensor.transpose(att_bank[:, kt * SEQ + qt * P:kt * SEQ + (qt + 1) * P],
                                                             prob[:, qt, kt * P:(kt + 1) * P], m.ident[:])
                            mm.then_inc(att_ps, 1)
                        elif what == "pv":
                            pe.wait_ge(att_read, turn["att"](s, what))
                            pe.wait_ge(v_ok, b + 1)
                            for qt in range(QT):
                                for kt in range(QT):
                                    mm = nc.tensor.matmul(att_bank[:, qt * D:(qt + 1) * D],
                                                          probT[:, kt * SEQ + qt * P:kt * SEQ + (qt + 1) * P],
                                                          v_b[:, v, kt, :], start=(kt == 0), stop=(kt == QT - 1))
                            mm.then_inc(att_ps, 1)
                        elif what == "xnT2":
                            pe.wait_ge(norm2.xn_ok, QT * (b + 1))
                            need(pe, tail_read, turn["tail"](s, what))
                            for qt in range(QT):
                                mm = nc.tensor.transpose(tail_bank[:, qt * P:(qt + 1) * P], m.xn2[:, v, qt, :], m.ident[:])
                            mm.then_inc(tail_ps, 1)
                        elif what == "conv":
                            pe.wait_ge(tail_read, turn["tail"](s, what))
                            pe.wait_ge(ones_ok, 1)
                            nc.tensor.matmul(tail_bank[0:NL, :], m.w_conv[:], m.xnT2[:, v, :],
                                             start=True, stop=True).then_inc(tail_ps, 1)

                steps(pe, step)

            @block.scalar
            def _(act):
                gates_norm.gelu(nc, act, m)

                def step(s, u):
                    for what, lag, k in order:
                        b, v, source = s - lag, (u - lag) % RING, what.removeprefix("read_")
                        if not live(b):
                            continue
                        if what == "read_logits":
                            act.wait_ge(logit_ps, turn["logit"](s, source) + 1)
                            nc.scalar.copy(logit[:, v].rearrange("p a b -> p (a b)"), logit_bank[:]).then_inc(logit_read, 1)
                        elif what == "read_full":
                            act.wait_ge(full_ps, turn["full"](s, source) + 1)
                            nc.scalar.copy(full_s[:, v].rearrange("p a b -> p (a b)"), full_bank).then_inc(full_read, 1)
                        elif what == "all":
                            act.wait_ge(neg_ok, b + 1)
                            need(act, gates_ok, b)
                            for g in range(NGATE):
                                nc.scalar.activation(row(e_all, g), row(logit[:, v], g), ACT.Exp,
                                                     bias=neg_top[:, v, g:g + 1], accum_out=z[:, v, g:g + 1])
                        elif what == "left":
                            act.wait_ge(top_ok, 8 * ROUNDS * (b + 1))
                            for g in range(NGATE):
                                e = nc.scalar.activation(row(e_left, g), row(left[:, v], g), ACT.Exp,
                                                         bias=neg_top[:, v, g:g + 1])
                            e.then_inc(exps_ok, 1)
                        elif what == "read_xgT":
                            act.wait_ge(gate_ps, turn["gate"](s, source) + 1)
                            nc.scalar.copy(xgT[:], gate_bank).then_inc(gate_read, 1)
                        elif what in ("read_main", "read_rot"):
                            act.wait_ge(proj_ps, turn["proj"](s, source) + 1)
                            i = int(what == "read_rot")
                            if i == 0:
                                need(act, qk_ok, b)
                            for q in range(2):
                                e = nc.scalar.activation(m.rope_terms[:, i, q * SEQ:(q + 1) * SEQ],
                                                         proj_bank[:, q * SEQ:(q + 1) * SEQ], ACT.Identity,
                                                         bias=m.b_qk_b[:, 2 * i + q:2 * i + q + 1])
                            e.then_inc(proj_read, 1)
                        elif what == "read_xnT":
                            act.wait_ge(proj_ps, turn["proj"](s, source) + 1)
                            nc.scalar.copy(m.xnT[:], proj_bank[:, 0:SEQ]).then_inc(proj_read, 1)
                        elif what == "probs":
                            act.wait_ge(nmax_ok, b + 1)
                            need(act, row_ok, b)
                            for qt in range(QT):
                                e = nc.scalar.activation(prob[:, qt, :], att_bank[:, qt * SEQ:(qt + 1) * SEQ], ACT.Exp,
                                                         bias=nmax_s[:, qt:qt + 1], scale=D ** -0.5,
                                                         accum_out=row_sum[:, qt:qt + 1])
                            e.then_inc(att_read, 1)
                        elif what == "read_probsT":
                            act.wait_ge(att_ps, turn["att"](s, source) + 1)
                            nc.scalar.copy(probT[:], att_bank[:]).then_inc(att_read, 1)
                        elif what == "read_xnT2":
                            act.wait_ge(tail_ps, turn["tail"](s, source) + 1)
                            need(act, kept, 32 * b)
                            nc.scalar.copy(m.xnT2[:, v, :], tail_bank).then_inc(tail_read, 1)
                        elif what == "scale":
                            norm_apply(nc, act, m, norm, m.ln_rstd, shift, m.xn[:, v], b)
                        elif what == "scale2":
                            settle(act, m, kept, 32 * b)
                            norm_apply(nc, act, m, norm2, m.ln2_rstd, shift2, m.xn2[:, v], b)
                        elif what == "read_o" and not with_attention:
                            act.wait_ge(gate_ps, turn["gate"](s, source) + 1)
                            need(act, x_ok, b)
                            nc.scalar.copy(o_raw[:].rearrange("p a b -> p (a b)"), gate_bank).then_inc(gate_read, 1)
                        elif what == "read_v":
                            act.wait_ge(proj_ps, turn["proj"](s, source) + 1)
                            need(act, v_ok, b)
                            nc.scalar.copy(v_raw[:].rearrange("p a b -> p (a b)"), proj_bank[:, 0:QT * D]).then_inc(proj_read, 1)
                        elif what == "read_conv":
                            settle(act, m, tail_ps, turn["tail"](s, source) + 1)
                            need(act, loaded, 48 * (b + 1))
                            nc.scalar.activation(m.gate_in[:, bass.ds(b * SEQ, SEQ)], tail_bank[0:NL, :], ACT.Identity,
                                                 bias=m.norm_gate[:, 0:1]).then_inc(tail_read, 1)

                steps(act, step)

            @block.vector
            def _(dve):
                gates_norm.statistics(nc, m)
                nc.vector.memset(xa[NL:NL + 1], 1.0).then_inc(ones_ok, 1)

                def step(s, u):
                    for what, lag, k in order:
                        b, v, source = s - lag, (u - lag) % RING, what.removeprefix("read_")
                        if not live(b):
                            continue
                        if what == "top":
                            links = 8 * (ROUNDS * b + k)
                            if k == 0:
                                dve.wait_ge(logit_read, b + 1)
                                need(dve, neg_ok, b)
                            src = (logit if k == 0 else left)[:, v]
                            for g in range(NGATE):
                                if g % 2 == 0:
                                    settle(dve, m, top_ok, links - 4 + g + 2)
                                nc.vector.max(top8[:, g, k, :], row(src, g)).then_inc(top_ok, 1)
                            for g in range(NGATE):
                                if g % 2 == 0:
                                    settle(dve, m, top_ok, links + g + 2)
                                nc.vector.match_replace(row(left[:, v], g), top8[:, g, k, :], row(src, g), LOWEST)\
                                    .then_inc(top_ok, 1)
                        elif what == "gates":
                            dve.wait_ge(exps_ok, b + 1)
                            nc.vector.reciprocal(z_inv[:], z[:, v]).then_inc(z_ok, 1)
                            dve.wait_ge(z_ok, b + 1)
                            dve.wait_ge(gates_ok, b + 1)
                            for qt in range(QT):
                                for i, (dst, other) in enumerate(((gated, full_s), (xg, xn_f))):
                                    g = 2 * qt + i
                                    nc.vector.scalar_tensor_tensor(out=dst[:, qt, :], in0=row(gates, g),
                                                                   scalar=z_inv[:, g:g + 1], in1=other[:, v, qt, :],
                                                                   op0=ALU.mult, op1=ALU.mult).then_inc(gated_ok, 1)
                        elif what == "read_o" and with_attention:
                            dve.wait_ge(gate_ps, turn["gate"](s, source) + 1)
                            dve.wait_ge(xb_ok, 2 * (b + 1))
                            nc.vector.tensor_tensor(m.x[:, bass.ds(b * QT, QT), :],
                                                    gate_bank.rearrange("p (a b) -> p a b", a=QT), xb[:],
                                                    ALU.add).then_inc(gate_read, 1)
                        elif what == "stats":
                            settle(dve, m, gate_read, turn["gate"](s, "o") + 1)
                            norm_stats(nc, dve, m, norm, m.ln_st, m.ln_mv, b)
                        elif what == "read_s":
                            dve.wait_ge(att_ps, turn["att"](s, source) + 1)
                            nc.vector.tensor_reduce(nmax[:], att_bank[:].rearrange("p (a b) -> p a b", a=QT), AX.X, ALU.max,
                                                    negate=True).then_inc(max_ok, 1)
                        elif what == "read_pv":
                            dve.wait_ge(att_ps, turn["att"](s, source) + 1)
                            nc.vector.reciprocal(row_inv[:], row_sum[:]).then_inc(row_ok, 1)
                            dve.wait_ge(row_ok, b + 1)
                            for qt in range(QT):
                                x = m.x[:, b * QT + qt, :]
                                nc.vector.scalar_tensor_tensor(out=x, in0=att_bank[:, qt * D:(qt + 1) * D],
                                                               scalar=row_inv[:, qt:qt + 1], in1=x, op0=ALU.mult,
                                                               op1=ALU.add).then_inc(x3_ok if qt < QT - 1 else att_read, 1)
                            settle(dve, m, x3_ok, b + 1)
                            dve.wait_ge(att_read, turn["att"](s, source) + 1)
                            norm_stats(nc, dve, m, norm2, m.ln2_st, m.ln2_mv, b)
                        elif what == "bn":
                            settle(dve, m, tail_read, turn["tail"](s, "conv") + 1)
                            nc.vector.bn_stats(m.bn_parts[:, b, :], m.gate_in[:, bass.ds(b * SEQ, SEQ)]).then_inc(bn_ok, 1)

                steps(dve, step)

            @block.gpsimd
            def _(pool):
                gates_norm.scale_and_shift(nc, pool, m)

                def step(s, u):
                    for what, lag, k in order:
                        b, v = s - lag, (u - lag) % RING
                        if not live(b):
                            continue
                        if what == "left":
                            pool.wait_ge(exps_ok, b + 1)
                            need(pool, gated_ok, NGATE * b)
                            nc.gpsimd.tensor_tensor(gates[:], e_all[:], e_left[:], ALU.subtract).then_inc(gates_ok, 1)
                            need(pool, *((gate_read, turn["gate"](s, "xgT")) if with_attention else (x_ok, b)))
                            nc.gpsimd.tensor_tensor(xb[:], m.x[:, bass.ds(b * QT, QT), :],
                                                    m.b_ffn[:].unsqueeze(1).broadcast_to([P, QT, D]),
                                                    ALU.add).then_inc(xb_ok, 1)
                        elif what == "xb":
                            pool.wait_ge(gated_ok, NGATE * (b + 1))
                            pool.wait_ge(xb_ok, 2 * b + 1)
                            nc.gpsimd.tensor_tensor(xb[:], xb[:], gated[:], ALU.add).then_inc(xb_ok, 1)
                        elif what == "all":
                            settle(pool, m, exps_ok, b - 2)
                            settle(pool, m, top_ok, 8 * ROUNDS * b + NGATE)
                            nc.gpsimd.tensor_scalar(neg_top[:, v], top8[:, :, 0, 0], -1.0, None,
                                                    ALU.mult).then_inc(neg_ok, 1)
                        elif what == "rstd":
                            norm_rstd_shift(nc, pool, m, norm, m.ln_mv, m.ln_rstd, shift, b)
                        elif what == "rstd2":
                            norm_rstd_shift(nc, pool, m, norm2, m.ln2_mv, m.ln2_rstd, shift2, b)
                        elif what == "add":
                            settle(pool, m, xb_ok, 2 * (b + 1))
                            settle(pool, m, gate_read, turn["gate"](s, "o") + 1)
                            pool.wait_ge(m.fills, 1)
                            nc.gpsimd.tensor_tensor(m.x[:, bass.ds(b * QT, QT), :], o_raw[:], xb[:], ALU.add).then_inc(x_ok, 1)
                        elif what == "v_bias":
                            pool.wait_ge(proj_read, turn["proj"](s, "v") + 1)
                            nc.gpsimd.tensor_tensor(v_b[:, v], v_raw[:], m.b_v_b[:].unsqueeze(1).broadcast_to([P, QT, D]),
                                                    ALU.add).then_inc(v_ok, 1)
                        elif what == "cos":
                            pool.wait_ge(proj_read, turn["proj"](s, "main") + 1)
                            nc.gpsimd.tensor_tensor(halves(m.rope_terms[:, 0]), halves(m.rope_terms[:, 0]),
                                                    m.rope_b[:, 0, :].unsqueeze(1).broadcast_to([P, 2, SEQ]),
                                                    ALU.mult).then_inc(term_ok, 1)
                        elif what == "sum":
                            pool.wait_ge(proj_read, turn["proj"](s, "rot") + 1)
                            nc.gpsimd.tensor_tensor(halves(m.rope_terms[:, 1]), halves(m.rope_terms[:, 1]),
                                                    m.rope_b[:, 1, :].unsqueeze(1).broadcast_to([P, 2, SEQ]),
                                                    ALU.mult).then_inc(term_ok, 1)
                            pool.wait_ge(term_ok, 2 * (b + 1))
                            nc.gpsimd.tensor_tensor(m.qkT[:], m.rope_terms[:, 0], m.rope_terms[:, 1],
                                                    ALU.add).then_inc(qk_ok, 1)
                        elif what == "nmax":
                            settle(pool, m, att_read, turn["att"](s, "s"))
                            settle(pool, m, max_ok, b + 1)
                            nc.gpsimd.tensor_scalar(nmax_s[:], nmax[:], D ** -0.5, None, ALU.mult).then_inc(nmax_ok, 1)

                steps(pool, step)

            @block.sync
            def _(sp):
                def load(b, v):
                    if isinstance(b, int) and b <= FIRST_LOOPED:
                        sp.wait_ge(gates_norm.gelu_ok, 1 if b < FIRST_LOOPED else GateNorm.PIECES)
                    settle(sp, m, loaded, 48 * b)
                    settle(sp, m, gated_ok, NGATE * (b - 2))
                    sp.dma_start(xa[0:NL, v, :], m.gate_in[:, bass.ds(b * SEQ, SEQ)]).then_inc(loaded, 16)
                    sp.dma_start(xnT_f[:, v, :], m.xnT_hbm[n, b]).then_inc(loaded, 16)
                    sp.dma_start(xn_f[:, v].rearrange("p a b -> p (a b)"), m.xn_hbm[n, b]).then_inc(loaded, 16)

                load(0, 0)

                def step(s, u):
                    for what, lag, k in order:
                        b, v = s - lag, (u - lag) % RING
                        if not live(b):
                            continue
                        if what == "load":
                            load(b, v)
                        elif what == "keep":
                            settle(sp, m, kept, 32 * b)
                            settle(sp, m, tail_read, turn["tail"](s, "conv") + 1)
                            sp.dma_start(m.xn_hbm[1, b], m.xn2[:, v].rearrange("p a b -> p (a b)")).then_inc(kept, 16)
                            sp.dma_start(m.xnT_hbm[1, b], m.xnT2[:, v, :]).then_inc(kept, 16)
                        elif what == "store" and not with_attention:
                            settle(sp, m, x_ok, b + 1)
                            sp.dma_start(m.out_dram[:, b], m.x[:, bass.ds(b * QT, QT), :]).then_inc(stored, 16)

                steps(sp, step)
                if with_attention:
                    sp.wait_ge(kept, 32 * NSEQ)
                else:
                    sp.wait_ge(stored, 16 * NSEQ)


def kernel(**inputs):
    import ml_dtypes as _ml
    import numpy as _np
    import concourse.bacc as _bacc
    from concourse.bass_utils import run_bass_kernel_spmd as _run

    f32 = _np.float32

    def got(name):
        return _np.ascontiguousarray(inputs["L0_" + name])

    order = [(par, d, pair) for par in range(2) for d in range(HD) for pair in range(NPAIR)]

    def column(par, d, pair):
        return (2 * pair + par) * HD + d

    cols = _np.array([column(*o) for o in order])
    partners = _np.array([column(par, d ^ 1 if 2 <= d < 6 else d, pair) for par, d, pair in order])
    n = _np.arange(SEQ)
    rope_a = _np.zeros((P, 2, SEQ), f32)
    for c, (par, d, pair) in enumerate(order):
        if 2 <= d < 6:
            angle = (n // 16 if d < 4 else n % 16).astype(f32)
            rope_a[c, 0], rope_a[c, 1] = _np.cos(angle), _np.sin(angle) if d % 2 else -_np.sin(angle)
        else:
            rope_a[c, 0] = 1.0
    inv = (f32(1.0) / f32(10000.0) ** (_np.arange(0, D, 2, dtype=f32) / f32(D))).astype(f32)
    angle = n.astype(f32)[:, None] * inv[None, :]
    rope_b = _np.zeros((D // 2, 2, 2, SEQ), f32)
    for e in range(2):
        rope_b[:, e, 0] = _np.cos(angle).T
        rope_b[:, e, 1] = (_np.sin(angle) if e else -_np.sin(angle)).T
    turned = _np.arange(D) ^ 1

    def weights(wq, wk, wv, take, partner):
        return _np.concatenate([wq[:, take], wk[:, take], wq[:, partner], wk[:, partner], wv], axis=1)

    def biases(bq, bk, take, partner):
        return _np.stack([bq[take], bk[take], bq[partner], bk[partner]], axis=1)

    w_conv = _np.zeros((D, NL), f32)
    w_gate = _np.zeros((NL + 1, 2 * D), f32)
    for i, gate in enumerate(("so", "si")):
        conv = got(f"ffn_{gate}_conv_w")
        for g in range(NG):
            w_conv[4 * g:4 * g + 4, i * NG + g] = conv[g]
        w_gate[i * NG:(i + 1) * NG, i * D:(i + 1) * D] = got(f"ffn_{gate}_lin_w").T
        w_gate[NL, i * D:(i + 1) * D] = got(f"ffn_{gate}_lin_b")
    norm_gate = _np.stack([_np.concatenate([got(f"ffn_so_{k}"), got(f"ffn_si_{k}")])
                           for k in ("conv_b", "gamma", "beta")], axis=1)
    k_ones = _np.zeros((2, 3, NPAIR, 2, SEQ), f32)
    for par in range(2):
        k_ones[par, :, :, par, :] = 1.0
    arrays = {
        "x": got("attn_a_hidden_states"),
        "ident": _np.eye(P, dtype=f32),
        "ident_bf": _np.eye(P, dtype=f32).astype(_ml.bfloat16),
        "k_ones": k_ones.reshape(MAXROWS, NH, SEQ).astype(_ml.bfloat16),
        "rope_a": rope_a,
        "rope_b": rope_b.reshape(D, 2, SEQ),
        "w_qkv_a": weights(got("attn_a_Wq"), got("attn_a_Wk"), got("attn_a_Wv"), cols, partners),
        "b_qk_a": biases(got("attn_a_bq"), got("attn_a_bk"), cols, partners),
        "b_v_a": got("attn_a_bv"),
        "w_o": got("attn_a_Wo"),
        "b_o": got("attn_a_bo"),
        "w_qkv_b": weights(got("attn_b_wq_w").T, got("attn_b_wk_w").T, got("attn_b_wv_w").T, _np.arange(D), turned),
        "b_qk_b": biases(got("attn_b_wq_b"), got("attn_b_wk_b"), _np.arange(D), turned),
        "b_v_b": got("attn_b_wv_b"),
        "w_conv": w_conv,
        "norm_gate": norm_gate,
        "w_gate": w_gate,
        "w_ffn": got("ffn_weight"),
        "b_ffn": got("ffn_bias"),
    }
    arrays = {k: _np.ascontiguousarray(a) for k, a in arrays.items()}
    nc = _bacc.Bacc("TRN2", target_bir_lowering=False, num_devices=1)
    t = {k: nc.dram_tensor("in_" + k, a.shape, mybir.dt.from_np(a.dtype), kind="ExternalInput").ap()
         for k, a in arrays.items()}
    out = nc.dram_tensor("out_0", (NSEQ, SEQ, D), F32, kind="ExternalOutput").ap()
    program(nc, t, out)
    r = _run(nc, [{"in_" + k: a for k, a in arrays.items()}], core_ids=[0])
    return r.results[0]["out_0"]
```
